# Optimizing a Trainium2 kernel written in Bass

```python
import numpy as np
import jax
import jax.numpy as jnp

def _softmax(x, axis=-1):
    return jax.nn.softmax(x, axis=axis)

def _gelu(x):
    return jax.nn.gelu(x, approximate=True)

def _silu(x):
    return jax.nn.silu(x)

def _sigmoid(x):
    return jax.nn.sigmoid(x)

def _layernorm(x, axis=-1, eps=1e-05):
    m = jnp.mean(x, axis=axis, keepdims=True)
    v = jnp.var(x, axis=axis, keepdims=True)
    return (x - m) / jnp.sqrt(v + eps)

def _scatter_add(tgt, idx, src, axis=0):
    return tgt.at[idx].add(src)

def _segment_sum(src, seg, n):
    return jax.ops.segment_sum(src, seg, n)
kernel_name = 'mk_gnn_preln_d2_gnn_r32_992deb'

def setup_inputs(seed: int=0):
    np.random.seed(seed)
    _w = jnp.asarray

    def _rec_inputs():
        import jax
        import jax.numpy as jnp
        _gk = jax.random.key(seed)
        x = -0.000202 + 1 * jax.random.normal(jax.random.fold_in(_gk, 1), (50000, 128), jnp.float32)
        src = jax.random.randint(jax.random.fold_in(_gk, 2), (25000,), 0, 50000, jnp.int32)
        dst = jax.random.randint(jax.random.fold_in(_gk, 3), (25000,), 0, 50000, jnp.int32)
        _o = jnp.argsort(dst, stable=True)
        src = src[_o]
        dst = dst[_o]
        return (x, src, dst)
    x, src, dst = _rec_inputs()

    def _L0_gnn_setup():
        import jax, jax.numpy as jnp
        import numpy as np
        N_NODES = 50000
        LN_EPS = 1e-05
        NEG_SLOPE = 0.01

        def _leaky(x):
            return jnp.where(x >= 0, x, NEG_SLOPE * x)

        def _layer_norm(x, g, b):
            mu = jnp.mean(x, axis=-1, keepdims=True)
            var = jnp.mean(jnp.square(x - mu), axis=-1, keepdims=True)
            return (x - mu) * jax.lax.rsqrt(var + LN_EPS) * g + b

        def _edge_conv(x, src, dst, W1, b1, W2, b2):
            x_i = x[dst]
            x_j = x[src]
            h = jnp.concatenate([x_i, x_j - x_i], axis=-1)
            m = _leaky(h @ W1 + b1) @ W2 + b2
            return jax.ops.segment_sum(m, dst, num_segments=N_NODES)
        key = jax.random.key(seed)
        ks = jax.random.split(key, 8)
        din, hid, E = (128, 128, 25000)

        def kaiming(k, fan_in, shape):
            gain = np.sqrt(2.0 / (1.0 + 0.01 ** 2))
            bound = gain * np.sqrt(3.0 / fan_in)
            return jax.random.uniform(k, shape, jnp.float32, -bound, bound)
        x = jax.random.normal(ks[0], (N_NODES, din), jnp.float32)
        edges = jax.random.randint(ks[1], (2, E), 0, N_NODES, jnp.int64)
        return {'task_features': x, 'task_edges': edges, 'W1_0': kaiming(ks[2], 2 * din, (2 * din, hid)), 'b1_0': jnp.zeros((hid,), jnp.float32), 'W2_0': kaiming(ks[3], hid, (hid, hid)), 'b2_0': jnp.zeros((hid,), jnp.float32), 'ln_g0': jnp.ones((hid,), jnp.float32), 'ln_b0': jnp.zeros((hid,), jnp.float32), 'W1_1': kaiming(ks[4], 2 * hid, (2 * hid, hid)), 'b1_1': jnp.zeros((hid,), jnp.float32), 'W2_1': kaiming(ks[5], hid, (hid, hid)), 'b2_1': jnp.zeros((hid,), jnp.float32), 'ln_g1': jnp.ones((hid,), jnp.float32), 'ln_b1': jnp.zeros((hid,), jnp.float32)}
    _L0_gnn_all = _L0_gnn_setup()
    _L0_gnn_in = {k: v for k, v in _L0_gnn_all.items() if k in ('W1_0', 'b1_0', 'W2_0', 'b2_0', 'ln_g0', 'ln_b0', 'W1_1', 'b1_1', 'W2_1', 'b2_1', 'ln_g1', 'ln_b1')}
    del _L0_gnn_all

    def _L1_gnn_setup():
        import jax, jax.numpy as jnp
        import numpy as np
        N = 50000
        E = 25000
        IN = 128
        OUT = 128
        H = 4
        C = OUT // H
        NEG_SLOPE = 0.2

        def _segment_softmax(scores, seg, n):
            seg_max = jax.ops.segment_max(scores, seg, num_segments=n)
            ex = jnp.exp(scores - seg_max[seg])
            seg_sum = jax.ops.segment_sum(ex, seg, num_segments=n)
            return ex / (seg_sum[seg] + 1e-16)
        key = jax.random.key(seed)
        ks = jax.random.split(key, 7)
        x = jax.random.normal(ks[0], (N, IN), dtype=jnp.float32)
        edge_index = jax.random.randint(ks[1], (2, E), 0, N, dtype=jnp.int32)
        s_in = 1.0 / np.sqrt(IN)
        W_gat = jax.random.normal(ks[2], (OUT, IN), dtype=jnp.float32) * s_in
        att_src = jax.random.normal(ks[3], (H, C), dtype=jnp.float32) * 0.1
        att_dst = jax.random.normal(ks[4], (H, C), dtype=jnp.float32) * 0.1
        bias = jnp.zeros((OUT,), dtype=jnp.float32)
        W_skip = jax.random.normal(ks[5], (OUT, IN), dtype=jnp.float32) * s_in
        return {'x': x, 'edge_index': edge_index, 'W_gat': W_gat, 'att_src': att_src, 'att_dst': att_dst, 'bias': bias, 'W_skip': W_skip}
    _L1_gnn_all = _L1_gnn_setup()
    _L1_gnn_in = {k: v for k, v in _L1_gnn_all.items() if k in ('W_gat', 'att_src', 'att_dst', 'bias', 'W_skip')}
    del _L1_gnn_all
    return {'x': x, 'src': src, 'dst': dst, 'L0_gnn_W1_0': _L0_gnn_in['W1_0'], 'L0_gnn_b1_0': _L0_gnn_in['b1_0'], 'L0_gnn_W2_0': _L0_gnn_in['W2_0'], 'L0_gnn_b2_0': _L0_gnn_in['b2_0'], 'L0_gnn_ln_g0': _L0_gnn_in['ln_g0'], 'L0_gnn_ln_b0': _L0_gnn_in['ln_b0'], 'L0_gnn_W1_1': _L0_gnn_in['W1_1'], 'L0_gnn_b1_1': _L0_gnn_in['b1_1'], 'L0_gnn_W2_1': _L0_gnn_in['W2_1'], 'L0_gnn_b2_1': _L0_gnn_in['b2_1'], 'L0_gnn_ln_g1': _L0_gnn_in['ln_g1'], 'L0_gnn_ln_b1': _L0_gnn_in['ln_b1'], 'L1_gnn_W_gat': _L1_gnn_in['W_gat'], 'L1_gnn_att_src': _L1_gnn_in['att_src'], 'L1_gnn_att_dst': _L1_gnn_in['att_dst'], 'L1_gnn_bias': _L1_gnn_in['bias'], 'L1_gnn_W_skip': _L1_gnn_in['W_skip']}

def reference(x, src, dst, L0_gnn_W1_0, L0_gnn_b1_0, L0_gnn_W2_0, L0_gnn_b2_0, L0_gnn_ln_g0, L0_gnn_ln_b0, L0_gnn_W1_1, L0_gnn_b1_1, L0_gnn_W2_1, L0_gnn_b2_1, L0_gnn_ln_g1, L0_gnn_ln_b1, L1_gnn_W_gat, L1_gnn_att_src, L1_gnn_att_dst, L1_gnn_bias, L1_gnn_W_skip):
    import jax
    import jax.numpy as jnp

    def _L0_gnn_ref(task_features, task_edges, W1_0, b1_0, W2_0, b2_0, ln_g0, ln_b0, W1_1, b1_1, W2_1, b2_1, ln_g1, ln_b1):
        import jax, jax.numpy as jnp
        import numpy as np
        N_NODES = 50000
        LN_EPS = 1e-05
        NEG_SLOPE = 0.01

        def _leaky(x):
            return jnp.where(x >= 0, x, NEG_SLOPE * x)

        def _layer_norm(x, g, b):
            mu = jnp.mean(x, axis=-1, keepdims=True)
            var = jnp.mean(jnp.square(x - mu), axis=-1, keepdims=True)
            return (x - mu) * jax.lax.rsqrt(var + LN_EPS) * g + b

        def _edge_conv(x, src, dst, W1, b1, W2, b2):
            x_i = x[dst]
            x_j = x[src]
            h = jnp.concatenate([x_i, x_j - x_i], axis=-1)
            m = _leaky(h @ W1 + b1) @ W2 + b2
            return jax.ops.segment_sum(m, dst, num_segments=N_NODES)
        src, dst = (task_edges[0], task_edges[1])
        h = task_features
        h = _edge_conv(h, src, dst, W1_0, b1_0, W2_0, b2_0)
        h = _leaky(_layer_norm(h, ln_g0, ln_b0))
        h = _edge_conv(h, src, dst, W1_1, b1_1, W2_1, b2_1)
        h = _leaky(_layer_norm(h, ln_g1, ln_b1))
        return h

    def _L1_gnn_ref(x, edge_index, W_gat, att_src, att_dst, bias, W_skip):
        import jax, jax.numpy as jnp
        import numpy as np
        N = 50000
        E = 25000
        IN = 128
        OUT = 128
        H = 4
        C = OUT // H
        NEG_SLOPE = 0.2

        def _segment_softmax(scores, seg, n):
            seg_max = jax.ops.segment_max(scores, seg, num_segments=n)
            ex = jnp.exp(scores - seg_max[seg])
            seg_sum = jax.ops.segment_sum(ex, seg, num_segments=n)
            return ex / (seg_sum[seg] + 1e-16)
        loops = jnp.arange(N, dtype=edge_index.dtype)
        src = jnp.concatenate([edge_index[0], loops])
        dst = jnp.concatenate([edge_index[1], loops])
        x_proj = (x @ W_gat.T).reshape(N, H, C)
        a_src = jnp.einsum('nhc,hc->nh', x_proj, att_src)
        a_dst = jnp.einsum('nhc,hc->nh', x_proj, att_dst)
        e = a_src[src] + a_dst[dst]
        e = jnp.where(e > 0, e, NEG_SLOPE * e)
        alpha = _segment_softmax(e, dst, N)
        msgs = alpha[:, :, None] * x_proj[src]
        agg = jax.ops.segment_sum(msgs, dst, num_segments=N)
        out = agg.reshape(N, OUT) + bias
        out = out + x @ W_skip.T
        return jax.nn.elu(out)
    edge_index = jnp.stack([src, dst])
    h = jnp.maximum(_layernorm(x, axis=-1), 0.0)
    x = x + _L0_gnn_ref(h, edge_index, L0_gnn_W1_0, L0_gnn_b1_0, L0_gnn_W2_0, L0_gnn_b2_0, L0_gnn_ln_g0, L0_gnn_ln_b0, L0_gnn_W1_1, L0_gnn_b1_1, L0_gnn_W2_1, L0_gnn_b2_1, L0_gnn_ln_g1, L0_gnn_ln_b1)
    h = jnp.maximum(_layernorm(x, axis=-1), 0.0)
    x = x + _L1_gnn_ref(h, edge_index, L1_gnn_W_gat, L1_gnn_att_src, L1_gnn_att_dst, L1_gnn_bias, L1_gnn_W_skip)
    return x

_drawn_inputs = setup_inputs


def setup_inputs(seed=0):
    import zlib

    import numpy as np

    out = dict(_drawn_inputs(seed))
    spreads = {'L0_gnn_b1_0': (0.0, 0.1),
     'L0_gnn_b2_0': (0.0, 0.1),
     'L0_gnn_ln_g0': (1.0, 0.2),
     'L0_gnn_ln_b0': (0.0, 0.1),
     'L0_gnn_b1_1': (0.0, 0.1),
     'L0_gnn_b2_1': (0.0, 0.1),
     'L0_gnn_ln_g1': (1.0, 0.2),
     'L0_gnn_ln_b1': (0.0, 0.1),
     'L1_gnn_bias': (0.0, 0.1)}
    factors = {}
    for name, (base, spread) in spreads.items():
        noise = np.random.default_rng([zlib.crc32(name.encode()), seed]).standard_normal(out[name].shape)
        drawn = base * np.exp(spread * noise) if base else spread * noise
        out[name] = jnp.asarray(drawn.astype(out[name].dtype))
    for name, factor in factors.items():
        out[name] = (out[name] * factor).astype(out[name].dtype)
    return out
```

```python
import concourse.bass as bass
from concourse import mybir
from contextlib import ExitStack

fp32 = mybir.dt.float32
fp16 = mybir.dt.float16
i32 = mybir.dt.int32
u8 = mybir.dt.uint8
ALU = mybir.AluOpType
ACT = mybir.ActivationFunctionType

D = 128
P = 128
H = 4
C = D // H
TG = 4
GE = TG * P
RING = 4
EPS = 1e-5
BIG = 1e30
SLOPE = 0.01
GAT_SLOPE = 0.2


def pipeline(eng, n, stages):
    lags = max(lag for lag, _ in stages)
    first = lags + RING
    turns = max((n - 1 - first) // RING, 0)

    def peeled(s):
        for lag, f in stages:
            if 0 <= s - lag < n:
                f(s - lag, (s - lag) % RING, (s - lag) // RING + 1)

    for s in range(first):
        peeled(s)
    with eng.Fori(0, turns) as i:
        for s in range(first, first + RING):
            for lag, f in stages:
                f(RING * i + (s - lag), (s - lag) % RING, i + ((s - lag) // RING + 1))
    for s in range(first + RING * turns, n + lags):
        peeled(s)


def pool_pipeline(eng, n, stage, after=None):
    after = after or (lambda g, k, it: None)
    for g in range(RING):
        stage(g, g, 1)
        if g:
            after(g - 1, g - 1, 1)
    with eng.Fori(2, n // RING + 1) as i:
        for k in range(RING):
            stage(RING * i + (k - RING), k, i)
            after(RING * i + (k - RING - 1), (k - 1) % RING, i if k else i - 1)
    for g in range(n // RING * RING, n):
        stage(g, g % RING, g // RING + 1)
        after(g - 1, (g - 1) % RING, (g - 1) // RING + 1)
    after(n - 1, (n - 1) % RING, (n - 1) // RING + 1)


def later(g):
    return not isinstance(g, int) or g >= RING


def gnn_kernel(nc, x, src, dst, W1, b1, W2, b2, ln_g, ln_b, W_gat, att_src, att_dst, gat_bias, W_skip, out):
    N = x.shape[0]
    E = src.shape[0]
    NG = (E + GE - 1) // GE
    NT = NG * TG
    EP = NT * P
    EJ = EP // P
    NONE = EP
    NCOL = 512
    assert NCOL * P > N and NT > P and E > (NT - 1) * P and E > (P - 1) * EJ

    ctx = ExitStack()
    with ctx:
        def sb(name, shape, dt=fp32, c=ctx):
            return c.enter_context(nc.sbuf_tensor(name, shape, dt))

        def ps(name, shape, c, dt=fp32):
            return c.enter_context(nc.psum_tensor(name, shape, dt))

        taken = []

        def sem(name):
            taken.append(nc.alloc_semaphore(name))
            return taken[-1]

        def end_stage():
            nc.clear_and_free_semaphores(list(taken))
            taken.clear()
            nc.all_engine_barrier()

        def dram(name, shape, dt=fp32):
            return nc.dram_tensor(name, shape, dt).ap()

        bounds_d = dram("bounds_d", (P * NCOL, 2), i32)
        eq_d = dram("eq_d", (1, EP), u8)
        eqr_d = dram("eqr_d", (1, EP), u8)
        cnt_d = dram("cnt_d", (1, EP))
        xs_d = dram("xs_d", (EP, D))
        xd_d = dram("xd_d", (EP, D))
        seg1_d = dram("seg1_d", (EP + 1, D))
        seg2_d = dram("seg2_d", (EP + 1, D))
        x1_d = dram("x1_d", (EP, D))
        hdT_d = dram("hdT_d", (NG, P, GE))
        pT_d = dram("pT_d", (NG, P, GE))
        score_d = dram("score_d", (2 * H, EP))
        alpha_d = dram("alpha_d", (2 * H, EP))

        ident = sb("ident", [P, P])
        ones_row = sb("ones_row", [1, P])
        eps = sb("eps", [P, 1])
        eq_bc = sb("eq_bc", [P, EP], u8)
        eqr_bc = sb("eqr_bc", [P, EP], u8)
        idx_sd = sb("idx_sd", [P, NT, 2], i32)
        idx_out = sb("idx_out", [P, NT], i32)
        bnd = sb("bnd", [P, NT, 2], i32)
        is_last = sb("is_last", [P, NT])
        is_first = sb("is_first", [P, NT])
        w1s = [sb(f"w1s{l}", [P, D]) for l in range(2)]
        w1d = [sb(f"w1d{l}", [P, D]) for l in range(2)]
        w2 = [sb(f"w2{l}", [P, D]) for l in range(2)]
        b1c = [sb(f"b1c{l}", [P, 1]) for l in range(2)]
        b2r = [sb(f"b2r{l}", [1, D]) for l in range(2)]
        gc = [sb(f"gc{l}", [P, 1]) for l in range(2)]
        bc = [sb(f"bc{l}", [P, 1]) for l in range(2)]
        wgT = sb("wgT", [P, D])
        wskT = sb("wskT", [P, D])
        wsum = sb("wsum", [P, D])
        score_s = sb("score_s", [P, 2 * H])
        score_dd = sb("score_dd", [P, 2 * H])
        spread_a = sb("spread_a", [2 * H, D])
        spread_b = sb("spread_b", [2 * H, D])
        bias_r = sb("bias_r", [1, D])
        empty_bc = sb("empty_bc", [P, 1, D])
        eqP = sb("eqP", [P, EJ])
        eqnP = sb("eqnP", [P, EJ])
        lead = [sb(f"lead{k}", [P, EJ]) for k in range(2)]
        neg_eq = [sb(f"neg_eq{k}", [P, EJ]) for k in range(2)]
        neg_lead = [sb(f"neg_lead{k}", [P, EJ]) for k in range(2)]

        def tile_rows(table, g):
            return table[bass.ds(g * GE, GE), :].rearrange("(t p) f -> p t f", p=P)

        def seg_dve(eng, link, heads, v, loc, pack, row, car, carry, psr, psc, name, maximum, total):
            for k in range(2):
                rev = slice(None, None, -1) if k else slice(None)
                end = 0 if k else EJ - 1
                mask = (neg_eq if maximum else (eqP, eqnP))[k]
                run = (neg_lead if maximum else lead)[k]
                op0, op1 = (ALU.add, ALU.max) if maximum else (ALU.mult, ALU.add)
                for h in range(heads):
                    link(eng.tensor_tensor_scan(out=loc[k][:, h, rev], data0=mask[:, rev], data1=v[:, h, rev],
                                                initial=-BIG if maximum else 0.0, op0=op0, op1=op1))
                for h in range(heads):
                    link(eng.tensor_copy(pack[:, h:h + 1], loc[k][:, h, end:end + 1]))
                    link(eng.tensor_copy(pack[:, heads + h:heads + h + 1], run[:, end:end + 1]))
                eng.sem_inc(name["pack"], 1)
                eng.wait_ge(name["row"], len(name["n"]) + 1)
                link(eng.tensor_copy(row[0:heads, :], psr[0:heads, 0:2 * P]))
                link(eng.memset(car[0:heads, :], -BIG if maximum else 0.0))
                o = slice(0, P) if k else slice(1, P + 1)
                link(eng.tensor_tensor_scan(out=car[0:heads, o][:, rev], data0=row[0:heads, P:2 * P][:, rev],
                                            data1=row[0:heads, 0:P][:, rev],
                                            initial=-BIG if maximum else 0.0, op0=op0, op1=op1))
                eng.sem_inc(name["scanned"], 1)
                eng.wait_ge(name["carry"], len(name["n"]) + 1)
                name["n"].append(k)
                link(eng.tensor_copy(carry[:, 0:heads], psc[:, 0:heads]))
                for h in range(heads):
                    link(eng.scalar_tensor_tensor(out=loc[k][:, h, :], in0=run[:, :], scalar=carry[:, h:h + 1],
                                                  in1=loc[k][:, h, :], op0=op0, op1=op1))
            a, b, t = (z[:, 0:heads, :] for z in (loc[0], loc[1], total))
            link(eng.tensor_tensor(t, a, b, ALU.max if maximum else ALU.add))
            if not maximum:
                link(eng.tensor_tensor(t, t, v[:, 0:heads, :], ALU.subtract))

        def seg_pe(eng, heads, pack, car, psr, psc, name):
            for k in range(2):
                n = len(name["n_pe"]) + 1
                name["n_pe"].append(k)
                eng.wait_ge(name["pack"], n)
                eng.transpose(psr[0:heads, 0:P], pack[:, 0:heads], ident[:, :])
                eng.transpose(psr[0:heads, P:2 * P], pack[:, heads:2 * heads], ident[:, :]).then_inc(name["row"], 1)
                eng.wait_ge(name["scanned"], n)
                o = slice(1, P + 1) if k else slice(0, P)
                eng.transpose(psc[:, 0:heads], car[0:heads, o], ident[0:heads, 0:heads]).then_inc(name["carry"], 1)

        def linker(eng, s):
            n = [0]

            def link(ins):
                n[0] += 1
                ins.then_inc(s, 1)
                eng.wait_ge(s, n[0])
            return link

        with ExitStack() as pc:
            ri = sb("ri", [P, 2, 4, P], i32, pc)
            rf = sb("rf", [P, 2, 4, P], fp32, pc)
            tf = sb("tf", [P, 4, 2 * P], fp32, pc)
            pm_i = sb("pm_i", [P, 3, EJ], i32, pc)
            pm = sb("pm", [P, 3, EJ], fp32, pc)
            wraw = sb("wraw", [P, 4, D], fp32, pc)
            wg_raw = sb("wg_raw", [P, D], fp32, pc)
            wsk_raw = sb("wsk_raw", [P, D], fp32, pc)
            att = sb("att", [P, 2 * H], fp32, pc)
            before = sb("before", [P, P], fp32, pc)
            iota_i = sb("iota_i", [P, NCOL], i32, pc)
            iota_h = sb("iota_h", [P, NCOL], fp16, pc)
            dst_i = sb("dst_i", [P, NT], i32, pc)
            part_i = sb("part_i", [P, 2, NT], i32, pc)
            part_f = sb("part_f", [P, 2, NT], fp32, pc)
            onehot_p = sb("onehot_p", [P, RING, P], fp16, pc)
            onehot_c = sb("onehot_c", [P, RING, NCOL], fp16, pc)
            zeros_h = sb("zeros_h", [P, NCOL], fp16, pc)
            hist = sb("hist", [P, NCOL], fp32, pc)
            cum = sb("cum", [P, NCOL], fp32, pc)
            some = sb("some", [P, NCOL], fp32, pc)
            fl = sb("fl", [P, 2, NCOL], fp32, pc)
            bnd_i = sb("bnd_i", [P, NCOL, 2], i32, pc)
            offs = sb("offs", [P, 1], fp32, pc)
            eq8 = sb("eq8", [P, EJ], u8, pc)
            eqr8 = sb("eqr8", [P, EJ], u8, pc)
            eqn_back = sb("eqn_back", [P, EJ], fp32, pc)
            flip = sb("flip", [P, P], fp32, pc)
            zrow = sb("zrow", [1, D], fp32, pc)
            onesP = sb("onesP", [P, 1, EJ], fp32, pc)
            cntP = sb("cntP", [P, 1, EJ], fp32, pc)
            loc = [sb(f"c_loc{k}", [P, 1, EJ], fp32, pc) for k in range(2)]
            pack = sb("c_pack", [P, 2], fp32, pc)
            row = sb("c_row", [1, 2 * P], fp32, pc)
            car = sb("c_car", [1, P + 1], fp32, pc)
            carry = sb("c_carry", [P, 1], fp32, pc)
            ptile = ps("ptile", [P, 4, 2 * P], pc)
            phist = ps("phist", [P, NCOL], pc)
            pflip = ps("pflip", [P, 512], pc)
            pmisc = ps("pmisc", [P, 512], pc)
            psr = ps("c_psr", [P, 512], pc)
            psc = ps("c_psc", [P, 512], pc)

            s_fill = sem("p_fill")
            s_rows = sem("p_rows")
            s_w = sem("p_w")
            s_att0 = sem("p_att0")
            s_iota = sem("p_iota")
            s_id = sem("p_id")
            s_bef = sem("p_bef")
            s_rf = sem("p_rf")
            s_tile = sem("p_tile")
            s_oh = sem("p_onehot")
            s_mm = sem("p_hist_step")
            s_wT = sem("p_wT")
            s_wTc = sem("p_wT_copied")
            s_wsc = sem("p_wscore")
            s_cum = sem("p_cum")
            s_off = sem("p_off")
            s_link = sem("p_link")
            s_bnd = sem("p_bounds")
            s_eq8 = sem("p_eq8")
            s_back = sem("p_back")
            s_flip = sem("p_flip")
            s_cnt = sem("p_cnt")
            s_st = sem("p_stored")
            s_eqst = sem("p_eq_stored")
            s_eqld = sem("p_eq_loaded")
            name = {k: sem("p_" + k) for k in ("pack", "row", "scanned", "carry")}
            name["n"], name["n_pe"] = [], []
            LT = NT - 1
            last_n = E - LT * P
            pl = P - 1
            pl_n = E - pl * EJ

            loads = []
            for k, a, sh in ((0, src, 0), (1, dst, 0), (3, dst, 1)):
                loads.append((ri[:, 0, k, :], a[sh:sh + P * P].rearrange("(p c) -> p c", c=P)))
                loads.append((ri[0:LT - P, 1, k, :], a[P * P + sh:LT * P + sh].rearrange("(p c) -> p c", c=P)))
                loads.append((ri[LT - P:NT - P, 1, k, 0:last_n - sh], a[LT * P + sh:E].rearrange("(a c) -> a c", a=1)))
            loads.append((ri[0:1, 0, 2, 1:P], dst[0:P - 1].rearrange("(a c) -> a c", a=1)))
            loads.append((ri[1:P, 0, 2, :], dst[P - 1:P * P - 1].rearrange("(p c) -> p c", c=P)))
            loads.append((ri[0:LT - P, 1, 2, :], dst[P * P - 1:LT * P - 1].rearrange("(p c) -> p c", c=P)))
            loads.append((ri[LT - P:NT - P, 1, 2, 0:last_n], dst[LT * P - 1:E - 1].rearrange("(a c) -> a c", a=1)))
            for k, sh in ((0, 0), (2, 1)):
                loads.append((pm_i[0:pl, k, :], dst[sh:pl * EJ + sh].rearrange("(p c) -> p c", c=EJ)))
                loads.append((pm_i[pl:P, k, 0:pl_n - sh], dst[pl * EJ + sh:E].rearrange("(a c) -> a c", a=1)))
            loads.append((pm_i[0:1, 1, 1:EJ], dst[0:EJ - 1].rearrange("(a c) -> a c", a=1)))
            loads.append((pm_i[1:pl, 1, :], dst[EJ - 1:pl * EJ - 1].rearrange("(p c) -> p c", c=EJ)))
            loads.append((pm_i[pl:P, 1, 0:pl_n + 1], dst[pl * EJ - 1:E].rearrange("(a c) -> a c", a=1)))

            weights = [(wraw[:, 2 * l + h, :], W1[l][h * D:(h + 1) * D, :]) for l in range(2) for h in range(2)]
            weights += [(w2[l][:, :], W2[l]) for l in range(2)]
            weights += [(wg_raw[:, :], W_gat), (wsk_raw[:, :], W_skip)]
            col = lambda v: v.rearrange("(p a) -> p a", a=1)
            rw = lambda v: v.rearrange("(a p) -> a p", a=1)
            for l in range(2):
                weights += [(b1c[l][:, :], col(b1[l])), (gc[l][:, :], col(ln_g[l])), (bc[l][:, :], col(ln_b[l])),
                            (b2r[l][:, :], rw(b2[l]))]
            weights += [(bias_r[:, :], rw(gat_bias)), (empty_bc[:, 0, :], rw(ln_b[1]).to_broadcast([P, D]))]
            for h in range(H):
                weights.append((att[h * C:(h + 1) * C, h:h + 1], att_src[h:h + 1, :].rearrange("a c -> c a")))
                weights.append((att[h * C:(h + 1) * C, H + h:H + h + 1], att_dst[h:h + 1, :].rearrange("a c -> c a")))

            with nc.Block() as block:
                @block.sync
                def _(eng):
                    eng.wait_ge(s_fill, 2)
                    for d, s in loads:
                        eng.dma_start(d, s).then_inc(s_rows, 16)
                    eng.wait_ge(s_bnd, 1)
                    eng.dma_start(bounds_d.rearrange("(p c) k -> p (c k)", p=P),
                                  bnd_i[:, :, :].rearrange("p c k -> p (c k)")).then_inc(s_st, 16)
                    eng.dma_start(seg1_d[EP:EP + 1, :], zrow[:, :]).then_inc(s_st, 16)
                    eng.dma_start(seg2_d[EP:EP + 1, :], zrow[:, :]).then_inc(s_st, 16)
                    eng.wait_ge(s_eq8, 1)
                    eng.dma_start(eq_d[0, 0:EP].rearrange("(p c) -> p c", c=EJ), eq8[:, :]).then_inc(s_eqst, 16)
                    eng.dma_start(eqr_d[0, :].rearrange("(p c) -> p c", c=EJ), eqr8[:, :]).then_inc(s_eqst, 16)
                    eng.wait_ge(s_eqst, 32)
                    eng.dma_start(eq_bc[:, :], eq_d.to_broadcast([P, EP])).then_inc(s_eqld, 16)
                    eng.dma_start(eqr_bc[:, :], eqr_d.to_broadcast([P, EP])).then_inc(s_eqld, 16)
                    eng.wait_ge(s_cnt, 1)
                    eng.dma_start(cnt_d[0, :].rearrange("(p c) -> p c", c=EJ), cntP[:, 0, :]).then_inc(s_st, 16)
                    eng.wait_ge(s_st, 64)
                    eng.wait_ge(s_eqld, 32)

                @block.scalar
                def _(eng):
                    eng.wait_ge(s_att0, 1)
                    with nc.allow_non_contiguous_dma(reason="vectors of 128 values, a value per partition"):
                        for d, s in weights:
                            eng.dma_start(d, s).then_inc(s_w, 16)
                    eng.wait_ge(s_w, 16 * len(weights))

                @block.gpsimd
                def _(eng):
                    eng.memset(ri[:, :, :, :], N).then_inc(s_fill, 1)
                    eng.memset(pm_i[:, :, :], N).then_inc(s_fill, 1)
                    eng.memset(att[:, :], 0.0).then_inc(s_att0, 1)
                    eng.iota(iota_i[:, :], [[1, NCOL]], base=0, channel_multiplier=0).then_inc(s_iota, 1)
                    eng.memset(zeros_h[:, :], 0.0).then_inc(s_iota, 1)
                    eng.memset(zrow[:, :], 0.0).then_inc(s_iota, 1)
                    eng.memset(ones_row[:, :], 1.0).then_inc(s_iota, 1)
                    eng.memset(onesP[:, :, :], 1.0).then_inc(s_iota, 1)
                    eng.memset(eps[:, :], EPS).then_inc(s_iota, 1)
                    eng.memset(ident[:, :], 0.0).then_inc(s_id, 1)
                    eng.memset(before[:, :], 1.0).then_inc(s_bef, 1)
                    eng.memset(spread_a[:, :], 1.0).then_inc(s_bef, 1)
                    eng.memset(spread_b[:, :], 1.0).then_inc(s_bef, 1)
                    eng.wait_ge(s_id, 1)
                    eng.affine_select(out=ident[:, :], in_=ident[:, :], compare_op=ALU.not_equal, fill=1.0,
                                      base=0, pattern=[[-1, P]], channel_multiplier=1).then_inc(s_id, 1)
                    eng.memset(flip[:, :], 0.0).then_inc(s_flip, 1)
                    eng.wait_ge(s_flip, 1)
                    eng.affine_select(out=flip[:, :], in_=flip[:, :], compare_op=ALU.not_equal, fill=1.0,
                                      base=1 - P, pattern=[[1, P]], channel_multiplier=1).then_inc(s_flip, 1)
                    eng.wait_ge(s_bef, 3)
                    eng.affine_select(out=before[:, :], in_=before[:, :], compare_op=ALU.is_gt, fill=0.0,
                                      base=0, pattern=[[1, P]], channel_multiplier=-1).then_inc(s_bef, 1)
                    for t, h0 in ((spread_a, 0), (spread_b, H)):
                        eng.affine_select(out=t[:, :], in_=t[:, :], compare_op=ALU.is_ge, fill=0.0,
                                          base=C * h0, pattern=[[1, D]], channel_multiplier=-C).then_inc(s_bef, 1)
                    eng.wait_ge(s_bef, 6)
                    for t, h0 in ((spread_a, 0), (spread_b, H)):
                        eng.affine_select(out=t[:, :], in_=t[:, :], compare_op=ALU.is_gt, fill=0.0,
                                          base=C - C * h0, pattern=[[-1, D]], channel_multiplier=C).then_inc(s_bef, 1)
                    eng.wait_ge(s_bef, 8)

                @block.vector
                def _(eng):
                    link = linker(eng, s_link)
                    eng.wait_ge(s_rows, 16 * len(loads))
                    eng.tensor_copy(rf[:, :, :, :], ri[:, :, :, :]).then_inc(s_rf, 1)
                    link(eng.tensor_copy(pm[:, :, :], pm_i[:, :, :]))
                    link(eng.tensor_tensor(eqP[:, :], pm[:, 0, :], pm[:, 1, :], ALU.is_equal))
                    link(eng.tensor_tensor(eqnP[:, :], pm[:, 0, :], pm[:, 2, :], ALU.is_equal))
                    eng.tensor_copy(eq8[:, :], eqP[:, :])
                    eng.tensor_copy(eqn_back[:, :], eqnP[:, ::-1]).then_inc(s_back, 1)
                    eng.wait_ge(s_flip, 3)
                    eng.tensor_copy(eqr8[:, :], pflip[:, 0:EJ]).then_inc(s_eq8, 1)
                    for k, m in enumerate((eqP, eqnP)):
                        rev = slice(None, None, -1) if k else slice(None)
                        link(eng.tensor_tensor_scan(out=lead[k][:, rev], data0=m[:, rev], data1=m[:, rev],
                                                    initial=1.0, op0=ALU.mult, op1=ALU.mult))
                        link(eng.tensor_scalar(neg_eq[k][:, :], m[:, :], 1.0, BIG, ALU.subtract, ALU.mult))
                        link(eng.tensor_scalar(neg_lead[k][:, :], lead[k][:, :], 1.0, BIG, ALU.subtract, ALU.mult))
                    eng.wait_ge(s_tile, 1)
                    link(eng.tensor_copy(tf[:, :, :], ptile[:, :, :]))
                    T = slice(0, NT)
                    link(eng.tensor_scalar(idx_sd[:, :, 0], tf[:, 0, T], float(N - 1), None, ALU.min))
                    link(eng.tensor_scalar(idx_sd[:, :, 1], tf[:, 1, T], float(N - 1), None, ALU.min))
                    link(eng.tensor_tensor(is_first[:, :], tf[:, 1, T], tf[:, 2, T], ALU.not_equal))
                    link(eng.tensor_tensor(is_last[:, :], tf[:, 1, T], tf[:, 3, T], ALU.not_equal))
                    link(eng.scalar_tensor_tensor(out=tf[:, 3, T], in0=tf[:, 1, T], scalar=float(2 * N),
                                                  in1=is_last[:, :], op0=ALU.subtract, op1=ALU.mult))
                    link(eng.tensor_scalar(idx_out[:, :], tf[:, 3, T], float(2 * N), None, ALU.add))
                    link(eng.tensor_copy(dst_i[:, :], tf[:, 1, T]))
                    link(eng.tensor_scalar(part_i[:, 0, :], dst_i[:, :], 9, None, ALU.logical_shift_right))
                    link(eng.tensor_scalar(part_i[:, 1, :], dst_i[:, :], NCOL - 1, None, ALU.bitwise_and))
                    link(eng.tensor_copy(part_f[:, :, :], part_i[:, :, :]))
                    eng.wait_ge(s_iota, 6)
                    link(eng.tensor_copy(iota_h[:, :], iota_i[:, :]))

                    def onehots(t, par, it):
                        if later(t):
                            eng.wait_ge(s_mm, t - RING + 1)
                        eng.tensor_scalar(onehot_p[:, par, :], iota_h[:, 0:P], part_f[:, 0, bass.ds(t, 1)],
                                          None, ALU.is_equal)
                        eng.tensor_scalar(onehot_c[:, par, :], iota_h[:, :], part_f[:, 1, bass.ds(t, 1)],
                                          None, ALU.is_equal).then_inc(s_oh, 1)
                    pipeline(eng, NT, [(0, onehots)])
                    eng.wait_ge(s_w, 16 * len(weights))
                    for l in range(2):
                        link(eng.tensor_copy(w1s[l][:, :], wraw[:, 2 * l + 1, :]))
                        link(eng.tensor_tensor(w1d[l][:, :], wraw[:, 2 * l, :], wraw[:, 2 * l + 1, :], ALU.subtract))
                    link(eng.scalar_tensor_tensor(out=empty_bc[:, 0, :], in0=empty_bc[:, 0, :], scalar=SLOPE,
                                                  in1=empty_bc[:, 0, :], op0=ALU.mult, op1=ALU.max))
                    eng.wait_ge(s_wT, 1)
                    link(eng.tensor_copy(wgT[:, :], pmisc[:, 0:D]))
                    link(eng.tensor_copy(wskT[:, :], pmisc[:, D:2 * D]))
                    link(eng.tensor_tensor(wsum[:, :], wgT[:, :], wskT[:, :], ALU.add))
                    s2 = pmisc[:, 2 * D:2 * D + 2 * H]
                    link(eng.tensor_copy(score_s[:, 0:H], s2[:, 0:H]))
                    link(eng.memset(score_s[:, H:2 * H], 0.0))
                    link(eng.tensor_copy(score_dd[:, 0:H], s2[:, H:2 * H]))
                    link(eng.tensor_tensor(score_dd[:, H:2 * H], s2[:, H:2 * H], score_s[:, 0:H], ALU.add))
                    eng.wait_ge(s_mm, NT + 1)
                    link(eng.tensor_copy(hist[:, :], phist[:, :]))
                    link(eng.tensor_tensor_scan(out=cum[:, :], data0=hist[:, :], data1=hist[:, :], initial=0.0,
                                                op0=ALU.add, op1=ALU.max))
                    eng.sem_inc(s_cum, 1)
                    eng.wait_ge(s_off, 1)
                    link(eng.tensor_copy(offs[:, :], psc[:, 256:257]))
                    link(eng.tensor_scalar(cum[:, :], cum[:, :], offs[:, 0:1], float(NONE), ALU.add, ALU.subtract))
                    link(eng.tensor_tensor(fl[:, 0, :], cum[:, :], hist[:, :], ALU.subtract))
                    link(eng.tensor_scalar(fl[:, 1, :], cum[:, :], 1.0, None, ALU.subtract))
                    link(eng.tensor_scalar(some[:, :], hist[:, :], 1.0, None, ALU.min))
                    for k in range(2):
                        link(eng.tensor_tensor(fl[:, k, :], fl[:, k, :], some[:, :], ALU.mult))
                        link(eng.tensor_scalar(bnd_i[:, :, k], fl[:, k, :], float(NONE), None, ALU.add))
                    eng.sem_inc(s_bnd, 1)
                    seg_dve(eng, link, 1, onesP, loc, pack, row, car, carry, psr, psc, name, False, cntP)
                    eng.sem_inc(s_cnt, 1)

                @block.tensor
                def _(eng):
                    eng.wait_ge(s_id, 2)
                    eng.wait_ge(s_back, 1)
                    eng.wait_ge(s_flip, 2)
                    eng.matmul(pflip[:, 0:EJ], flip[:, :], eqn_back[:, :], start=True, stop=True).then_inc(s_flip, 1)
                    eng.wait_ge(s_rf, 1)
                    for k in range(4):
                        for half in range(2):
                            last = eng.transpose(ptile[:, k, half * P:(half + 1) * P], rf[:, half, k, :], ident[:, :])
                    last.then_inc(s_tile, 1)
                    eng.wait_ge(s_iota, 6)
                    eng.matmul(phist[:, :], zeros_h[:, 0:P], zeros_h[:, :], start=True, stop=False)

                    def count(t, par, it):
                        eng.wait_ge(s_oh, t + 1)
                        eng.matmul(phist[:, :], onehot_p[:, par, :], onehot_c[:, par, :], start=False,
                                   stop=False).then_inc(s_mm, 1)
                    pipeline(eng, NT, [(0, count)])
                    eng.matmul(phist[:, :], zeros_h[:, 0:P], zeros_h[:, :], start=False, stop=True).then_inc(s_mm, 1)
                    eng.wait_ge(s_w, 16 * len(weights))
                    eng.transpose(pmisc[:, 0:D], wg_raw[:, :], ident[:, :])
                    eng.transpose(pmisc[:, D:2 * D], wsk_raw[:, :], ident[:, :])
                    eng.matmul(pmisc[:, 2 * D:2 * D + 2 * H], wg_raw[:, :], att[:, :], start=True,
                               stop=True).then_inc(s_wT, 1)
                    eng.wait_ge(s_bef, 8)
                    eng.wait_ge(s_cum, 1)
                    eng.matmul(psc[:, 256:257], before[:, :], cum[:, NCOL - 1:NCOL], start=True,
                               stop=True).then_inc(s_off, 1)
                    seg_pe(eng, 1, pack, car, psr, psc, name)

        end_stage()

        NF = N // GE
        tail = (N - NF * GE) // TG
        assert tail * TG + NF * GE == N and tail <= P
        with ExitStack() as pc:
            xt = sb("d_xt", [P, RING, TG, D], fp32, pc)
            x1 = sb("d_x1", [P, RING, TG, D], fp32, pc)
            xn = sb("d_xn", [P, RING, TG, D], fp32, pc)
            st = sb("d_st", [P, RING, TG, 6], fp32, pc)
            mv = sb("d_mv", [P, RING, TG, 2], fp32, pc)
            lnv, r0, hv, rr, rs = (sb("d_" + s, [P, RING, TG], fp32, pc) for s in ("lnv", "r0", "hv", "rr", "rs"))
            hT = sb("d_hT", [P, RING, GE], fp32, pc)
            neg = sb("d_neg", [P, RING, GE], fp32, pc)
            ex = sb("d_ex", [P, RING, GE], fp32, pc)
            yy = sb("d_yy", [P, RING, GE], fp32, pc)
            yo = sb("d_yo", [P, RING, TG, D], fp32, pc)
            bslot = sb("d_bslot", [P, RING, TG, 2], i32, pc)
            islot = sb("d_islot", [P, RING, TG], i32, pc)
            psT = [ps(f"d_psT{k}", [P, GE], pc) for k in range(RING)]
            psO = [ps(f"d_psO{k}", [P, GE], pc) for k in range(RING)]
            ld = [sem(f"d_ld{k}") for k in range(RING)]
            stored = [sem(f"d_stored{k}") for k in range(RING)]
            slot_set = [sem(f"d_slot_set{k}") for k in range(RING)]
            looked = [sem(f"d_looked{k}") for k in range(RING)]
            kept = [sem(f"d_kept{k}") for k in range(RING)]
            x1_ok, st_ok, mv_ok, hv_ok, lnv_ok, r0_ok, rs_ok, xn_ok, T_ok, h_ok, O_ok, neg_ok, ex_ok, yy_ok, yo_ok, pool_go = (
                sem("d_" + s) for s in ("x1_ok", "st_ok", "mv_ok", "hv_ok", "lnv_ok", "r0_ok", "rs_ok", "xn_ok", "T_ok",
                                        "h_ok", "O_ok", "neg_ok", "ex_ok", "yy_ok", "yo_ok", "pool_go"))
            ndone = NF + 1

            def npart(g):
                return tail if isinstance(g, int) and g == NF else P

            def node_rows(t, g):
                n = npart(g)
                return t[bass.ds(g * GE, n * TG), :].rearrange("(p j) f -> p j f", j=TG)

            with nc.Block() as block:
                @block.sync
                def _(eng):
                    def load(g, k, it):
                        n = npart(g)
                        if later(g):
                            eng.wait_ge(x1_ok, g - RING + 1)
                        eng.dma_start(xt[0:n, k, :, :], node_rows(x, g)).then_inc(ld[k], 16)

                    def store(g, k, it):
                        n = npart(g)
                        eng.wait_ge(yo_ok, g + 1)
                        eng.dma_start(node_rows(out, g), yo[0:n, k, :, :]).then_inc(stored[k], 16)
                    pipeline(eng, ndone, [(0, load), (3, store)])
                    for k in range(RING):
                        eng.wait_ge(stored[k], 16 * ((ndone + RING - 1 - k) // RING))

                @block.vector
                def _(eng):
                    def add_stats(g, k, it):
                        n = npart(g)
                        eng.wait_ge(ld[k], 16 * it)
                        eng.tensor_tensor(x1[0:n, k, :, :], xt[0:n, k, :, :],
                                          empty_bc[0:n, :, :].to_broadcast([n, TG, D]), ALU.add).then_inc(x1_ok, 1)
                        eng.wait_ge(x1_ok, g + 1)
                        for j in range(TG):
                            last = eng.bn_stats(st[0:n, k, j, :], x1[0:n, k, j, :])
                        last.then_inc(st_ok, 1)

                    def negative(g, k, it):
                        n = npart(g)
                        eng.wait_ge(st_ok, g + 4 if isinstance(g, int) and g + 4 <= ndone else (
                            ndone if isinstance(g, int) else g + 4))
                        eng.wait_ge(O_ok, g + 1)
                        eng.tensor_scalar(neg[0:n, k, :], psO[k][0:n, :], 0.0, None, ALU.min).then_inc(neg_ok, 1)

                    def aggregate(g, k, it):
                        n = npart(g)
                        if isinstance(g, int):
                            eng.wait_ge(st_ok, g + 1)
                        for j in range(TG):
                            last = eng.bn_aggr(mv[0:n, k, j, :], st[0:n, k, j, :])
                        last.then_inc(mv_ok, 1)
                        eng.wait_ge(mv_ok, g + 1)
                        eng.tensor_scalar(hv[0:n, k, :], mv[0:n, k, :, 1], EPS, -0.5, ALU.add, ALU.mult).then_inc(hv_ok, 1)

                    def normalise(g, k, it):
                        n = npart(g)
                        eng.wait_ge(r0_ok, g + 1)
                        eng.tensor_tensor(rr[0:n, k, :], r0[0:n, k, :], r0[0:n, k, :], ALU.mult).then_inc(rs_ok, 1)
                        eng.wait_ge(hv_ok, g + 1)
                        eng.wait_ge(rs_ok, 3 * g + 1)
                        eng.tensor_tensor(rr[0:n, k, :], rr[0:n, k, :], hv[0:n, k, :], ALU.mult).then_inc(rs_ok, 1)
                        eng.wait_ge(rs_ok, 3 * g + 2)
                        eng.scalar_tensor_tensor(out=rs[0:n, k, :], in0=rr[0:n, k, :], scalar=1.5, in1=r0[0:n, k, :],
                                                 op0=ALU.add, op1=ALU.mult).then_inc(rs_ok, 1)
                        if later(g):
                            eng.wait_ge(T_ok, g - RING + 1)
                        eng.wait_ge(rs_ok, 3 * g + 3)
                        for j in range(TG):
                            last = eng.tensor_scalar(xn[0:n, k, j, :], x1[0:n, k, j, :], mv[0:n, k, j, 0:1],
                                                     rs[0:n, k, j:j + 1], ALU.subtract, ALU.mult)
                        last.then_inc(xn_ok, 1)

                    def finish(g, k, it):
                        n = npart(g)
                        eng.wait_ge(ex_ok, g + 1)
                        eng.scalar_tensor_tensor(out=yy[0:n, k, :], in0=psO[k][0:n, :], scalar=0.0, in1=ex[0:n, k, :],
                                                 op0=ALU.max, op1=ALU.add).then_inc(yy_ok, 1)
                        eng.wait_ge(yy_ok, g + 1)
                        if later(g):
                            eng.wait_ge(stored[k], 16 * (it - 1))
                        eng.scalar_tensor_tensor(out=yo[0:n, k, :, :].rearrange("p j f -> p (j f)"), in0=yy[0:n, k, :],
                                                 scalar=-1.0, in1=x1[0:n, k, :, :].rearrange("p j f -> p (j f)"),
                                                 op0=ALU.add, op1=ALU.add).then_inc(yo_ok, 1)
                    pipeline(eng, ndone, [(0, add_stats), (3, negative), (0, aggregate), (1, normalise), (3, finish)])

                @block.tensor
                def _(eng):
                    def turn(g, k, it):
                        n = npart(g)
                        eng.wait_ge(xn_ok, g + 1)
                        if later(g):
                            eng.wait_ge(h_ok, g - RING + 1)
                        for j in range(TG):
                            last = eng.transpose(psT[k][:, j * P:j * P + n], xn[0:n, k, j, :], ident[0:n, 0:n])
                        last.then_inc(T_ok, 1)

                    def project(g, k, it):
                        n = npart(g)
                        eng.wait_ge(h_ok, g + 1)
                        if later(g):
                            eng.wait_ge(yy_ok, g - RING + 1)
                        for j in range(TG):
                            o = psO[k][0:n, j * D:(j + 1) * D]
                            eng.matmul(o, hT[:, k, j * P:j * P + n], wsum[:, :], start=True, stop=False)
                            last = eng.matmul(o, ones_row[:, 0:n], bias_r[:, :], start=False, stop=True)
                        last.then_inc(O_ok, 1)
                    pipeline(eng, ndone, [(2, project), (1, turn)])

                @block.scalar
                def _(eng):
                    def root(g, k, it):
                        n = npart(g)
                        eng.wait_ge(mv_ok, g + 1)
                        eng.activation(lnv[0:n, k, :], mv[0:n, k, :, 1], ACT.Ln, bias=eps[0:n, :]).then_inc(lnv_ok, 1)
                        eng.wait_ge(lnv_ok, g + 1)
                        eng.activation(r0[0:n, k, :], lnv[0:n, k, :], ACT.Exp, scale=-0.5).then_inc(r0_ok, 1)

                    def relu(g, k, it):
                        n = npart(g)
                        eng.wait_ge(T_ok, g + 1)
                        if later(g):
                            eng.wait_ge(O_ok, g - RING + 1)
                        v = lambda t: t.rearrange("p (j n) -> p j n", j=TG)[:, :, 0:n]
                        eng.activation(v(hT[:, k, :]), v(psT[k][:, :]), ACT.Relu).then_inc(h_ok, 1)

                    def expo(g, k, it):
                        n = npart(g)
                        eng.wait_ge(neg_ok, g + 1)
                        eng.activation(ex[0:n, k, :], neg[0:n, k, :], ACT.Exp).then_inc(ex_ok, 1)
                    eng.preload_act_table_set("natural_log_exp_and_others")
                    pipeline(eng, ndone, [(3, expo), (0, root), (1, relu)])

                @block.gpsimd
                def _(eng):
                    def look(g, k, it):
                        eng.tensor_copy(islot[:, k, :], idx_sd[:, bass.ds(g * TG, TG), 0]).then_inc(slot_set[k], 1)
                        eng.wait_ge(pool_go, 1)
                        eng.wait_ge(slot_set[k], it)
                        for j in range(TG):
                            eng.indirect_dma_start(bslot[:, k, j, :], None, bounds_d,
                                                   bass.IndirectOffsetOnAxis(islot[:, k, j:j + 1], 0)
                                                   ).then_inc(looked[k], 16)

                    def keep(g, k, it):
                        eng.wait_ge(looked[k], 16 * TG * it)
                        eng.tensor_copy(bnd[:, bass.ds(g * TG, TG), :], bslot[:, k, :, :]).then_inc(kept[k], 1)
                    eng.sem_inc(pool_go, 1)
                    pool_pipeline(eng, NG, look, keep)

        end_stage()

        def sems(prefix, names):
            return [sem(prefix + s) for s in names.split()]

        def ring_sems(name):
            return [sem(f"{name}{k}") for k in range(RING)]

        def used(g, depth):
            return not isinstance(g, int) or g >= depth

        def conv(l):
            pre = f"v{l}_"
            a = 1 - l
            rev = slice(None, None, -1) if l else slice(None)
            table = (seg1_d, seg2_d)[l]
            is_end = (is_last, is_first)[l]
            wd, ws, w2l = w1d[l], w1s[l], w2[l]

            def place(g):
                return g * -1 + (NG - 1) if l else g

            def mask(g):
                return (eqr_bc if l else eq_bc)[:, bass.ds(g * GE, GE)]

            with ExitStack() as pc:
                if l == 0:
                    xg = sb(pre + "xg", [P, RING, TG, 2, D], fp32, pc)
                    xn = sb(pre + "xn", [P, RING, TG, 2, D], fp32, pc)
                    st = sb(pre + "st", [P, RING, TG, 2, 6], fp32, pc)
                    mv = sb(pre + "mv", [P, RING, TG, 2, 2], fp32, pc)
                    sd = sb(pre + "sd", [P, RING, TG, 2], fp32, pc)
                    rs = sb(pre + "rs", [P, RING, TG, 2], fp32, pc)
                    islot = sb(pre + "islot", [P, RING, TG, 2], i32, pc)
                else:
                    zg = sb(pre + "zg", [P, RING, TG, D], fp32, pc)
                    zd = sb(pre + "zd", [P, RING, TG, D], fp32, pc)
                    spread = sb(pre + "spread", [P, RING, GE], fp32, pc)
                    islot = sb(pre + "islot", [P, RING, TG], i32, pc)
                hx = sb(pre + "hx", [P, RING, 2, GE], fp32, pc)
                hid = sb(pre + "hid", [P, RING, GE], fp32, pc)
                run = sb(pre + "run", [P, RING, GE], fp32, pc)
                zst = sb(pre + "zst", [P, RING, TG, 6], fp32, pc)
                zmv = sb(pre + "zmv", [P, RING, TG, 2], fp32, pc)
                zsd = sb(pre + "zsd", [P, RING, TG], fp32, pc)
                zrs = sb(pre + "zrs", [P, RING, TG], fp32, pc)
                zsc = sb(pre + "zsc", [P, RING, TG], fp32, pc)
                zof = sb(pre + "zof", [P, RING, TG], fp32, pc)
                zr = sb(pre + "zr", [P, RING, TG, D], fp32, pc)
                cnt = sb(pre + "cnt", [1, RING, GE], fp32, pc)
                psS = ps(pre + "psS", [P, GE], pc)
                psD = ps(pre + "psD", [P, GE], pc)
                psM = [ps(pre + f"psM{k}", [P, GE], pc) for k in range(2)]
                psZ = [ps(pre + f"psZ{k}", [P, GE], pc) for k in range(RING)]
                (st_ok, mv_ok, sd_ok, rs_ok, xn_ok, T_ok, hS_ok, spread_ok, hD_ok, h_ok, M_ok, hid_ok, bent_ok, run_ok, Z_ok, zst_ok,
                 zmv_ok, zsd_ok, zsc_ok, zr_ok, pool_go) = sems(
                    pre, "st_ok mv_ok sd_ok rs_ok xn_ok T_ok hS_ok spread_ok hD_ok h_ok M_ok hid_ok bent_ok run_ok Z_ok zst_ok "
                    "zmv_ok zsd_ok zsc_ok zr_ok pool_go")
                slot_set, free, got, raw, cld, stored = (ring_sems(pre + s) for s in (
                    "slot_set", "free", "got", "raw", "cnt_ld", "stored"))

                with nc.Block() as block:
                    @block.gpsimd
                    def _(eng):
                        def gather(g, k, it):
                            eng.wait_ge(free[k], it)
                            if l == 0:
                                eng.tensor_copy(islot[:, k, :, :], idx_sd[:, bass.ds(g * TG, TG), :]).then_inc(slot_set[k], 1)
                            else:
                                eng.tensor_copy(islot[:, k, :], bnd[:, bass.ds(place(g) * TG, TG), 1]).then_inc(slot_set[k], 1)
                            eng.wait_ge(pool_go, 1)
                            eng.wait_ge(slot_set[k], it)
                            for j in range(TG):
                                if l == 0:
                                    for side in range(2):
                                        eng.indirect_dma_start(
                                            xg[:, k, j, side, :], None, x,
                                            bass.IndirectOffsetOnAxis(islot[:, k, j, side:side + 1], 0)).then_inc(got[k], 16)
                                else:
                                    eng.indirect_dma_start(
                                        zg[:, k, j, :], None, seg1_d,
                                        bass.IndirectOffsetOnAxis(islot[:, k, j:j + 1], 0)).then_inc(got[k], 16)
                        eng.sem_inc(pool_go, 1)
                        pool_pipeline(eng, NG, gather)

                    @block.sync
                    def _(eng):
                        def move_in(g, k, it):
                            if later(g):
                                eng.wait_ge(Z_ok, g - RING + 1)
                            eng.dma_start(cnt[:, k, :], cnt_d[:, bass.ds(place(g) * GE, GE)]).then_inc(cld[k], 16)
                            if l == 0:
                                eng.wait_ge(got[k], 32 * TG * it)
                                eng.dma_start(tile_rows(xs_d, g), xg[:, k, :, 0, :]).then_inc(raw[k], 16)
                                eng.dma_start(tile_rows(xd_d, g), xg[:, k, :, 1, :]).then_inc(raw[k], 16)
                            else:
                                if later(g):
                                    eng.wait_ge(T_ok, g - RING + 1)
                                eng.dma_start(zd[:, k, :, :], tile_rows(seg1_d, place(g))).then_inc(raw[k], 16)

                        def release(g, k, it):
                            if l == 0:
                                eng.wait_ge(raw[k], 32 * it)
                                eng.wait_ge(xn_ok, g + 1)
                            else:
                                eng.wait_ge(T_ok, g + 1)
                            eng.sem_inc(free[k], 1)

                        def store(g, k, it):
                            eng.wait_ge(zr_ok, g + 1)
                            eng.dma_start(tile_rows(table, place(g)), zr[:, k, :, :]).then_inc(stored[k], 16)
                        for k in range(RING):
                            eng.sem_inc(free[k], 1)
                        pipeline(eng, NG, [(0, move_in), (a, release), (a + 4, store)])
                        for k in range(RING):
                            eng.wait_ge(stored[k], 16 * ((NG + RING - 1 - k) // RING))

                    @block.vector
                    def _(eng):
                        def x_stats(g, k, it):
                            eng.wait_ge(got[k], 32 * TG * it)
                            for j in range(TG):
                                for side in range(2):
                                    last = eng.bn_stats(st[:, k, j, side, :], xg[:, k, j, side, :])
                            last.then_inc(st_ok, 1)

                        def z_stats(g, k, it):
                            eng.wait_ge(Z_ok, g + 1)
                            for j in range(TG):
                                last = eng.bn_stats(zst[:, k, j, :], psZ[k][:, j * D:(j + 1) * D])
                            last.then_inc(zst_ok, 1)

                        def add_up(g, k, it):
                            if not isinstance(g, int):
                                eng.wait_ge(zst_ok, g)
                                if l == 0:
                                    eng.wait_ge(st_ok, g + a + 3)
                            if later(g):
                                eng.wait_ge(Z_ok, g - RING + 1)
                            eng.wait_ge(hid_ok, g + 1)
                            eng.scalar_tensor_tensor(out=hid[:, k, :], in0=hid[:, k, :], scalar=SLOPE, in1=hid[:, k, :],
                                                     op0=ALU.mult, op1=ALU.max).then_inc(bent_ok, 1)
                            if used(g, 1):
                                eng.wait_ge(run_ok, g)
                            eng.wait_ge(bent_ok, g + 1)
                            end = 0 if l else GE - 1
                            eng.tensor_tensor_scan(
                                out=run[:, k, rev], data0=mask(g), data1=hid[:, k, rev],
                                initial=run[:, (k - 1) % RING, end:end + 1] if used(g, 1) else 0.0,
                                op0=ALU.mult, op1=ALU.add).then_inc(run_ok, 1)

                        def x_aggregate(g, k, it):
                            if isinstance(g, int):
                                eng.wait_ge(st_ok, g + 1)
                            for j in range(TG):
                                for side in range(2):
                                    last = eng.bn_aggr(mv[:, k, j, side, :], st[:, k, j, side, :])
                            last.then_inc(mv_ok, 1)

                        def z_aggregate(g, k, it):
                            if isinstance(g, int):
                                eng.wait_ge(zst_ok, g + 1)
                            for j in range(TG):
                                last = eng.bn_aggr(zmv[:, k, j, :], zst[:, k, j, :])
                            last.then_inc(zmv_ok, 1)

                        def normalise(g, k, it):
                            eng.wait_ge(sd_ok, g + 1)
                            eng.reciprocal(rs[:, k, :, :], sd[:, k, :, :]).then_inc(rs_ok, 1)
                            if later(g):
                                eng.wait_ge(T_ok, g - RING + 1)
                            eng.wait_ge(rs_ok, g + 1)
                            for j in range(TG):
                                for side in range(2):
                                    last = eng.tensor_scalar(xn[:, k, j, side, :], xg[:, k, j, side, :],
                                                             mv[:, k, j, side, 0:1], rs[:, k, j, side:side + 1],
                                                             ALU.subtract, ALU.mult)
                            last.then_inc(xn_ok, 1)

                        def bend(g, k, it):
                            eng.wait_ge(hS_ok, g + 1)
                            eng.wait_ge(hD_ok, g + 1)
                            eng.scalar_tensor_tensor(out=hx[:, k, :, :], in0=hx[:, k, :, :], scalar=SLOPE,
                                                     in1=hx[:, k, :, :], op0=ALU.mult, op1=ALU.max).then_inc(h_ok, 1)

                        def hand_on(g, k, it):
                            if later(g):
                                eng.wait_ge(hD_ok, g - RING + 1)
                            if used(g, 1):
                                eng.wait_ge(spread_ok, g)
                            eng.wait_ge(T_ok, g + 1)
                            eng.tensor_tensor_scan(
                                out=spread[:, k, rev], data0=mask(g), data1=psD[:, rev],
                                initial=spread[:, (k - 1) % RING, 0:1] if used(g, 1) else 0.0,
                                op0=ALU.mult, op1=ALU.add).then_inc(spread_ok, 1)

                        def z_scales(g, k, it):
                            eng.wait_ge(zsd_ok, g + 1)
                            eng.reciprocal(zrs[:, k, :], zsd[:, k, :]).then_inc(zsc_ok, 1)
                            if later(g):
                                eng.wait_ge(zr_ok, g - RING + 1)
                            eng.wait_ge(zsc_ok, 3 * g + 1)
                            eng.tensor_tensor(zsc[:, k, :], zrs[:, k, :], is_end[:, bass.ds(place(g) * TG, TG)],
                                              ALU.mult).then_inc(zsc_ok, 1)
                            eng.wait_ge(zsc_ok, 3 * g + 2)
                            eng.scalar_tensor_tensor(out=zof[:, k, :], in0=zmv[:, k, :, 0], scalar=-1.0, in1=zsc[:, k, :],
                                                     op0=ALU.mult, op1=ALU.mult).then_inc(zsc_ok, 1)
                        if l == 0:
                            pipeline(eng, NG, [(0, x_stats), (4, z_stats), (3, add_up), (0, x_aggregate),
                                               (4, z_aggregate), (1, normalise), (5, z_scales)])
                        else:
                            pipeline(eng, NG, [(1, bend), (3, z_stats), (2, add_up), (3, z_aggregate), (0, hand_on), (4, z_scales)])

                    @block.tensor
                    def _(eng):
                        def turn(g, k, it):
                            if used(g, 1):
                                if l == 0:
                                    eng.wait_ge(h_ok, g)
                                else:
                                    eng.wait_ge(hS_ok, g)
                                    eng.wait_ge(spread_ok, g)
                            if l == 0:
                                eng.wait_ge(xn_ok, g + 1)
                            else:
                                eng.wait_ge(raw[k], 16 * it)
                                eng.wait_ge(got[k], 16 * TG * it)
                            for j in range(TG):
                                c = slice(j * P, (j + 1) * P)
                                eng.transpose(psS[:, c], xn[:, k, j, 0, :] if l == 0 else zg[:, k, j, :], ident[:, :])
                                last = eng.transpose(psD[:, c], xn[:, k, j, 1, :] if l == 0 else zd[:, k, j, :], ident[:, :])
                            last.then_inc(T_ok, 1)

                        def hidden(g, k, it):
                            if used(g, 2):
                                eng.wait_ge(hid_ok, g - 1)
                            eng.wait_ge(h_ok, g + 1)
                            eng.matmul(psM[k % 2][:, :], ws[:, :], hx[:, k, 0, :], start=True, stop=False)
                            eng.matmul(psM[k % 2][:, :], wd[:, :], hx[:, k, 1, :], start=False, stop=True).then_inc(M_ok, 1)

                        def second(g, k, it):
                            if later(g):
                                eng.wait_ge(zr_ok, g - RING + 1)
                            eng.wait_ge(cld[k], 16 * it)
                            eng.wait_ge(run_ok, g + 1)
                            for j in range(TG):
                                o = psZ[k][:, j * D:(j + 1) * D]
                                c = slice(j * P, (j + 1) * P)
                                eng.matmul(o, run[:, k, c], w2l[:, :], start=True, stop=False)
                                last = eng.matmul(o, cnt[0:1, k, c], b2r[l][:, :], start=False, stop=True)
                            last.then_inc(Z_ok, 1)
                        pipeline(eng, NG, [(a + 1, hidden), (a, turn), (a + 2, second)])

                    @block.scalar
                    def _(eng):
                        def x_root(g, k, it):
                            eng.wait_ge(mv_ok, g + 1)
                            eng.activation(sd[:, k, :, :], mv[:, k, :, :, 1], ACT.Sqrt, bias=eps[:, :]).then_inc(sd_ok, 1)

                        def inputs(g, k, it):
                            if later(g):
                                eng.wait_ge(M_ok, g - RING + 1)
                            eng.wait_ge(T_ok, g + 1)
                            if l == 0:
                                eng.activation(hx[:, k, 0, :], psS[:, :], ACT.Relu)
                                eng.activation(hx[:, k, 1, :], psD[:, :], ACT.Relu).then_inc(h_ok, 1)
                            else:
                                eng.activation(hx[:, k, 0, :], psS[:, :], ACT.Identity, bias=bc[0][:, :],
                                               scale=gc[0][:, :]).then_inc(hS_ok, 1)
                                eng.wait_ge(spread_ok, g + 1)
                                eng.activation(hx[:, k, 1, :], spread[:, k, :], ACT.Identity, bias=bc[0][:, :],
                                               scale=gc[0][:, :]).then_inc(hD_ok, 1)

                        def biased(g, k, it):
                            if later(g):
                                eng.wait_ge(run_ok, g - RING + 1)
                            eng.wait_ge(M_ok, g + 1)
                            eng.activation(hid[:, k, :], psM[k % 2][:, :], ACT.Identity, bias=b1c[l][:, :]).then_inc(hid_ok, 1)

                        def z_root(g, k, it):
                            eng.wait_ge(zmv_ok, g + 1)
                            eng.activation(zsd[:, k, :], zmv[:, k, :, 1], ACT.Sqrt, bias=eps[:, :]).then_inc(zsd_ok, 1)

                        def z_normalise(g, k, it):
                            if later(g):
                                eng.wait_ge(stored[k], 16 * (it - 1))
                            eng.wait_ge(zsc_ok, 3 * g + 3)
                            for j in range(TG):
                                last = eng.activation(zr[:, k, j, :], psZ[k][:, j * D:(j + 1) * D], ACT.Identity,
                                                      bias=zof[:, k, j:j + 1], scale=zsc[:, k, j:j + 1])
                            last.then_inc(zr_ok, 1)
                        work = [(a + 1, biased), (a, inputs), (a + 3, z_root), (a + 4, z_normalise)]
                        pipeline(eng, NG, [(0, x_root)] + work if l == 0 else work)

        conv(0)
        end_stage()
        conv(1)
        end_stage()

        with ExitStack() as pc:
            zg = sb("a_zg", [P, RING, TG, D], fp32, pc)
            zd = sb("a_zd", [P, RING, TG, D], fp32, pc)
            xr = sb("a_xr", [P, RING, 2, TG, D], fp32, pc)
            x1 = sb("a_x1", [P, RING, 2, TG, D], fp32, pc)
            hh = sb("a_hh", [P, 2, 2, GE], fp32, pc)
            spread = sb("a_spread", [P, RING, GE], fp32, pc)
            st = sb("a_st", [P, RING, 2, TG, 6], fp32, pc)
            mv = sb("a_mv", [P, RING, 2, TG, 2], fp32, pc)
            sd = sb("a_sd", [P, RING, 2, TG], fp32, pc)
            rs = sb("a_rs", [P, RING, 2, TG], fp32, pc)
            xn = sb("a_xn", [P, 2, 2, TG, D], fp32, pc)
            q = sb("a_q", [P, RING, 2, GE], fp32, pc)
            pt = sb("a_pt", [P, RING, GE], fp32, pc)
            sc = sb("a_sc", [2 * H, RING, GE], fp32, pc)
            islot = sb("a_islot", [P, RING, TG], i32, pc)
            psA = [ps(f"a_psA{k}", [P, GE], pc) for k in range(2)]
            psR = [ps(f"a_psR{k}", [P, GE], pc) for k in range(2)]
            psQ = [ps(f"a_psQ{k}", [P, GE], pc) for k in range(2)]
            psP = ps("a_psP", [P, GE], pc)
            psC = ps("a_psC", [2 * H, GE], pc)
            (T_ok, hS_ok, spread_ok, hD_ok, h_ok, R_ok, x1_ok, st_ok, mv_ok, sd_ok, rs_ok, xn_ok, Q_ok, q_ok, P_ok, pt_ok,
             sc_ok, pool_go) = sems("a_", "T_ok hS_ok spread_ok hD_ok h_ok R_ok x1_ok st_ok mv_ok sd_ok rs_ok xn_ok Q_ok q_ok "
                                    "P_ok pt_ok sc_ok pool_go")
            slot_set, free, got, zld, xld, x1_st, q_st, p_st = (ring_sems("a_" + s) for s in (
                "slot_set", "free", "got", "zd_ld", "x_ld", "x1_st", "q_st", "p_st"))

            with nc.Block() as block:
                @block.gpsimd
                def _(eng):
                    def gather(g, k, it):
                        eng.wait_ge(free[k], it)
                        eng.tensor_copy(islot[:, k, :], bnd[:, bass.ds(g * TG, TG), 0]).then_inc(slot_set[k], 1)
                        eng.wait_ge(pool_go, 1)
                        eng.wait_ge(slot_set[k], it)
                        for j in range(TG):
                            eng.indirect_dma_start(zg[:, k, j, :], None, seg2_d,
                                                   bass.IndirectOffsetOnAxis(islot[:, k, j:j + 1], 0)).then_inc(got[k], 16)
                    eng.sem_inc(pool_go, 1)
                    pool_pipeline(eng, NG, gather)

                @block.sync
                def _(eng):
                    def load(g, k, it):
                        if later(g):
                            eng.wait_ge(T_ok, g - RING + 1)
                        eng.dma_start(zd[:, k, :, :], tile_rows(seg2_d, g)).then_inc(zld[k], 16)
                        if later(g):
                            eng.wait_ge(x1_ok, g - RING + 1)
                        eng.dma_start(xr[:, k, 0, :, :], tile_rows(xs_d, g)).then_inc(xld[k], 16)
                        eng.dma_start(xr[:, k, 1, :, :], tile_rows(xd_d, g)).then_inc(xld[k], 16)

                    def release(g, k, it):
                        eng.wait_ge(T_ok, g + 1)
                        eng.sem_inc(free[k], 1)

                    def store_x1(g, k, it):
                        eng.wait_ge(x1_ok, g + 1)
                        eng.dma_start(tile_rows(x1_d, g), x1[:, k, 1, :, :]).then_inc(x1_st[k], 16)

                    def store(g, k, it):
                        eng.wait_ge(q_ok, g + 1)
                        eng.wait_ge(pt_ok, g + 1)
                        eng.wait_ge(sc_ok, g + 1)
                        eng.dma_start(hdT_d[bass.ds(g, 1), :, :].rearrange("a p n -> (a p) n"), q[:, k, 1, :]).then_inc(q_st[k], 16)
                        eng.dma_start(pT_d[bass.ds(g, 1), :, :].rearrange("a p n -> (a p) n"), pt[:, k, :]).then_inc(p_st[k], 16)
                        eng.dma_start(score_d[:, bass.ds(g * GE, GE)], sc[:, k, :]).then_inc(p_st[k], 16)
                    for k in range(RING):
                        eng.sem_inc(free[k], 1)
                    pipeline(eng, NG, [(0, load), (0, release), (1, store_x1), (3, store)])
                    for k in range(RING):
                        n = (NG + RING - 1 - k) // RING
                        eng.wait_ge(x1_st[k], 16 * n)
                        eng.wait_ge(q_st[k], 16 * n)
                        eng.wait_ge(p_st[k], 32 * n)

                @block.vector
                def _(eng):
                    def bend(g, k, it):
                        eng.wait_ge(hS_ok, g + 1)
                        eng.wait_ge(hD_ok, g + 1)
                        eng.scalar_tensor_tensor(out=hh[:, k % 2, :, :], in0=hh[:, k % 2, :, :], scalar=SLOPE,
                                                 in1=hh[:, k % 2, :, :], op0=ALU.mult, op1=ALU.max).then_inc(h_ok, 1)

                    def add_x(g, k, it):
                        eng.wait_ge(xld[k], 32 * it)
                        if later(g):
                            eng.wait_ge(x1_st[k], 16 * (it - 1))
                            eng.wait_ge(xn_ok, g - RING + 1)
                        eng.wait_ge(R_ok, g + 1)
                        f = lambda t, side: t[:, k, side, :, :].rearrange("p j f -> p (j f)")
                        eng.tensor_tensor(f(x1, 0), psR[0][:, :], f(xr, 0), ALU.add)
                        eng.tensor_tensor(f(x1, 1), psR[1][:, :], f(xr, 1), ALU.add).then_inc(x1_ok, 1)
                        eng.wait_ge(x1_ok, g + 1)
                        for side in range(2):
                            for j in range(TG):
                                last = eng.bn_stats(st[:, k, side, j, :], x1[:, k, side, j, :])
                        last.then_inc(st_ok, 1)

                    def hand_on(g, k, it):
                        if not isinstance(g, int):
                            eng.wait_ge(st_ok, g)
                        if later(g):
                            eng.wait_ge(hD_ok, g - RING + 1)
                        if used(g, 1):
                            eng.wait_ge(spread_ok, g)
                        eng.wait_ge(T_ok, g + 1)
                        eng.tensor_tensor_scan(
                            out=spread[:, k, :], data0=eq_bc[:, bass.ds(g * GE, GE)], data1=psA[1][:, :],
                            initial=spread[:, (k - 1) % RING, GE - 1:GE] if used(g, 1) else 0.0,
                            op0=ALU.mult, op1=ALU.add).then_inc(spread_ok, 1)

                    def aggregate(g, k, it):
                        if isinstance(g, int):
                            eng.wait_ge(st_ok, g + 1)
                        for side in range(2):
                            for j in range(TG):
                                last = eng.bn_aggr(mv[:, k, side, j, :], st[:, k, side, j, :])
                        last.then_inc(mv_ok, 1)

                    def normalise(g, k, it):
                        eng.wait_ge(sd_ok, g + 1)
                        eng.reciprocal(rs[:, k, :, :], sd[:, k, :, :]).then_inc(rs_ok, 1)
                        if used(g, 2):
                            eng.wait_ge(Q_ok, g - 1)
                        eng.wait_ge(rs_ok, g + 1)
                        for side in range(2):
                            for j in range(TG):
                                last = eng.tensor_scalar(xn[:, k % 2, side, j, :], x1[:, k, side, j, :],
                                                         mv[:, k, side, j, 0:1], rs[:, k, side, j:j + 1],
                                                         ALU.subtract, ALU.mult)
                        last.then_inc(xn_ok, 1)
                    pipeline(eng, NG, [(1, bend), (1, add_x), (0, hand_on), (1, aggregate), (2, normalise)])

                @block.tensor
                def _(eng):
                    def turn(g, k, it):
                        if used(g, 1):
                            eng.wait_ge(hS_ok, g)
                            eng.wait_ge(spread_ok, g)
                        eng.wait_ge(zld[k], 16 * it)
                        eng.wait_ge(got[k], 16 * TG * it)
                        for j in range(TG):
                            eng.transpose(psA[0][:, j * P:(j + 1) * P], zg[:, k, j, :], ident[:, :])
                            last = eng.transpose(psA[1][:, j * P:(j + 1) * P], zd[:, k, j, :], ident[:, :])
                        last.then_inc(T_ok, 1)

                    def rows(g, k, it):
                        if used(g, 1):
                            eng.wait_ge(x1_ok, g)
                        eng.wait_ge(h_ok, g + 1)
                        for side in range(2):
                            for j in range(TG):
                                last = eng.transpose(psR[side][:, j * D:(j + 1) * D], hh[:, k % 2, side, j * P:(j + 1) * P],
                                                     ident[:, :])
                        last.then_inc(R_ok, 1)

                    def turn_again(g, k, it):
                        if used(g, 1):
                            eng.wait_ge(q_ok, g)
                        eng.wait_ge(xn_ok, g + 1)
                        for side in range(2):
                            for j in range(TG):
                                last = eng.transpose(psQ[side][:, j * P:(j + 1) * P], xn[:, k % 2, side, j, :], ident[:, :])
                        last.then_inc(Q_ok, 1)

                    def project(g, k, it):
                        if used(g, 1):
                            eng.wait_ge(pt_ok, g)
                            eng.wait_ge(sc_ok, g)
                        eng.wait_ge(q_ok, g + 1)
                        eng.matmul(psP[:, :], wgT[:, :], q[:, k, 0, :], start=True, stop=True)
                        eng.matmul(psC[:, :], score_s[:, :], q[:, k, 0, :], start=True, stop=False)
                        eng.matmul(psC[:, :], score_dd[:, :], q[:, k, 1, :], start=False, stop=True).then_inc(P_ok, 1)
                    pipeline(eng, NG, [(1, rows), (0, turn), (3, project), (2, turn_again)])

                @block.scalar
                def _(eng):
                    def affine_s(g, k, it):
                        if used(g, 2):
                            eng.wait_ge(R_ok, g - 1)
                        eng.wait_ge(T_ok, g + 1)
                        eng.activation(hh[:, k % 2, 0, :], psA[0][:, :], ACT.Identity, bias=bc[1][:, :],
                                       scale=gc[1][:, :]).then_inc(hS_ok, 1)

                    def affine_d(g, k, it):
                        eng.wait_ge(spread_ok, g + 1)
                        eng.activation(hh[:, k % 2, 1, :], spread[:, k, :], ACT.Identity, bias=bc[1][:, :],
                                       scale=gc[1][:, :]).then_inc(hD_ok, 1)

                    def root(g, k, it):
                        eng.wait_ge(mv_ok, g + 1)
                        eng.activation(sd[:, k, :, :], mv[:, k, :, :, 1], ACT.Sqrt, bias=eps[:, :]).then_inc(sd_ok, 1)

                    def relu(g, k, it):
                        if later(g):
                            eng.wait_ge(P_ok, g - RING + 1)
                            eng.wait_ge(q_st[k], 16 * (it - 1))
                        eng.wait_ge(Q_ok, g + 1)
                        eng.activation(q[:, k, 0, :], psQ[0][:, :], ACT.Relu)
                        eng.activation(q[:, k, 1, :], psQ[1][:, :], ACT.Relu).then_inc(q_ok, 1)

                    def scores(g, k, it):
                        if later(g):
                            eng.wait_ge(p_st[k], 32 * (it - 1))
                        eng.wait_ge(P_ok, g + 1)
                        eng.activation(pt[:, k, :], psP[:, :], ACT.Copy).then_inc(pt_ok, 1)
                        eng.activation(sc[:, k, :], psC[:, :], ACT.Copy).then_inc(sc_ok, 1)
                    pipeline(eng, NG, [(0, affine_s), (3, scores), (1, root), (0, affine_d), (2, relu)])

        end_stage()

        with ExitStack() as pc:
            se = sb("s_se", [P, H, EJ], fp32, pc)
            sl = sb("s_sl", [P, H, EJ], fp32, pc)
            mx = sb("s_mx", [P, H, EJ], fp32, pc)
            sm = sb("s_sm", [P, H, EJ], fp32, pc)
            loc = [sb(f"s_loc{k}", [P, H, EJ], fp32, pc) for k in range(2)]
            pack = sb("s_pack", [P, 2 * H], fp32, pc)
            row = sb("s_row", [H, 2 * P], fp32, pc)
            car = sb("s_car", [H, P + 1], fp32, pc)
            carry = sb("s_carry", [P, H], fp32, pc)
            psr = ps("s_psr", [P, 512], pc)
            psc = ps("s_psc", [P, 512], pc)
            s_ld, s_link, s_arg, s_exp, s_al, s_st = sems("s_", "ld link arg exp al st")
            name = {k: sem("s_" + k) for k in ("pack", "row", "scanned", "carry")}
            name["n"], name["n_pe"] = [], []

            def by_partition(t, h):
                return t[h:h + 1, :].rearrange("a (p c) -> (a p) c", c=EJ)

            with nc.Block() as block:
                @block.sync
                def _(eng):
                    for h in range(H):
                        eng.dma_start(se[:, h, :], by_partition(score_d, h)).then_inc(s_ld, 16)
                        eng.dma_start(sl[:, h, :], by_partition(score_d, H + h)).then_inc(s_ld, 16)
                    eng.wait_ge(s_al, 1)
                    for h in range(H):
                        eng.dma_start(by_partition(alpha_d, h), se[:, h, :]).then_inc(s_st, 16)
                        eng.dma_start(by_partition(alpha_d, H + h), sl[:, h, :]).then_inc(s_st, 16)
                    eng.wait_ge(s_st, 32 * H)

                @block.vector
                def _(eng):
                    link = linker(eng, s_link)
                    eng.wait_ge(s_ld, 32 * H)
                    for t in (se, sl):
                        link(eng.scalar_tensor_tensor(out=t[:, :, :], in0=t[:, :, :], scalar=GAT_SLOPE, in1=t[:, :, :],
                                                      op0=ALU.mult, op1=ALU.max))
                    seg_dve(eng, link, H, se, loc, pack, row, car, carry, psr, psc, name, True, mx)
                    link(eng.tensor_tensor(mx[:, :, :], mx[:, :, :], sl[:, :, :], ALU.max))
                    link(eng.tensor_tensor(se[:, :, :], se[:, :, :], mx[:, :, :], ALU.subtract))
                    link(eng.tensor_tensor(sl[:, :, :], sl[:, :, :], mx[:, :, :], ALU.subtract))
                    eng.sem_inc(s_arg, 1)
                    eng.wait_ge(s_exp, 2)
                    seg_dve(eng, link, H, se, loc, pack, row, car, carry, psr, psc, name, False, sm)
                    link(eng.scalar_tensor_tensor(out=sm[:, :, :], in0=sm[:, :, :], scalar=1e-16, in1=sl[:, :, :],
                                                  op0=ALU.add, op1=ALU.add))
                    link(eng.reciprocal(sm[:, :, :], sm[:, :, :]))
                    link(eng.tensor_tensor(se[:, :, :], se[:, :, :], sm[:, :, :], ALU.mult))
                    link(eng.tensor_tensor(sl[:, :, :], sl[:, :, :], sm[:, :, :], ALU.mult))
                    eng.sem_inc(s_al, 1)

                @block.tensor
                def _(eng):
                    for _ in range(2):
                        seg_pe(eng, H, pack, car, psr, psc, name)

                @block.scalar
                def _(eng):
                    eng.wait_ge(s_arg, 1)
                    eng.activation(se[:, :, :], se[:, :, :], ACT.Exp).then_inc(s_exp, 1)
                    eng.activation(sl[:, :, :], sl[:, :, :], ACT.Exp).then_inc(s_exp, 1)

        end_stage()

        with ExitStack() as pc:
            qd = sb("b_qd", [P, RING, GE], fp32, pc)
            pt = sb("b_pt", [P, RING, GE], fp32, pc)
            x1 = sb("b_x1", [P, RING, TG, D], fp32, pc)
            al = sb("b_al", [2 * H, RING, GE], fp32, pc)
            wl = sb("b_wl", [P, RING, GE], fp32, pc)
            msg = sb("b_msg", [P, RING, GE], fp32, pc)
            own = sb("b_own", [P, RING, GE], fp32, pc)
            run = sb("b_run", [P, RING, GE], fp32, pc)
            agg = sb("b_agg", [P, RING, GE], fp32, pc)
            neg = sb("b_neg", [P, RING, GE], fp32, pc)
            ex = sb("b_ex", [P, RING, GE], fp32, pc)
            yy = sb("b_yy", [P, RING, GE], fp32, pc)
            yo = sb("b_yo", [P, RING, TG, D], fp32, pc)
            islot = sb("b_islot", [P, RING, TG], i32, pc)
            psE = ps("b_psE", [P, GE], pc)
            psL = ps("b_psL", [P, GE], pc)
            psP = ps("b_psP", [P, GE], pc)
            psO = [ps(f"b_psO{k}", [P, GE], pc) for k in range(RING)]
            (A_ok, wl_ok, msg_ok, own_ok, run_ok, agg_ok, O_ok, neg_ok, ex_ok, yy_ok, pool_go) = sems(
                "b_", "A_ok wl_ok msg_ok own_ok run_ok agg_ok O_ok neg_ok ex_ok yy_ok pool_go")
            ld, xld, yo_ok, slot_set, sent = (ring_sems("b_" + s) for s in ("ld", "x_ld", "yo_ok", "slot_set", "sent"))

            with nc.Block() as block:
                @block.sync
                def _(eng):
                    def load(g, k, it):
                        if later(g):
                            eng.wait_ge(O_ok, g - RING + 1)
                        eng.dma_start(qd[:, k, :], hdT_d[bass.ds(g, 1), :, :].rearrange("a p n -> (a p) n")).then_inc(ld[k], 16)
                        eng.dma_start(pt[:, k, :], pT_d[bass.ds(g, 1), :, :].rearrange("a p n -> (a p) n")).then_inc(ld[k], 16)
                        eng.dma_start(al[:, k, :], alpha_d[:, bass.ds(g * GE, GE)]).then_inc(ld[k], 16)
                        if later(g):
                            eng.wait_ge(yo_ok[k], it - 1)
                        eng.dma_start(x1[:, k, :, :], tile_rows(x1_d, g)).then_inc(xld[k], 16)
                    pipeline(eng, NG, [(0, load)])

                @block.tensor
                def _(eng):
                    def spread_weights(g, k, it):
                        if used(g, 1):
                            eng.wait_ge(msg_ok, g)
                            eng.wait_ge(wl_ok, g)
                            eng.wait_ge(own_ok, g)
                        eng.wait_ge(ld[k], 48 * it)
                        eng.matmul(psE[:, :], spread_a[:, :], al[:, k, :], start=True, stop=True)
                        eng.matmul(psL[:, :], spread_b[:, :], al[:, k, :], start=True, stop=True)
                        eng.matmul(psP[:, :], wgT[:, :], qd[:, k, :], start=True, stop=True).then_inc(A_ok, 1)

                    def output(g, k, it):
                        if later(g):
                            eng.wait_ge(yy_ok, g - RING + 1)
                        eng.wait_ge(agg_ok, g + 1)
                        for j in range(TG):
                            o = psO[k][:, j * D:(j + 1) * D]
                            c = slice(j * P, (j + 1) * P)
                            eng.matmul(o, agg[:, k, c], ident[:, :], start=True, stop=False)
                            eng.matmul(o, qd[:, k, c], wskT[:, :], start=False, stop=False)
                            last = eng.matmul(o, ones_row[:, :], bias_r[:, :], start=False, stop=True)
                        last.then_inc(O_ok, 1)
                    pipeline(eng, NG, [(1, output), (0, spread_weights)])

                @block.scalar
                def _(eng):
                    def weights_of_loops(g, k, it):
                        if later(g):
                            eng.wait_ge(own_ok, g - RING + 1)
                        eng.wait_ge(A_ok, g + 1)
                        eng.activation(wl[:, k, :], psL[:, :], ACT.Copy).then_inc(wl_ok, 1)

                    def expo(g, k, it):
                        eng.wait_ge(neg_ok, g + 1)
                        eng.activation(ex[:, k, :], neg[:, k, :], ACT.Exp).then_inc(ex_ok, 1)
                    pipeline(eng, NG, [(2, expo), (0, weights_of_loops)])

                @block.vector
                def _(eng):
                    def sums(g, k, it):
                        eng.wait_ge(A_ok, g + 1)
                        eng.tensor_tensor(msg[:, k, :], pt[:, k, :], psE[:, :], ALU.mult).then_inc(msg_ok, 1)
                        eng.wait_ge(wl_ok, g + 1)
                        eng.tensor_tensor(own[:, k, :], wl[:, k, :], psP[:, :], ALU.mult).then_inc(own_ok, 1)
                        if used(g, 1):
                            eng.wait_ge(run_ok, g)
                        eng.wait_ge(msg_ok, g + 1)
                        eng.tensor_tensor_scan(
                            out=run[:, k, :], data0=eq_bc[:, bass.ds(g * GE, GE)], data1=msg[:, k, :],
                            initial=run[:, (k - 1) % RING, GE - 1:GE] if used(g, 1) else 0.0,
                            op0=ALU.mult, op1=ALU.add).then_inc(run_ok, 1)
                        if later(g):
                            eng.wait_ge(O_ok, g - RING + 1)
                        eng.wait_ge(own_ok, g + 1)
                        eng.wait_ge(run_ok, g + 1)
                        eng.tensor_tensor(agg[:, k, :], run[:, k, :], own[:, k, :], ALU.add).then_inc(agg_ok, 1)

                    def negative(g, k, it):
                        eng.wait_ge(O_ok, g + 1)
                        eng.tensor_scalar(neg[:, k, :], psO[k][:, :], 0.0, None, ALU.min).then_inc(neg_ok, 1)

                    def finish(g, k, it):
                        eng.wait_ge(ex_ok, g + 1)
                        eng.scalar_tensor_tensor(out=yy[:, k, :], in0=psO[k][:, :], scalar=0.0, in1=ex[:, k, :],
                                                 op0=ALU.max, op1=ALU.add).then_inc(yy_ok, 1)
                        eng.wait_ge(xld[k], 16 * it)
                        if later(g):
                            eng.wait_ge(sent[k], 16 * TG * (it - 1))
                        eng.tensor_copy(islot[:, k, :], idx_out[:, bass.ds(g * TG, TG)]).then_inc(slot_set[k], 1)
                        eng.wait_ge(yy_ok, g + 1)
                        eng.scalar_tensor_tensor(out=yo[:, k, :, :].rearrange("p j f -> p (j f)"), in0=yy[:, k, :],
                                                 scalar=-1.0, in1=x1[:, k, :, :].rearrange("p j f -> p (j f)"),
                                                 op0=ALU.add, op1=ALU.add).then_inc(yo_ok[k], 1)
                    pipeline(eng, NG, [(2, negative), (0, sums), (2, finish)])

                @block.gpsimd
                def _(eng):
                    def scatter(g, k, it):
                        eng.wait_ge(pool_go, 1)
                        eng.wait_ge(slot_set[k], it)
                        eng.wait_ge(yo_ok[k], it)
                        for j in range(TG):
                            eng.indirect_dma_start(out, bass.IndirectOffsetOnAxis(islot[:, k, j:j + 1], 0), yo[:, k, j, :],
                                                   None, bounds_check=N - 1, oob_is_err=False).then_inc(sent[k], 16)
                    eng.sem_inc(pool_go, 1)
                    pool_pipeline(eng, NG, scatter)
                    for k in range(RING):
                        eng.wait_ge(sent[k], 16 * TG * ((NG + RING - 1 - k) // RING))


_INS = ['x', 'src', 'dst', 'L0_gnn_W1_0', 'L0_gnn_b1_0', 'L0_gnn_W2_0', 'L0_gnn_b2_0', 'L0_gnn_ln_g0', 'L0_gnn_ln_b0',
        'L0_gnn_W1_1', 'L0_gnn_b1_1', 'L0_gnn_W2_1', 'L0_gnn_b2_1', 'L0_gnn_ln_g1', 'L0_gnn_ln_b1', 'L1_gnn_W_gat',
        'L1_gnn_att_src', 'L1_gnn_att_dst', 'L1_gnn_bias', 'L1_gnn_W_skip']


def kernel(**inputs):
    import numpy as _np
    import concourse.bacc as _bacc
    from concourse import mybir as _mybir
    from concourse.bass_utils import run_bass_kernel_spmd as _run

    nc = _bacc.Bacc("TRN2", target_bir_lowering=False, num_devices=1)
    arrays, args = {}, {}
    for name in _INS:
        a = _np.ascontiguousarray(inputs[name])
        arrays[f"in_{name}_dram"] = a
        args[name] = nc.dram_tensor(f"in_{name}_dram", a.shape, _mybir.dt.from_np(a.dtype), kind="ExternalInput").ap()
    x = inputs["x"]
    out = nc.dram_tensor("out_0_dram", x.shape, _mybir.dt.from_np(_np.asarray(x).dtype), kind="ExternalOutput").ap()
    both = lambda key: [args[f"L0_gnn_{key}{l}"] for l in range(2)]
    gnn_kernel(nc, args["x"], args["src"], args["dst"], both("W1_"), both("b1_"), both("W2_"), both("b2_"),
               both("ln_g"), both("ln_b"), args["L1_gnn_W_gat"], args["L1_gnn_att_src"], args["L1_gnn_att_dst"],
               args["L1_gnn_bias"], args["L1_gnn_W_skip"], out)
    r = _run(nc, [arrays], core_ids=[0])
    return r.results[0]["out_0_dram"]
```

```python
import concourse.bass as bass
from concourse import mybir
from contextlib import ExitStack

fp32 = mybir.dt.float32
fp16 = mybir.dt.float16
bf16 = mybir.dt.bfloat16
i32 = mybir.dt.int32
u8 = mybir.dt.uint8
ALU = mybir.AluOpType
ACT = mybir.ActivationFunctionType

D = 128
P = 128
H = 4
C = D // H
TG = 4
GE = TG * P
RING = 4
EPS = 1e-5
BIG = 1e30
SLOPE = 0.01
GAT_SLOPE = 0.2


def pipeline(eng, n, stages, ring=RING):
    lags = max(lag for lag, _ in stages)
    first = lags + ring
    turns = max((n - 1 - first) // ring, 0)

    def peeled(s):
        for lag, f in stages:
            if 0 <= s - lag < n:
                f(s - lag, (s - lag) % ring, (s - lag) // ring + 1)

    for s in range(first):
        peeled(s)
    with eng.Fori(0, turns) as i:
        for s in range(first, first + ring):
            for lag, f in stages:
                f(ring * i + (s - lag), (s - lag) % ring, i + ((s - lag) // ring + 1))
    for s in range(first + ring * turns, n + lags):
        peeled(s)


def pool_pipeline(eng, n, stage, after=None, ring=RING):
    after = after or (lambda g, k, it: None)
    for g in range(ring):
        stage(g, g, 1)
        if g:
            after(g - 1, g - 1, 1)
    with eng.Fori(2, n // ring + 1) as i:
        for k in range(ring):
            stage(ring * i + (k - ring), k, i)
            after(ring * i + (k - ring - 1), (k - 1) % ring, i if k else i - 1)
    for g in range(n // ring * ring, n):
        stage(g, g % ring, g // ring + 1)
        after(g - 1, (g - 1) % ring, (g - 1) // ring + 1)
    after(n - 1, (n - 1) % ring, (n - 1) // ring + 1)


def later(g):
    return not isinstance(g, int) or g >= RING


def gnn_kernel(nc, x, src, dst, W1, b1, W2, b2, ln_g, ln_b, W_gat, att_src, att_dst, gat_bias, W_skip, out):
    N = x.shape[0]
    E = src.shape[0]
    NG = (E + GE - 1) // GE
    NT = NG * TG
    EP = NT * P
    EJ = EP // P
    NONE = EP
    NCOL = 512
    assert NCOL * P > N and NT > P and E > (NT - 1) * P and E > (P - 1) * EJ

    ctx = ExitStack()
    with ctx:
        def sb(name, shape, dt=fp32, c=ctx):
            return c.enter_context(nc.sbuf_tensor(name, shape, dt))

        def ps(name, shape, c, dt=fp32):
            return c.enter_context(nc.psum_tensor(name, shape, dt))

        taken = []

        def sem(name):
            taken.append(nc.alloc_semaphore(name))
            return taken[-1]

        def end_stage():
            nc.clear_and_free_semaphores(list(taken))
            taken.clear()
            nc.all_engine_barrier()

        def dram(name, shape, dt=fp32):
            return nc.dram_tensor(name, shape, dt).ap()

        bounds_d = dram("bounds_d", (P * NCOL, 2), i32)
        eq_d = dram("eq_d", (1, EP), u8)
        eqr_d = dram("eqr_d", (1, EP), u8)
        cnt_d = dram("cnt_d", (6, EP), bf16)
        split_d = dram("split_d", (3, 3 * D), bf16)
        xs_d = dram("xs_d", (EP, D))
        xd_d = dram("xd_d", (EP, D))
        seg1_d = dram("seg1_d", (EP + 1, D))
        seg2_d = dram("seg2_d", (EP + 1, D))
        x1_d = dram("x1_d", (EP, D))
        qd_d = dram("qd_d", (NG, P, GE))
        qs_d = dram("qs_d", (NG, P, GE))
        score_d = dram("score_d", (2 * H, EP))
        alpha_d = dram("alpha_d", (6 * H, EP), bf16)

        ident = sb("ident", [P, P])
        eps = sb("eps", [P, 1])
        eq_bc = sb("eq_bc", [P, EP], u8)
        eqr_bc = sb("eqr_bc", [P, EP], u8)
        idx_sd = sb("idx_sd", [P, NT, 2], i32)
        idx_out = sb("idx_out", [P, NT], i32)
        bnd = sb("bnd", [P, NT, 2], i32)
        is_last = sb("is_last", [P, NT])
        is_first = sb("is_first", [P, NT])
        w1s = [sb(f"w1s{l}", [P, D]) for l in range(2)]
        w1d = [sb(f"w1d{l}", [P, D]) for l in range(2)]
        w2 = [sb(f"w2{l}", [P, D]) for l in range(2)]
        b1c = [sb(f"b1c{l}", [P, 1]) for l in range(2)]
        b2_6 = [sb(f"b2_6{l}", [6, D], bf16) for l in range(2)]
        bias_3 = sb("bias_3", [3, TG, D], bf16)
        ones_3 = sb("ones_3", [3, GE], bf16)
        gc = [sb(f"gc{l}", [P, 1]) for l in range(2)]
        bc = [sb(f"bc{l}", [P, 1]) for l in range(2)]
        wgT = sb("wgT", [P, D])
        wskT = sb("wskT", [P, D])
        wsum = sb("wsum", [P, D])
        score_s = sb("score_s", [P, 2 * H])
        score_dd = sb("score_dd", [P, 2 * H])
        spread = sb("spread", [6 * H, 2, D], bf16)
        bias_c = sb("bias_c", [P, 1])
        empty_bc = sb("empty_bc", [P, 1, D])
        before = sb("before", [P, P])
        iota_h = sb("iota_h", [P, NCOL], fp16)
        part_f = sb("part_f", [P, 2, NT])
        zeros_h = sb("zeros_h", [P, NCOL], fp16)
        eqP = sb("eqP", [P, EJ])
        eqnP = sb("eqnP", [P, EJ])
        lead = [sb(f"lead{k}", [P, EJ]) for k in range(2)]
        neg_eq = [sb(f"neg_eq{k}", [P, EJ]) for k in range(2)]
        neg_lead = [sb(f"neg_lead{k}", [P, EJ]) for k in range(2)]

        def tile_rows(table, g):
            return table[bass.ds(g * GE, GE), :].rearrange("(t p) f -> p t f", p=P)

        def seg_dve(eng, link, heads, v, loc, pack, row, car, carry, psr, psc, name, maximum, total):
            for k in range(2):
                rev = slice(None, None, -1) if k else slice(None)
                end = 0 if k else EJ - 1
                mask = (neg_eq if maximum else (eqP, eqnP))[k]
                run = (neg_lead if maximum else lead)[k]
                op0, op1 = (ALU.add, ALU.max) if maximum else (ALU.mult, ALU.add)
                for h in range(heads):
                    link(eng.tensor_tensor_scan(out=loc[k][:, h, rev], data0=mask[:, rev], data1=v[:, h, rev],
                                                initial=-BIG if maximum else 0.0, op0=op0, op1=op1))
                eng.tensor_copy(pack[:, 0:heads], loc[k][:, 0:heads, end])
                link(eng.tensor_copy(pack[:, heads:2 * heads], run[:, end:end + 1].to_broadcast([P, heads])))
                eng.sem_inc(name["pack"], 1)
                eng.wait_ge(name["row"], len(name["n"]) + 1)
                link(eng.tensor_copy(row[0:heads, :], psr[0:heads, 0:2 * P]))
                link(eng.memset(car[0:heads, :], -BIG if maximum else 0.0))
                o = slice(0, P) if k else slice(1, P + 1)
                link(eng.tensor_tensor_scan(out=car[0:heads, o][:, rev], data0=row[0:heads, P:2 * P][:, rev],
                                            data1=row[0:heads, 0:P][:, rev],
                                            initial=-BIG if maximum else 0.0, op0=op0, op1=op1))
                eng.sem_inc(name["scanned"], 1)
                eng.wait_ge(name["carry"], len(name["n"]) + 1)
                name["n"].append(k)
                link(eng.tensor_copy(carry[:, 0:heads], psc[:, 0:heads]))
                for h in range(heads):
                    link(eng.scalar_tensor_tensor(out=loc[k][:, h, :], in0=run[:, :], scalar=carry[:, h:h + 1],
                                                  in1=loc[k][:, h, :], op0=op0, op1=op1))
            a, b, t = (z[:, 0:heads, :] for z in (loc[0], loc[1], total))
            link(eng.tensor_tensor(t, a, b, ALU.max if maximum else ALU.add))
            if not maximum:
                link(eng.tensor_tensor(t, t, v[:, 0:heads, :], ALU.subtract))

        def seg_pe(eng, heads, pack, car, psr, psc, name):
            for k in range(2):
                n = len(name["n_pe"]) + 1
                name["n_pe"].append(k)
                eng.wait_ge(name["pack"], n)
                eng.transpose(psr[0:heads, 0:P], pack[:, 0:heads], ident[:, :])
                eng.transpose(psr[0:heads, P:2 * P], pack[:, heads:2 * heads], ident[:, :]).then_inc(name["row"], 1)
                eng.wait_ge(name["scanned"], n)
                o = slice(1, P + 1) if k else slice(0, P)
                eng.transpose(psc[:, 0:heads], car[0:heads, o], ident[0:heads, 0:heads]).then_inc(name["carry"], 1)

        def linker(eng, s):
            n = [0]

            def link(ins):
                n[0] += 1
                ins.then_inc(s, 1)
                eng.wait_ge(s, n[0])
            return link

        def split(eng, link, parts, v, rest):
            link(eng.tensor_copy(parts[0], v))
            for k in (1, 2):
                link(eng.tensor_tensor(rest, v if k == 1 else rest, parts[k - 1], ALU.subtract))
                link(eng.tensor_copy(parts[k], rest))

        def used(g, depth):
            return not isinstance(g, int) or g >= depth

        def sems(prefix, names):
            return [sem(prefix + s) for s in names.split()]

        def ring_sems(name, ring=RING):
            return [sem(f"{name}{k}") for k in range(ring)]

        RE = 3
        hist_ctx = ExitStack()
        xg = sb("xg", [P, RE, TG, 2, D], fp32, hist_ctx)
        with ExitStack() as pc:
            islot0 = sb("islot0", [P, RE, TG, 2], i32, pc)
            spread_a = sb("spread_a", [2 * H, D], fp32, pc)
            spread_b = sb("spread_b", [2 * H, D], fp32, pc)
            brow = sb("brow", [1, 3 * D], fp32, pc)
            brest = sb("brest", [1, 3 * D], fp32, pc)
            spread_h = sb("spread_h", [2 * H, 2, D], bf16, pc)
            bsplit = sb("bsplit", [1, 3, 3 * D], bf16, pc)
            cnt2 = sb("cnt2", [P, 2, EJ], bf16, pc)
            ri = sb("ri", [P, 2, 4, P], i32, pc)
            rf = sb("rf", [P, 2, 4, P], fp32, pc)
            tf = sb("tf", [P, 4, 2 * P], fp32, pc)
            pm_i = sb("pm_i", [P, 3, EJ], i32, pc)
            pm = sb("pm", [P, 3, EJ], fp32, pc)
            wraw = sb("wraw", [P, 4, D], fp32, pc)
            wg_raw = sb("wg_raw", [P, D], fp32, pc)
            wsk_raw = sb("wsk_raw", [P, D], fp32, pc)
            att = sb("att", [P, 2 * H], fp32, pc)
            iota_i = sb("iota_i", [P, NCOL], i32, pc)
            dst_i = sb("dst_i", [P, NT], i32, pc)
            part_i = sb("part_i", [P, 2, NT], i32, pc)
            eq8 = sb("eq8", [P, EJ], u8, pc)
            eqr8 = sb("eqr8", [P, EJ], u8, pc)
            eqn_back = sb("eqn_back", [P, EJ], fp32, pc)
            flip = sb("flip", [P, P], fp32, pc)
            zrow = sb("zrow", [1, D], fp32, pc)
            onesP = sb("onesP", [P, 1, EJ], fp32, pc)
            cntP = sb("cntP", [P, 1, EJ], fp32, pc)
            loc = [sb(f"c_loc{k}", [P, 1, EJ], fp32, pc) for k in range(2)]
            pack = sb("c_pack", [P, 2], fp32, pc)
            row = sb("c_row", [1, 2 * P], fp32, pc)
            car = sb("c_car", [1, P + 1], fp32, pc)
            carry = sb("c_carry", [P, 1], fp32, pc)
            ptile = ps("ptile", [P, 4, 2 * P], pc)
            pflip = ps("pflip", [P, 512], pc)
            pmisc = ps("pmisc", [P, 512], pc)
            psr = ps("c_psr", [P, 512], pc)
            psc = ps("c_psc", [P, 512], pc)

            s_fill = sem("p_fill")
            s_rows = sem("p_rows")
            s_w = sem("p_w")
            s_att0 = sem("p_att0")
            s_iota = sem("p_iota")
            s_id = sem("p_id")
            s_bef = sem("p_bef")
            s_rf = sem("p_rf")
            s_tile = sem("p_tile")
            s_wT = sem("p_wT")
            s_wTc = sem("p_wT_copied")
            s_wsc = sem("p_wscore")
            s_link = sem("p_link")
            s_eq8 = sem("p_eq8")
            s_back = sem("p_back")
            s_flip = sem("p_flip")
            s_cnt = sem("p_cnt")
            s_st = sem("p_stored")
            s_split = sem("p_split")
            index_ok = sem("p_index_ok")
            early, early_set = sem("p_early"), sem("p_early_set")
            s_spst = sem("p_split_stored")
            s_spread = sem("p_spread")
            s_eqst = sem("p_eq_stored")
            s_eqld = sem("p_eq_loaded")
            name = {k: sem("p_" + k) for k in ("pack", "row", "scanned", "carry")}
            name["n"], name["n_pe"] = [], []
            LT = NT - 1
            last_n = E - LT * P
            pl = P - 1
            pl_n = E - pl * EJ

            loads = []
            for k, a, sh in ((0, src, 0), (1, dst, 0), (3, dst, 1)):
                loads.append((ri[:, 0, k, :], a[sh:sh + P * P].rearrange("(p c) -> p c", c=P)))
                loads.append((ri[0:LT - P, 1, k, :], a[P * P + sh:LT * P + sh].rearrange("(p c) -> p c", c=P)))
                loads.append((ri[LT - P:NT - P, 1, k, 0:last_n - sh], a[LT * P + sh:E].rearrange("(a c) -> a c", a=1)))
            loads.append((ri[0:1, 0, 2, 1:P], dst[0:P - 1].rearrange("(a c) -> a c", a=1)))
            loads.append((ri[1:P, 0, 2, :], dst[P - 1:P * P - 1].rearrange("(p c) -> p c", c=P)))
            loads.append((ri[0:LT - P, 1, 2, :], dst[P * P - 1:LT * P - 1].rearrange("(p c) -> p c", c=P)))
            loads.append((ri[LT - P:NT - P, 1, 2, 0:last_n], dst[LT * P - 1:E - 1].rearrange("(a c) -> a c", a=1)))
            for k, sh in ((0, 0), (2, 1)):
                loads.append((pm_i[0:pl, k, :], dst[sh:pl * EJ + sh].rearrange("(p c) -> p c", c=EJ)))
                loads.append((pm_i[pl:P, k, 0:pl_n - sh], dst[pl * EJ + sh:E].rearrange("(a c) -> a c", a=1)))
            loads.append((pm_i[0:1, 1, 1:EJ], dst[0:EJ - 1].rearrange("(a c) -> a c", a=1)))
            loads.append((pm_i[1:pl, 1, :], dst[EJ - 1:pl * EJ - 1].rearrange("(p c) -> p c", c=EJ)))
            loads.append((pm_i[pl:P, 1, 0:pl_n + 1], dst[pl * EJ - 1:E].rearrange("(a c) -> a c", a=1)))

            weights = [(wraw[:, 2 * l + h, :], W1[l][h * D:(h + 1) * D, :]) for l in range(2) for h in range(2)]
            weights += [(w2[l][:, :], W2[l]) for l in range(2)]
            weights += [(wg_raw[:, :], W_gat), (wsk_raw[:, :], W_skip)]
            col = lambda v: v.rearrange("(p a) -> p a", a=1)
            rw = lambda v: v.rearrange("(a p) -> a p", a=1)
            for l in range(2):
                weights += [(b1c[l][:, :], col(b1[l])), (gc[l][:, :], col(ln_g[l])),
                            (bc[l][:, :], col(ln_b[l])), (brow[:, l * D:(l + 1) * D], rw(b2[l]))]
            weights += [(brow[:, 2 * D:3 * D], rw(gat_bias)), (bias_c[:, :], col(gat_bias)), (empty_bc[:, 0, :], rw(ln_b[1]).to_broadcast([P, D]))]
            for h in range(H):
                weights.append((att[h * C:(h + 1) * C, h:h + 1], att_src[h:h + 1, :].rearrange("a c -> c a")))
                weights.append((att[h * C:(h + 1) * C, H + h:H + h + 1], att_dst[h:h + 1, :].rearrange("a c -> c a")))

            with nc.Block() as block:
                @block.sync
                def _(eng):
                    eng.wait_ge(s_fill, 2)
                    for d, s in loads[0::2]:
                        eng.dma_start(d, s).then_inc(s_rows, 16)
                    eng.wait_ge(s_iota, 6)
                    eng.dma_start(seg1_d[EP:EP + 1, :], zrow[:, :]).then_inc(s_st, 16)
                    eng.dma_start(seg2_d[EP:EP + 1, :], zrow[:, :]).then_inc(s_st, 16)
                    eng.wait_ge(s_eq8, 1)
                    eng.dma_start(eq_d[0, 0:EP].rearrange("(p c) -> p c", c=EJ), eq8[:, :]).then_inc(s_eqst, 16)
                    eng.dma_start(eqr_d[0, :].rearrange("(p c) -> p c", c=EJ), eqr8[:, :]).then_inc(s_eqst, 16)
                    eng.wait_ge(s_cnt, 1)
                    for k in range(6):
                        eng.dma_start(cnt_d[k, :].rearrange("(p c) -> p c", c=EJ), cnt2[:, k // 3, :]).then_inc(s_st, 16)
                    eng.wait_ge(s_spread, 1)
                    for k in range(3):
                        eng.dma_start(spread[2 * H * k:2 * H * (k + 1), :, :], spread_h[:, :, :]).then_inc(s_eqld, 16)
                    eng.wait_ge(s_split, 1)
                    eng.dma_start(split_d.rearrange("(a k) f -> a (k f)", a=1),
                                  bsplit[:, :, :].rearrange("a k f -> a (k f)")).then_inc(s_spst, 16)
                    eng.wait_ge(s_spst, 16)
                    for j in range(TG):
                        eng.dma_start(bias_3[:, j, :], split_d[:, 2 * D:3 * D]).then_inc(s_eqld, 16)
                    eng.wait_ge(s_st, 16 * 8)
                    eng.wait_ge(s_eqld, 16 * (3 + TG))
                    eng.wait_ge(s_eqst, 32)
                    eng.wait_ge(early, 32 * TG * RE)

                @block.scalar
                def _(eng):
                    eng.wait_ge(s_fill, 2)
                    for d, s in loads[1::2]:
                        eng.dma_start(d, s).then_inc(s_rows, 16)
                    eng.wait_ge(s_att0, 1)
                    with nc.allow_non_contiguous_dma(reason="vectors of 128 values, a value per partition"):
                        for d, s in weights:
                            eng.dma_start(d, s).then_inc(s_w, 16)
                    eng.wait_ge(s_w, 16 * len(weights))

                @block.gpsimd
                def _(eng):
                    eng.memset(ri[:, :, :, :], N).then_inc(s_fill, 1)
                    eng.memset(pm_i[:, :, :], N).then_inc(s_fill, 1)
                    eng.memset(att[:, :], 0.0).then_inc(s_att0, 1)
                    eng.iota(iota_i[:, :], [[1, NCOL]], base=0, channel_multiplier=0).then_inc(s_iota, 1)
                    eng.memset(zeros_h[:, :], 0.0).then_inc(s_iota, 1)
                    eng.memset(zrow[:, :], 0.0).then_inc(s_iota, 1)
                    eng.memset(ones_3[:, :], 1.0).then_inc(s_iota, 1)
                    eng.memset(onesP[:, :, :], 1.0).then_inc(s_iota, 1)
                    eng.memset(eps[:, :], EPS).then_inc(s_iota, 1)
                    eng.memset(ident[:, :], 0.0).then_inc(s_id, 1)
                    eng.memset(before[:, :], 1.0).then_inc(s_bef, 1)
                    eng.memset(spread_a[:, :], 1.0).then_inc(s_bef, 1)
                    eng.memset(spread_b[:, :], 1.0).then_inc(s_bef, 1)
                    eng.wait_ge(s_id, 1)
                    eng.affine_select(out=ident[:, :], in_=ident[:, :], compare_op=ALU.not_equal, fill=1.0,
                                      base=0, pattern=[[-1, P]], channel_multiplier=1).then_inc(s_id, 1)
                    eng.memset(flip[:, :], 0.0).then_inc(s_flip, 1)
                    eng.wait_ge(s_flip, 1)
                    eng.affine_select(out=flip[:, :], in_=flip[:, :], compare_op=ALU.not_equal, fill=1.0,
                                      base=1 - P, pattern=[[1, P]], channel_multiplier=1).then_inc(s_flip, 1)
                    eng.wait_ge(s_bef, 3)
                    eng.affine_select(out=before[:, :], in_=before[:, :], compare_op=ALU.is_gt, fill=0.0,
                                      base=0, pattern=[[1, P]], channel_multiplier=-1).then_inc(s_bef, 1)
                    for t, h0 in ((spread_a, 0), (spread_b, H)):
                        eng.affine_select(out=t[:, :], in_=t[:, :], compare_op=ALU.is_ge, fill=0.0,
                                          base=C * h0, pattern=[[1, D]], channel_multiplier=-C).then_inc(s_bef, 1)
                    eng.wait_ge(s_bef, 6)
                    for t, h0 in ((spread_a, 0), (spread_b, H)):
                        eng.affine_select(out=t[:, :], in_=t[:, :], compare_op=ALU.is_gt, fill=0.0,
                                          base=C - C * h0, pattern=[[-1, D]], channel_multiplier=C).then_inc(s_bef, 1)
                    eng.wait_ge(index_ok, 1)
                    for e in range(RE):
                        eng.tensor_copy(islot0[:, e, :, :], idx_sd[:, e * TG:(e + 1) * TG, :]).then_inc(early_set, 1)
                    eng.wait_ge(early_set, RE)
                    for e in range(RE):
                        for j in range(TG):
                            for side in range(2):
                                eng.indirect_dma_start(xg[:, e, j, side, :], None, x,
                                                       bass.IndirectOffsetOnAxis(islot0[:, e, j, side:side + 1], 0)
                                                       ).then_inc(early, 16)

                @block.vector
                def _(eng):
                    link = linker(eng, s_link)
                    eng.wait_ge(s_rows, 16 * len(loads))
                    eng.tensor_copy(rf[:, :, :, :], ri[:, :, :, :]).then_inc(s_rf, 1)
                    eng.wait_ge(s_tile, 1)
                    link(eng.tensor_copy(tf[:, :, :], ptile[:, :, :]))
                    T = slice(0, NT)
                    link(eng.tensor_scalar(idx_sd[:, :, 0], tf[:, 0, T], float(N - 1), None, ALU.min))
                    link(eng.tensor_scalar(idx_sd[:, :, 1], tf[:, 1, T], float(N - 1), None, ALU.min))
                    eng.sem_inc(index_ok, 1)
                    link(eng.tensor_copy(pm[:, :, :], pm_i[:, :, :]))
                    link(eng.tensor_tensor(eqP[:, :], pm[:, 0, :], pm[:, 1, :], ALU.is_equal))
                    link(eng.tensor_tensor(eqnP[:, :], pm[:, 0, :], pm[:, 2, :], ALU.is_equal))
                    eng.tensor_copy(eq8[:, :], eqP[:, :])
                    eng.tensor_copy(eqn_back[:, :], eqnP[:, ::-1]).then_inc(s_back, 1)
                    eng.wait_ge(s_flip, 3)
                    eng.tensor_copy(eqr8[:, :], pflip[:, 0:EJ]).then_inc(s_eq8, 1)
                    for k, m in enumerate((eqP, eqnP)):
                        rev = slice(None, None, -1) if k else slice(None)
                        link(eng.tensor_tensor_scan(out=lead[k][:, rev], data0=m[:, rev], data1=m[:, rev],
                                                    initial=1.0, op0=ALU.mult, op1=ALU.mult))
                        link(eng.tensor_scalar(neg_eq[k][:, :], m[:, :], 1.0, BIG, ALU.subtract, ALU.mult))
                        link(eng.tensor_scalar(neg_lead[k][:, :], lead[k][:, :], 1.0, BIG, ALU.subtract, ALU.mult))
                    link(eng.tensor_tensor(is_first[:, :], tf[:, 1, T], tf[:, 2, T], ALU.not_equal))
                    link(eng.tensor_tensor(is_last[:, :], tf[:, 1, T], tf[:, 3, T], ALU.not_equal))
                    link(eng.scalar_tensor_tensor(out=tf[:, 3, T], in0=tf[:, 1, T], scalar=float(2 * N),
                                                  in1=is_last[:, :], op0=ALU.subtract, op1=ALU.mult))
                    link(eng.tensor_scalar(idx_out[:, :], tf[:, 3, T], float(2 * N), None, ALU.add))
                    link(eng.tensor_copy(dst_i[:, :], tf[:, 1, T]))
                    link(eng.tensor_scalar(part_i[:, 0, :], dst_i[:, :], 9, None, ALU.logical_shift_right))
                    link(eng.tensor_scalar(part_i[:, 1, :], dst_i[:, :], NCOL - 1, None, ALU.bitwise_and))
                    link(eng.tensor_copy(part_f[:, :, :], part_i[:, :, :]))
                    link(eng.tensor_scalar(part_f[:, 1, :], part_f[:, 1, :], -1.0, 1.0, ALU.mult, ALU.add))
                    eng.wait_ge(s_iota, 6)
                    link(eng.tensor_copy(iota_h[:, :], iota_i[:, :]))

                    seg_dve(eng, link, 1, onesP, loc, pack, row, car, carry, psr, psc, name, False, cntP)
                    link(eng.tensor_copy(cnt2[:, 0, :], cntP[:, 0, :]))
                    link(eng.tensor_tensor(cnt2[:, 1, :], cntP[:, 0, :], cnt2[:, 0, :], ALU.subtract))
                    eng.sem_inc(s_cnt, 1)
                    eng.wait_ge(s_w, 16 * len(weights))
                    for l in range(2):
                        link(eng.tensor_copy(w1s[l][:, :], wraw[:, 2 * l + 1, :]))
                        link(eng.tensor_tensor(w1d[l][:, :], wraw[:, 2 * l, :], wraw[:, 2 * l + 1, :], ALU.subtract))
                    link(eng.scalar_tensor_tensor(out=empty_bc[:, 0, :], in0=empty_bc[:, 0, :], scalar=SLOPE,
                                                  in1=empty_bc[:, 0, :], op0=ALU.mult, op1=ALU.max))
                    link(eng.tensor_scalar(empty_bc[:, 0, :], empty_bc[:, 0, :], 1.0, None, ALU.subtract))
                    eng.wait_ge(s_bef, 8)
                    link(eng.tensor_copy(spread_h[:, 0, :], spread_a[:, :]))
                    link(eng.tensor_copy(spread_h[:, 1, :], spread_b[:, :]))
                    eng.sem_inc(s_spread, 1)
                    split(eng, link, [bsplit[:, k, :] for k in range(3)], brow[:, :], brest[:, :])
                    eng.sem_inc(s_split, 1)
                    eng.wait_ge(s_wT, 1)
                    link(eng.tensor_copy(wgT[:, :], pmisc[:, 0:D]))
                    link(eng.tensor_copy(wskT[:, :], pmisc[:, D:2 * D]))
                    link(eng.tensor_tensor(wsum[:, :], wgT[:, :], wskT[:, :], ALU.add))
                    s2 = pmisc[:, 2 * D:2 * D + 2 * H]
                    link(eng.tensor_copy(score_s[:, 0:H], s2[:, 0:H]))
                    link(eng.memset(score_s[:, H:2 * H], 0.0))
                    link(eng.tensor_copy(score_dd[:, 0:H], s2[:, H:2 * H]))
                    link(eng.tensor_tensor(score_dd[:, H:2 * H], s2[:, H:2 * H], score_s[:, 0:H], ALU.add))

                @block.tensor
                def _(eng):
                    eng.wait_ge(s_id, 2)
                    eng.wait_ge(s_rf, 1)
                    for k in range(4):
                        for half in range(2):
                            last = eng.transpose(ptile[:, k, half * P:(half + 1) * P], rf[:, half, k, :], ident[:, :])
                    last.then_inc(s_tile, 1)
                    eng.wait_ge(s_back, 1)
                    eng.wait_ge(s_flip, 2)
                    eng.matmul(pflip[:, 0:EJ], flip[:, :], eqn_back[:, :], start=True, stop=True).then_inc(s_flip, 1)
                    eng.wait_ge(s_iota, 6)
                    seg_pe(eng, 1, pack, car, psr, psc, name)
                    eng.wait_ge(s_w, 16 * len(weights))
                    eng.transpose(pmisc[:, 0:D], wg_raw[:, :], ident[:, :])
                    eng.transpose(pmisc[:, D:2 * D], wsk_raw[:, :], ident[:, :])
                    eng.matmul(pmisc[:, 2 * D:2 * D + 2 * H], wg_raw[:, :], att[:, :], start=True,
                               stop=True).then_inc(s_wT, 1)

        end_stage()

        NF = N // GE
        tail = (N - NF * GE) // TG
        ndone = NF + 1
        RD = 6
        assert tail * TG + NF * GE == N and tail <= P and ndone == 2 * NG and NT == 2 * ndone
        phist = ps("phist", [P, NCOL], hist_ctx)
        with ExitStack() as pc:
            xt = sb("d_xt", [P, RD, TG, D], fp32, pc)
            x1 = sb("d_x1", [P, RD, TG, D], fp32, pc)
            xn = sb("d_xn", [P, RD, TG, D], fp32, pc)
            st = sb("d_st", [P, RD, TG, 6], fp32, pc)
            mv = sb("d_mv", [P, RD, TG, 2], fp32, pc)
            lnv, r0, sq, hv, rr, rs, off = (sb("d_" + s, [P, RD, TG], fp32, pc) for s in "lnv r0 sq hv rr rs off".split())
            hT = sb("d_hT", [P, RD, GE], fp32, pc)
            ex = sb("d_ex", [P, RD, GE], fp32, pc)
            part = sb("d_part", [P, RD, TG, D], fp32, pc)
            yo = sb("d_yo", [P, RD, TG, D], fp32, pc)
            onehot_p = sb("d_onehot_p", [P, 6, P], fp16, pc)
            ramp = sb("d_ramp", [P, 6, NCOL], fp16, pc)
            islot = sb("d_islot", [P, RE, TG, 2], i32, pc)
            psT = [ps(f"d_psT{k}", [P, GE], pc) for k in range(2)]
            psO = [ps(f"d_psO{k}", [P, GE], pc) for k in range(3)]
            ld, stored = ring_sems("d_ld", RD), ring_sems("d_stored", RD)
            slot_set, got, raw, free = (ring_sems("d_" + s, RE) for s in ("slot_set", "got", "raw", "free"))
            (x1_ok, st_ok, mv_ok, hv_ok, lnv_ok, r0_ok, sq_ok, rr_ok, rs_ok, off_ok, xn_ok, T_ok, h_ok, O_ok, ex_ok,
             part_ok, yo_ok, onehot_ok, ramp_ok, counted, masks_ld, pool_go) = sems("d_", "x1_ok st_ok mv_ok hv_ok lnv_ok r0_ok sq_ok rr_ok rs_ok off_ok xn_ok T_ok "
                                             "h_ok O_ok ex_ok part_ok yo_ok onehot_ok ramp_ok counted masks_ld pool_go")

            def npart(g):
                return tail if isinstance(g, int) and g == NF else P

            def node_rows(t, g):
                n = npart(g)
                return t[bass.ds(g * GE, n * TG), :].rearrange("(p j) f -> p j f", j=TG)

            with nc.Block() as block:
                @block.sync
                def _(eng):
                    def load(g, k, it):
                        n = npart(g)
                        if used(g, RD):
                            eng.wait_ge(x1_ok, g - RD + 1)
                        eng.dma_start(xt[0:n, k, :, :], node_rows(x, g)).then_inc(ld[k], 16)
                        if isinstance(g, int) and g == RD + 2:
                            eng.dma_start(eq_bc[:, :], eq_d.to_broadcast([P, EP])).then_inc(masks_ld, 16)
                        if isinstance(g, int) and g == 2 * RD + 2:
                            eng.dma_start(eqr_bc[:, :], eqr_d.to_broadcast([P, EP])).then_inc(masks_ld, 16)

                    def store(g, k, it):
                        n = npart(g)
                        eng.wait_ge(yo_ok, g + 1)
                        eng.dma_start(node_rows(out, g), yo[0:n, k, :, :]).then_inc(stored[k], 16)

                    def edge_rows(g, k, it):
                        s, e = k // 2, RE * it + (k // 2 - RE)
                        if k % 2 == 0:
                            if not isinstance(it, int) or it > 1:
                                eng.wait_ge(got[s], 32 * TG * (it - 1))
                            eng.dma_start(tile_rows(xs_d, e), xg[:, s, :, 0, :]).then_inc(raw[s], 16)
                            eng.dma_start(tile_rows(xd_d, e), xg[:, s, :, 1, :]).then_inc(raw[s], 16)
                        else:
                            eng.wait_ge(raw[s], 32 * it)
                            eng.sem_inc(free[s], 1)
                    for s in range(RE):
                        eng.sem_inc(free[s], 1)
                    pipeline(eng, ndone, [(0, load), (12, store), (0, edge_rows)], RD)
                    eng.wait_ge(masks_ld, 16 * 6)
                    for k in range(RD):
                        eng.wait_ge(stored[k], 16 * ((ndone + RD - 1 - k) // RD))

                @block.gpsimd
                def _(eng):
                    def gather(e, s, it):
                        if isinstance(e, int) and e < RE:
                            eng.sem_inc(slot_set[s], 1)
                            return
                        eng.wait_ge(free[s], it)
                        eng.tensor_copy(islot[:, s, :, :], idx_sd[:, bass.ds(e * TG, TG), :]).then_inc(slot_set[s], 1)
                        eng.wait_ge(pool_go, 1)
                        eng.wait_ge(slot_set[s], it)
                        for j in range(TG):
                            for side in range(2):
                                eng.indirect_dma_start(
                                    xg[:, s, j, side, :], None, x,
                                    bass.IndirectOffsetOnAxis(islot[:, s, j, side:side + 1], 0)).then_inc(got[s], 16)
                    eng.sem_inc(pool_go, 1)
                    pool_pipeline(eng, NG, gather, ring=RE)

                @block.vector
                def _(eng):
                    def add(g, k, it):
                        n = npart(g)
                        if used(g, RD):
                            eng.wait_ge(part_ok, g - RD + 1)
                        eng.wait_ge(ld[k], 16 * it)
                        eng.tensor_tensor(x1[0:n, k, :, :], xt[0:n, k, :, :],
                                          empty_bc[0:n, :, :].to_broadcast([n, TG, D]), ALU.add).then_inc(x1_ok, 1)

                    def root_step_1(g, k, it):
                        n = npart(g)
                        eng.wait_ge(sq_ok, g + 1)
                        eng.wait_ge(hv_ok, g + 1)
                        eng.tensor_tensor(rr[0:n, k, :], sq[0:n, k, :], hv[0:n, k, :], ALU.mult).then_inc(rr_ok, 1)

                    def stats(g, k, it):
                        n = npart(g)
                        eng.wait_ge(x1_ok, g + 1)
                        for j in range(TG):
                            last = eng.bn_stats(st[0:n, k, j, :], x1[0:n, k, j, :])
                        last.then_inc(st_ok, 1)

                    def one_hots(g, k, it):
                        if used(g, 3):
                            eng.wait_ge(counted, g - 2)
                        for t in range(2):
                            last = eng.tensor_scalar(onehot_p[:, (2 * k + t) % 6, :], iota_h[:, 0:P],
                                                     part_f[:, 0, bass.ds(2 * g + t, 1)], None, ALU.is_equal)
                        last = eng.tensor_scalar(ramp[:, 2 * k % 6, :], iota_h[:, :], part_f[:, 1, bass.ds(2 * g, 1)], 0.0,
                                                 ALU.add, ALU.max)
                        last.then_inc(onehot_ok, 1)

                    def root_step_2(g, k, it):
                        n = npart(g)
                        if used(g, RD):
                            eng.wait_ge(xn_ok, g - RD + 1)
                        eng.wait_ge(rr_ok, g + 1)
                        eng.scalar_tensor_tensor(out=rs[0:n, k, :], in0=rr[0:n, k, :], scalar=1.5, in1=r0[0:n, k, :],
                                                 op0=ALU.add, op1=ALU.mult).then_inc(rs_ok, 1)

                    def out_part(g, k, it):
                        n = npart(g)
                        eng.wait_ge(ex_ok, g + 1)
                        eng.scalar_tensor_tensor(out=part[0:n, k, :, :].rearrange("p j f -> p (j f)"), in0=ex[0:n, k, :],
                                                 scalar=1.0, in1=x1[0:n, k, :, :].rearrange("p j f -> p (j f)"),
                                                 op0=ALU.min, op1=ALU.add).then_inc(part_ok, 1)

                    def offset(g, k, it):
                        n = npart(g)
                        eng.wait_ge(rs_ok, g + 1)
                        if not isinstance(g, int):
                            eng.wait_ge(st_ok, g + 2)
                        eng.scalar_tensor_tensor(out=off[0:n, k, :], in0=mv[0:n, k, :, 0], scalar=-1.0, in1=rs[0:n, k, :],
                                                 op0=ALU.mult, op1=ALU.mult).then_inc(off_ok, 1)

                    def aggregate(g, k, it):
                        n = npart(g)
                        if isinstance(g, int):
                            eng.wait_ge(st_ok, g + 1)
                        for j in range(TG):
                            last = eng.bn_aggr(mv[0:n, k, j, :], st[0:n, k, j, :])
                        last.then_inc(mv_ok, 1)

                    def finish(g, k, it):
                        n = npart(g)
                        eng.wait_ge(part_ok, g + 1)
                        if used(g, RD):
                            eng.wait_ge(stored[k], 16 * (it - 1))
                        eng.scalar_tensor_tensor(out=yo[0:n, k, :, :].rearrange("p j f -> p (j f)"), in0=psO[k % 3][0:n, :],
                                                 scalar=0.0, in1=part[0:n, k, :, :].rearrange("p j f -> p (j f)"),
                                                 op0=ALU.max, op1=ALU.add).then_inc(yo_ok, 1)

                    def half_variance(g, k, it):
                        n = npart(g)
                        eng.wait_ge(mv_ok, g + 1)
                        eng.tensor_scalar(hv[0:n, k, :], mv[0:n, k, :, 1], EPS, -0.5, ALU.add, ALU.mult).then_inc(hv_ok, 1)
                    pipeline(eng, ndone, [(0, add), (1, root_step_1), (0, stats), (1, root_step_2), (5, out_part), (1, offset),
                                          (5, finish), (0, aggregate), (0, half_variance), (0, one_hots)], RD)

                @block.tensor
                def _(eng):
                    def count(g, k, it):
                        eng.wait_ge(onehot_ok, g + 1)
                        eng.wait_ge(ramp_ok, g + 1)
                        for t in range(2):
                            b = (2 * k + t) % 6
                            last = eng.matmul(phist[:, :], onehot_p[:, b, :], ramp[:, b, :], start=False, stop=False)
                        last.then_inc(counted, 1)

                    def turn(g, k, it):
                        n = npart(g)
                        eng.wait_ge(xn_ok, g + 1)
                        if used(g, 2):
                            eng.wait_ge(h_ok, g - 1)
                        for j in range(TG):
                            last = eng.transpose(psT[k % 2][:, j * P:j * P + n], xn[0:n, k, j, :], ident[0:n, 0:n])
                        last.then_inc(T_ok, 1)

                    def project(g, k, it):
                        n = npart(g)
                        if used(g, 3):
                            eng.wait_ge(yo_ok, g - 2)
                        eng.wait_ge(h_ok, g + 1)
                        eng.matmul(psO[k % 3][0:n, :], ones_3[:, 0:n], bias_3[:, :, :].rearrange("a j f -> a (j f)"),
                                   start=True, stop=False)
                        for j in range(TG):
                            last = eng.matmul(psO[k % 3][0:n, j * D:(j + 1) * D], hT[:, k, j * P:j * P + n], wsum[:, :],
                                              start=False, stop=j == TG - 1)
                        last.then_inc(O_ok, 1)
                    eng.matmul(phist[:, :], zeros_h[:, 0:P], zeros_h[:, :], start=True, stop=False)
                    pipeline(eng, ndone, [(1, count), (3, project), (1, turn)], RD)
                    eng.matmul(phist[:, :], zeros_h[:, 0:P], zeros_h[:, :], start=False, stop=True)

                @block.scalar
                def _(eng):
                    def copy_turned(g, k, it):
                        n = npart(g)
                        eng.wait_ge(T_ok, g + 1)
                        if used(g, RD):
                            eng.wait_ge(O_ok, g - RD + 1)
                        v = lambda t: t.rearrange("p (j n) -> p j n", j=TG)[:, :, 0:n]
                        eng.activation(v(hT[:, k, :]), v(psT[k % 2][:, :]), ACT.Copy).then_inc(h_ok, 1)

                    def normalise(g, k, it):
                        n = npart(g)
                        eng.wait_ge(off_ok, g + 1)
                        if used(g, RD):
                            eng.wait_ge(T_ok, g - RD + 1)
                        for j in range(TG):
                            last = eng.activation(xn[0:n, k, j, :], x1[0:n, k, j, :], ACT.Relu,
                                                  bias=off[0:n, k, j:j + 1], scale=rs[0:n, k, j:j + 1])
                        last.then_inc(xn_ok, 1)

                    def expo(g, k, it):
                        n = npart(g)
                        eng.wait_ge(O_ok, g + 1)
                        if used(g, RD):
                            eng.wait_ge(part_ok, g - RD + 1)
                        eng.activation(ex[0:n, k, :], psO[k % 3][0:n, :], ACT.Exp).then_inc(ex_ok, 1)

                    def root(g, k, it):
                        n = npart(g)
                        eng.wait_ge(mv_ok, g + 1)
                        eng.activation(lnv[0:n, k, :], mv[0:n, k, :, 1], ACT.Ln, bias=eps[0:n, :]).then_inc(lnv_ok, 1)
                        if used(g, RD):
                            eng.wait_ge(rs_ok, g - RD + 1)
                        eng.wait_ge(lnv_ok, g + 1)
                        eng.activation(r0[0:n, k, :], lnv[0:n, k, :], ACT.Exp, scale=-0.5).then_inc(r0_ok, 1)
                        eng.wait_ge(r0_ok, g + 1)
                        eng.activation(sq[0:n, k, :], r0[0:n, k, :], ACT.Square).then_inc(sq_ok, 1)
                    def ramps(g, k, it):
                        if used(g, 3):
                            eng.wait_ge(counted, g - 2)
                        eng.activation(ramp[:, (2 * k + 1) % 6, :], iota_h[:, :], ACT.Relu,
                                       bias=part_f[:, 1, bass.ds(2 * g + 1, 1)]).then_inc(ramp_ok, 1)
                    eng.preload_act_table_set("natural_log_exp_and_others")
                    for l in range(2):
                        for k in range(2):
                            eng.dma_start(b2_6[l][3 * k:3 * k + 3, :], split_d[:, l * D:(l + 1) * D]).then_inc(masks_ld, 16)
                    pipeline(eng, ndone, [(0, root), (4, expo), (3, copy_turned), (1, normalise), (0, ramps)], RD)

        end_stage()

        with hist_ctx, ExitStack() as pc:
            hist = sb("n_hist", [P, NCOL], fp32, pc)
            cum = sb("n_cum", [P, NCOL], fp32, pc)
            some = sb("n_some", [P, NCOL], fp32, pc)
            fl = sb("n_fl", [P, 2, NCOL], fp32, pc)
            bnd_i = sb("n_bnd_i", [P, NCOL, 2], i32, pc)
            offs = sb("n_offs", [P, 1], fp32, pc)
            psc = ps("n_psc", [P, 512], pc)
            s_link, s_cum, s_off, s_bnd, s_st = sems("n_", "link cum off bnd st")
            with nc.Block() as block:
                @block.vector
                def _(eng):
                    link = linker(eng, s_link)
                    link(eng.tensor_copy(some[:, :], phist[:, :]))
                    eng.tensor_copy(cum[:, 0:1], some[:, 0:1])
                    link(eng.tensor_tensor(cum[:, 1:NCOL], some[:, 1:NCOL], some[:, 0:NCOL - 1], ALU.subtract))
                    eng.sem_inc(s_cum, 1)
                    eng.tensor_copy(hist[:, 0:1], cum[:, 0:1])
                    link(eng.tensor_tensor(hist[:, 1:NCOL], cum[:, 1:NCOL], cum[:, 0:NCOL - 1], ALU.subtract))
                    link(eng.tensor_scalar(some[:, :], hist[:, :], 1.0, None, ALU.min))
                    eng.wait_ge(s_off, 1)
                    link(eng.tensor_copy(offs[:, :], psc[:, 0:1]))
                    link(eng.tensor_scalar(cum[:, :], cum[:, :], offs[:, 0:1], float(NONE), ALU.add, ALU.subtract))
                    link(eng.tensor_tensor(fl[:, 0, :], cum[:, :], hist[:, :], ALU.subtract))
                    link(eng.tensor_scalar(fl[:, 1, :], cum[:, :], 1.0, None, ALU.subtract))
                    for k in range(2):
                        link(eng.tensor_tensor(fl[:, k, :], fl[:, k, :], some[:, :], ALU.mult))
                        link(eng.tensor_scalar(bnd_i[:, :, k], fl[:, k, :], float(NONE), None, ALU.add))
                    eng.sem_inc(s_bnd, 1)

                @block.tensor
                def _(eng):
                    eng.wait_ge(s_cum, 1)
                    eng.matmul(psc[:, 0:1], before[:, :], cum[:, NCOL - 1:NCOL], start=True, stop=True).then_inc(s_off, 1)

                @block.sync
                def _(eng):
                    eng.wait_ge(s_bnd, 1)
                    eng.dma_start(bounds_d.rearrange("(p c) k -> p (c k)", p=P),
                                  bnd_i[:, :, :].rearrange("p c k -> p (c k)")).then_inc(s_st, 16)
                    eng.wait_ge(s_st, 16)

        end_stage()

        def conv(l):
            pre = f"v{l}_"
            rev = slice(None, None, -1) if l else slice(None)
            table = (seg1_d, seg2_d)[l]
            is_end = (is_last, is_first)[l]
            wd, ws, w2l = w1d[l], w1s[l], w2[l]

            def place(g):
                return g * -1 + (NG - 1) if l else g

            def mask(g):
                return (eqr_bc if l else eq_bc)[:, bass.ds(g * GE, GE)]

            with ExitStack() as pc:
                if l == 0:
                    xg = sb(pre + "xg", [P, RING, TG, 2, D], fp32, pc)
                    xn = sb(pre + "xn", [P, RING, TG, 2, D], fp32, pc)
                    st = sb(pre + "st", [P, RING, TG, 2, 6], fp32, pc)
                    mv = sb(pre + "mv", [P, RING, TG, 2, 2], fp32, pc)
                    sd = sb(pre + "sd", [P, RING, TG, 2], fp32, pc)
                    rs = sb(pre + "rs", [P, RING, TG, 2], fp32, pc)
                    off = sb(pre + "off", [P, RING, TG, 2], fp32, pc)
                    bslot = sb(pre + "bslot", [P, RING, TG, 2], i32, pc)
                else:
                    zg = sb(pre + "zg", [P, RING, TG, D], fp32, pc)
                    zd = sb(pre + "zd", [P, RING, TG, D], fp32, pc)
                    handed = sb(pre + "handed", [P, RING, GE], fp32, pc)
                islot = sb(pre + "islot", [P, RING, TG], i32, pc)
                hx = sb(pre + "hx", [P, RING, 2, GE], fp32, pc)
                hid = sb(pre + "hid", [P, RING, GE], fp32, pc)
                run = sb(pre + "run", [P, RING, GE], fp32, pc)
                zst = sb(pre + "zst", [P, RING, TG, 6], fp32, pc)
                zmv = sb(pre + "zmv", [P, RING, TG, 2], fp32, pc)
                zsd = sb(pre + "zsd", [P, RING, TG], fp32, pc)
                zrs = sb(pre + "zrs", [P, RING, TG], fp32, pc)
                zsc = sb(pre + "zsc", [P, RING, TG], fp32, pc)
                zof = sb(pre + "zof", [P, RING, TG], fp32, pc)
                zr = sb(pre + "zr", [P, RING, TG, D], fp32, pc)
                cnt = sb(pre + "cnt", [6, RING, GE], bf16, pc)
                psS = ps(pre + "psS", [P, GE], pc)
                psD = ps(pre + "psD", [P, GE], pc)
                psM = [ps(pre + f"psM{k}", [P, GE], pc) for k in range(2)]
                psZ = [ps(pre + f"psZ{k}", [P, GE], pc) for k in range(RING)]
                (st_ok, mv_ok, sd_ok, rs_ok, off_ok, xn_ok, T_ok, hS_ok, handed_ok, hD_ok, h_ok, M_ok, hid_ok, bent_ok, run_ok, Z_ok,
                 zst_ok, zmv_ok, zsd_ok, zrs_ok, zsc_ok, zof_ok, zr_ok, pool_go) = sems(
                    pre, "st_ok mv_ok sd_ok rs_ok off_ok xn_ok T_ok hS_ok handed_ok hD_ok h_ok M_ok hid_ok bent_ok run_ok Z_ok "
                    "zst_ok zmv_ok zsd_ok zrs_ok zsc_ok zof_ok zr_ok pool_go")
                slot_set, free, got, ld, cld, stored = (ring_sems(pre + s) for s in (
                    "slot_set", "free", "got", "ld", "cnt_ld", "stored"))

                with nc.Block() as block:
                    @block.gpsimd
                    def _(eng):
                        def look(g, k, it):
                            eng.tensor_copy(islot[:, k, :], idx_sd[:, bass.ds(g * TG, TG), 0]).then_inc(slot_set[k], 1)
                            eng.wait_ge(pool_go, 1)
                            eng.wait_ge(slot_set[k], it)
                            for j in range(TG):
                                eng.indirect_dma_start(bslot[:, k, j, :], None, bounds_d,
                                                       bass.IndirectOffsetOnAxis(islot[:, k, j:j + 1], 0)
                                                       ).then_inc(got[k], 16)

                        def keep(g, k, it):
                            eng.wait_ge(got[k], 16 * TG * it)
                            eng.tensor_copy(bnd[:, bass.ds(g * TG, TG), :], bslot[:, k, :, :]).then_inc(free[k], 1)

                        def gather(g, k, it):
                            eng.wait_ge(free[k], it)
                            eng.tensor_copy(islot[:, k, :], bnd[:, bass.ds(place(g) * TG, TG), 1]).then_inc(slot_set[k], 1)
                            eng.wait_ge(pool_go, 1)
                            eng.wait_ge(slot_set[k], it)
                            for j in range(TG):
                                eng.indirect_dma_start(
                                    zg[:, k, j, :], None, seg1_d,
                                    bass.IndirectOffsetOnAxis(islot[:, k, j:j + 1], 0)).then_inc(got[k], 16)
                        eng.sem_inc(pool_go, 1)
                        if l == 0:
                            pool_pipeline(eng, NG, look, keep)
                        else:
                            pool_pipeline(eng, NG, gather)

                    @block.sync
                    def _(eng):
                        def load(g, k, it):
                            if l == 0:
                                if later(g):
                                    eng.wait_ge(xn_ok, g - RING + 1)
                                eng.dma_start(xg[:, k, :, 0, :], tile_rows(xs_d, g)).then_inc(ld[k], 16)
                                eng.dma_start(xg[:, k, :, 1, :], tile_rows(xd_d, g)).then_inc(ld[k], 16)
                            else:
                                if later(g):
                                    eng.wait_ge(T_ok, g - RING + 1)
                                eng.dma_start(zd[:, k, :, :], tile_rows(seg1_d, place(g))).then_inc(ld[k], 16)

                        def load_counts(g, k, it):
                            if later(g):
                                eng.wait_ge(Z_ok, g - RING + 1)
                            eng.dma_start(cnt[:, k, :], cnt_d[:, bass.ds(place(g) * GE, GE)]).then_inc(cld[k], 16)

                        def release(g, k, it):
                            eng.wait_ge(T_ok, g + 1)
                            eng.sem_inc(free[k], 1)

                        def store(g, k, it):
                            eng.wait_ge(zr_ok, g + 1)
                            eng.dma_start(tile_rows(table, place(g)), zr[:, k, :, :]).then_inc(stored[k], 16)
                        if l == 0:
                            pipeline(eng, NG, [(0, load), (6, load_counts), (13, store)])
                        else:
                            for k in range(RING):
                                eng.sem_inc(free[k], 1)
                            pipeline(eng, NG, [(0, load), (RING, release), (6, load_counts), (13, store)])
                        for k in range(RING):
                            eng.wait_ge(stored[k], 16 * ((NG + RING - 1 - k) // RING))

                    @block.vector
                    def _(eng):
                        def x_stats(g, k, it):
                            eng.wait_ge(ld[k], 32 * it)
                            for j in range(TG):
                                for side in range(2):
                                    last = eng.bn_stats(st[:, k, j, side, :], xg[:, k, j, side, :])
                            last.then_inc(st_ok, 1)

                        def z_stats(g, k, it):
                            eng.wait_ge(Z_ok, g + 1)
                            for j in range(TG):
                                last = eng.bn_stats(zst[:, k, j, :], psZ[k][:, j * D:(j + 1) * D])
                            last.then_inc(zst_ok, 1)

                        def bend_hidden(g, k, it):
                            eng.wait_ge(hid_ok, g + 1)
                            eng.scalar_tensor_tensor(out=hid[:, k, :], in0=hid[:, k, :], scalar=SLOPE, in1=hid[:, k, :],
                                                     op0=ALU.mult, op1=ALU.max).then_inc(bent_ok, 1)

                        def add_up(g, k, it):
                            if not isinstance(g, int):
                                eng.wait_ge(zst_ok, g - 1)
                                if l == 0:
                                    eng.wait_ge(st_ok, g + 7)
                            if later(g):
                                eng.wait_ge(Z_ok, g - RING + 1)
                            if used(g, 1):
                                eng.wait_ge(run_ok, g)
                            eng.wait_ge(bent_ok, g + 1)
                            end = 0 if l else GE - 1
                            eng.tensor_tensor_scan(
                                out=run[:, k, rev], data0=mask(g), data1=hid[:, k, rev],
                                initial=run[:, (k - 1) % RING, end:end + 1] if used(g, 1) else 0.0,
                                op0=ALU.mult, op1=ALU.add).then_inc(run_ok, 1)

                        def x_aggregate(g, k, it):
                            if isinstance(g, int):
                                eng.wait_ge(st_ok, g + 1)
                            for j in range(TG):
                                for side in range(2):
                                    last = eng.bn_aggr(mv[:, k, j, side, :], st[:, k, j, side, :])
                            last.then_inc(mv_ok, 1)

                        def z_aggregate(g, k, it):
                            if isinstance(g, int):
                                eng.wait_ge(zst_ok, g + 1)
                            for j in range(TG):
                                last = eng.bn_aggr(zmv[:, k, j, :], zst[:, k, j, :])
                            last.then_inc(zmv_ok, 1)

                        def x_scales(g, k, it):
                            eng.wait_ge(sd_ok, g + 1)
                            eng.reciprocal(rs[:, k, :, :], sd[:, k, :, :]).then_inc(rs_ok, 1)

                        def x_offsets(g, k, it):
                            if later(g):
                                eng.wait_ge(xn_ok, g - RING + 1)
                            eng.wait_ge(rs_ok, g + 1)
                            eng.scalar_tensor_tensor(out=off[:, k, :, :], in0=mv[:, k, :, :, 0], scalar=-1.0,
                                                     in1=rs[:, k, :, :], op0=ALU.mult, op1=ALU.mult).then_inc(off_ok, 1)

                        def bend(g, k, it):
                            eng.wait_ge(hS_ok, g + 1)
                            eng.wait_ge(hD_ok, g + 1)
                            eng.scalar_tensor_tensor(out=hx[:, k, :, :], in0=hx[:, k, :, :], scalar=SLOPE,
                                                     in1=hx[:, k, :, :], op0=ALU.mult, op1=ALU.max).then_inc(h_ok, 1)

                        def hand_on(g, k, it):
                            if later(g):
                                eng.wait_ge(hD_ok, g - RING + 1)
                            if used(g, 1):
                                eng.wait_ge(handed_ok, g)
                            eng.wait_ge(T_ok, g + 1)
                            eng.tensor_tensor_scan(
                                out=handed[:, k, rev], data0=mask(g), data1=psD[:, rev],
                                initial=handed[:, (k - 1) % RING, 0:1] if used(g, 1) else 0.0,
                                op0=ALU.mult, op1=ALU.add).then_inc(handed_ok, 1)

                        def z_scale_1(g, k, it):
                            eng.wait_ge(zsd_ok, g + 1)
                            eng.reciprocal(zrs[:, k, :], zsd[:, k, :]).then_inc(zrs_ok, 1)

                        def z_scale_2(g, k, it):
                            if later(g):
                                eng.wait_ge(zr_ok, g - RING + 1)
                            eng.wait_ge(zrs_ok, g + 1)
                            eng.tensor_tensor(zsc[:, k, :], zrs[:, k, :], is_end[:, bass.ds(place(g) * TG, TG)],
                                              ALU.mult).then_inc(zsc_ok, 1)

                        def z_offset(g, k, it):
                            eng.wait_ge(zsc_ok, g + 1)
                            eng.scalar_tensor_tensor(out=zof[:, k, :], in0=zmv[:, k, :, 0], scalar=-1.0, in1=zsc[:, k, :],
                                                     op0=ALU.mult, op1=ALU.mult).then_inc(zof_ok, 1)

                        def input_d(g, k, it):
                            if later(g):
                                eng.wait_ge(M_ok, g - RING + 1)
                            eng.wait_ge(T_ok, g + 1)
                            eng.tensor_copy(hx[:, k, 1, :], psD[:, :]).then_inc(hD_ok, 1)
                        if l == 0:
                            pipeline(eng, NG, [(0, x_stats), (1, x_scales), (9, z_scale_1), (6, bend_hidden), (1, x_offsets),
                                               (9, z_scale_2), (8, z_stats), (9, z_offset), (3, input_d), (6, add_up),
                                               (0, x_aggregate), (8, z_aggregate)])
                        else:
                            pipeline(eng, NG, [(3, bend), (9, z_scale_1), (8, z_stats), (9, z_scale_2), (6, bend_hidden),
                                               (1, hand_on), (9, z_offset), (6, add_up), (8, z_aggregate)])

                    @block.tensor
                    def _(eng):
                        def turn(g, k, it):
                            if used(g, 1):
                                eng.wait_ge(hS_ok, g)
                                eng.wait_ge(hD_ok if l == 0 else handed_ok, g)
                            if l == 0:
                                eng.wait_ge(xn_ok, g + 1)
                            else:
                                eng.wait_ge(ld[k], 16 * it)
                                eng.wait_ge(got[k], 16 * TG * it)
                            for j in range(TG):
                                c = slice(j * P, (j + 1) * P)
                                eng.transpose(psS[:, c], xn[:, k, j, 0, :] if l == 0 else zg[:, k, j, :], ident[:, :])
                                last = eng.transpose(psD[:, c], xn[:, k, j, 1, :] if l == 0 else zd[:, k, j, :], ident[:, :])
                            last.then_inc(T_ok, 1)

                        def hidden(g, k, it):
                            if used(g, 2):
                                eng.wait_ge(hid_ok, g - 1)
                            if l == 0:
                                eng.wait_ge(hS_ok, g + 1)
                                eng.wait_ge(hD_ok, g + 1)
                            else:
                                eng.wait_ge(h_ok, g + 1)
                            eng.matmul(psM[k % 2][:, :], ws[:, :], hx[:, k, 0, :], start=True, stop=False)
                            eng.matmul(psM[k % 2][:, :], wd[:, :], hx[:, k, 1, :], start=False, stop=True).then_inc(M_ok, 1)

                        def second(g, k, it):
                            if later(g):
                                eng.wait_ge(zr_ok, g - RING + 1)
                            eng.wait_ge(cld[k], 16 * it)
                            eng.wait_ge(run_ok, g + 1)
                            for j in range(TG):
                                o = psZ[k][:, j * D:(j + 1) * D]
                                c = slice(j * P, (j + 1) * P)
                                eng.matmul(o, cnt[:, k, c], b2_6[l][:, :], start=True, stop=False)
                                last = eng.matmul(o, run[:, k, c], w2l[:, :], start=False, stop=True)
                            last.then_inc(Z_ok, 1)
                        pipeline(eng, NG, [(7, second), (4, hidden), (2 - 2 * l, turn)])

                    @block.scalar
                    def _(eng):
                        def x_root(g, k, it):
                            eng.wait_ge(mv_ok, g + 1)
                            eng.activation(sd[:, k, :, :], mv[:, k, :, :, 1], ACT.Sqrt, bias=eps[:, :]).then_inc(sd_ok, 1)

                        def x_normalise(g, k, it):
                            eng.wait_ge(off_ok, g + 1)
                            if later(g):
                                eng.wait_ge(T_ok, g - RING + 1)
                            for j in range(TG):
                                for side in range(2):
                                    last = eng.activation(xn[:, k, j, side, :], xg[:, k, j, side, :], ACT.Relu,
                                                          bias=off[:, k, j, side:side + 1], scale=rs[:, k, j, side:side + 1])
                            last.then_inc(xn_ok, 1)

                        def input_s(g, k, it):
                            if later(g):
                                eng.wait_ge(M_ok, g - RING + 1)
                            eng.wait_ge(T_ok, g + 1)
                            eng.activation(hx[:, k, 0, :], psS[:, :], ACT.Identity, bias=bc[0][:, :],
                                           scale=gc[0][:, :]).then_inc(hS_ok, 1)

                        def inputs(g, k, it):
                            if later(g):
                                eng.wait_ge(M_ok, g - RING + 1)
                            eng.wait_ge(T_ok, g + 1)
                            if l == 0:
                                eng.activation(hx[:, k, 0, :], psS[:, :], ACT.Copy).then_inc(hS_ok, 1)
                            else:
                                eng.wait_ge(handed_ok, g + 1)
                                eng.activation(hx[:, k, 1, :], handed[:, k, :], ACT.Identity, bias=bc[0][:, :],
                                               scale=gc[0][:, :]).then_inc(hD_ok, 1)

                        def biased(g, k, it):
                            if later(g):
                                eng.wait_ge(run_ok, g - RING + 1)
                            eng.wait_ge(M_ok, g + 1)
                            eng.activation(hid[:, k, :], psM[k % 2][:, :], ACT.Identity, bias=b1c[l][:, :]).then_inc(hid_ok, 1)

                        def z_root(g, k, it):
                            eng.wait_ge(zmv_ok, g + 1)
                            eng.activation(zsd[:, k, :], zmv[:, k, :, 1], ACT.Sqrt, bias=eps[:, :]).then_inc(zsd_ok, 1)

                        def z_normalise(g, k, it):
                            if later(g):
                                eng.wait_ge(stored[k], 16 * (it - 1))
                            eng.wait_ge(zof_ok, g + 1)
                            for j in range(TG):
                                last = eng.activation(zr[:, k, j, :], psZ[k][:, j * D:(j + 1) * D], ACT.Identity,
                                                      bias=zof[:, k, j:j + 1], scale=zsc[:, k, j:j + 1])
                            last.then_inc(zr_ok, 1)
                        if l == 0:
                            pipeline(eng, NG, [(0, x_root), (8, z_root), (3, inputs), (5, biased), (9, z_normalise), (1, x_normalise)])
                        else:
                            pipeline(eng, NG, [(1, input_s), (8, z_root), (5, biased), (1, inputs), (9, z_normalise)])

        conv(0)
        end_stage()
        conv(1)
        end_stage()

        with ExitStack() as pc:
            zg = sb("a_zg", [P, RING, TG, D], fp32, pc)
            zd = sb("a_zd", [P, RING, TG, D], fp32, pc)
            xr = sb("a_xr", [P, RING, 2, TG, D], fp32, pc)
            x1 = sb("a_x1", [P, RING, 2, TG, D], fp32, pc)
            hh = sb("a_hh", [P, RING, 2, GE], fp32, pc)
            handed = sb("a_handed", [P, RING, GE], fp32, pc)
            st = sb("a_st", [P, RING, 2, TG, 6], fp32, pc)
            mv = sb("a_mv", [P, RING, 2, TG, 2], fp32, pc)
            sd = sb("a_sd", [P, RING, 2, TG], fp32, pc)
            rs = sb("a_rs", [P, RING, 2, TG], fp32, pc)
            xn = sb("a_xn", [P, 2, 2, TG, D], fp32, pc)
            q = sb("a_q", [P, RING, 2, GE], fp32, pc)
            off = sb("a_off", [P, RING, 2, TG], fp32, pc)
            sc = sb("a_sc", [2 * H, RING, GE], fp32, pc)
            islot = sb("a_islot", [P, RING, TG], i32, pc)
            psA = [ps(f"a_psA{k}", [P, GE], pc) for k in range(2)]
            psR = [ps(f"a_psR{k}", [P, GE], pc) for k in range(2)]
            psQ = [ps(f"a_psQ{k}", [P, GE], pc) for k in range(2)]
            psC = [ps(f"a_psC{k}", [2 * H, GE], pc) for k in range(2)]
            (T_ok, hS_ok, handed_ok, hD_ok, h_ok, R_ok, x1_ok, st_ok, mv_ok, sd_ok, rs_ok, off_ok, xn_ok, Q_ok, q_ok, C_ok,
             sc_ok, pool_go) = sems("a_", "T_ok hS_ok handed_ok hD_ok h_ok R_ok x1_ok st_ok mv_ok sd_ok rs_ok off_ok xn_ok "
                                    "Q_ok q_ok C_ok sc_ok pool_go")
            slot_set, free, got, zld, xld, x1_st, q_st, sc_st = (ring_sems("a_" + s) for s in (
                "slot_set", "free", "got", "zd_ld", "x_ld", "x1_st", "q_st", "sc_st"))

            with nc.Block() as block:
                @block.gpsimd
                def _(eng):
                    def gather(g, k, it):
                        eng.wait_ge(free[k], it)
                        eng.tensor_copy(islot[:, k, :], bnd[:, bass.ds(g * TG, TG), 0]).then_inc(slot_set[k], 1)
                        eng.wait_ge(pool_go, 1)
                        eng.wait_ge(slot_set[k], it)
                        for j in range(TG):
                            eng.indirect_dma_start(zg[:, k, j, :], None, seg2_d,
                                                   bass.IndirectOffsetOnAxis(islot[:, k, j:j + 1], 0)).then_inc(got[k], 16)
                    eng.sem_inc(pool_go, 1)
                    pool_pipeline(eng, NG, gather)

                @block.sync
                def _(eng):
                    def load_z(g, k, it):
                        if later(g):
                            eng.wait_ge(T_ok, g - RING + 1)
                        eng.dma_start(zd[:, k, :, :], tile_rows(seg2_d, g)).then_inc(zld[k], 16)

                    def load_x(g, k, it):
                        if later(g):
                            eng.wait_ge(x1_ok, g - RING + 1)
                        eng.dma_start(xr[:, k, 0, :, :], tile_rows(xs_d, g)).then_inc(xld[k], 16)
                        eng.dma_start(xr[:, k, 1, :, :], tile_rows(xd_d, g)).then_inc(xld[k], 16)

                    def release(g, k, it):
                        eng.wait_ge(T_ok, g + 1)
                        eng.sem_inc(free[k], 1)

                    def store_x1(g, k, it):
                        eng.wait_ge(x1_ok, g + 1)
                        eng.dma_start(tile_rows(x1_d, g), x1[:, k, 1, :, :]).then_inc(x1_st[k], 16)

                    def store_q(g, k, it):
                        eng.wait_ge(q_ok, g + 1)
                        for side, t in enumerate((qs_d, qd_d)):
                            eng.dma_start(t[bass.ds(g, 1), :, :].rearrange("a p n -> (a p) n"), q[:, k, side, :]).then_inc(q_st[k], 16)

                    def store_scores(g, k, it):
                        eng.wait_ge(sc_ok, g + 1)
                        eng.dma_start(score_d[:, bass.ds(g * GE, GE)], sc[:, k, :]).then_inc(sc_st[k], 16)
                    for k in range(RING):
                        eng.sem_inc(free[k], 1)
                    pipeline(eng, NG, [(0, load_z), (RING, release), (RING, load_x), (9, store_x1), (12, store_q),
                                       (14, store_scores)])
                    for k in range(RING):
                        n = (NG + RING - 1 - k) // RING
                        eng.wait_ge(x1_st[k], 16 * n)
                        eng.wait_ge(q_st[k], 32 * n)
                        eng.wait_ge(sc_st[k], 16 * n)

                @block.vector
                def _(eng):
                    def bend(g, k, it):
                        eng.wait_ge(hS_ok, g + 1)
                        eng.wait_ge(hD_ok, g + 1)
                        eng.scalar_tensor_tensor(out=hh[:, k, :, :], in0=hh[:, k, :, :], scalar=SLOPE,
                                                 in1=hh[:, k, :, :], op0=ALU.mult, op1=ALU.max).then_inc(h_ok, 1)

                    def add_x(g, k, it):
                        eng.wait_ge(xld[k], 32 * it)
                        if later(g):
                            eng.wait_ge(x1_st[k], 16 * (it - 1))
                            eng.wait_ge(xn_ok, g - RING + 1)
                        eng.wait_ge(R_ok, g + 1)
                        f = lambda t, side: t[:, k, side, :, :].rearrange("p j f -> p (j f)")
                        eng.tensor_tensor(f(x1, 0), psR[0][:, :], f(xr, 0), ALU.add)
                        eng.tensor_tensor(f(x1, 1), psR[1][:, :], f(xr, 1), ALU.add).then_inc(x1_ok, 1)
                        eng.wait_ge(x1_ok, g + 1)
                        for side in range(2):
                            for j in range(TG):
                                last = eng.bn_stats(st[:, k, side, j, :], x1[:, k, side, j, :])
                        last.then_inc(st_ok, 1)

                    def hand_on(g, k, it):
                        if not isinstance(g, int):
                            eng.wait_ge(st_ok, g - 2)
                        if later(g):
                            eng.wait_ge(hD_ok, g - RING + 1)
                        if used(g, 1):
                            eng.wait_ge(handed_ok, g)
                        eng.wait_ge(T_ok, g + 1)
                        eng.tensor_tensor_scan(
                            out=handed[:, k, :], data0=eq_bc[:, bass.ds(g * GE, GE)], data1=psA[1][:, :],
                            initial=handed[:, (k - 1) % RING, GE - 1:GE] if used(g, 1) else 0.0,
                            op0=ALU.mult, op1=ALU.add).then_inc(handed_ok, 1)

                    def aggregate(g, k, it):
                        if isinstance(g, int):
                            eng.wait_ge(st_ok, g + 1)
                        for side in range(2):
                            for j in range(TG):
                                last = eng.bn_aggr(mv[:, k, side, j, :], st[:, k, side, j, :])
                        last.then_inc(mv_ok, 1)

                    def scales(g, k, it):
                        eng.wait_ge(sd_ok, g + 1)
                        eng.reciprocal(rs[:, k, :, :], sd[:, k, :, :]).then_inc(rs_ok, 1)

                    def offsets(g, k, it):
                        if later(g):
                            eng.wait_ge(xn_ok, g - RING + 1)
                        eng.wait_ge(rs_ok, g + 1)
                        eng.scalar_tensor_tensor(out=off[:, k, :, :], in0=mv[:, k, :, :, 0], scalar=-1.0, in1=rs[:, k, :, :],
                                                 op0=ALU.mult, op1=ALU.mult).then_inc(off_ok, 1)
                    pipeline(eng, NG, [(4, add_x), (5, scales), (2, bend), (5, offsets), (1, hand_on), (4, aggregate)])

                @block.tensor
                def _(eng):
                    def turn(g, k, it):
                        if used(g, 1):
                            eng.wait_ge(hS_ok, g)
                            eng.wait_ge(handed_ok, g)
                        eng.wait_ge(zld[k], 16 * it)
                        eng.wait_ge(got[k], 16 * TG * it)
                        for j in range(TG):
                            eng.transpose(psA[0][:, j * P:(j + 1) * P], zg[:, k, j, :], ident[:, :])
                            last = eng.transpose(psA[1][:, j * P:(j + 1) * P], zd[:, k, j, :], ident[:, :])
                        last.then_inc(T_ok, 1)

                    def rows(g, k, it):
                        if used(g, 1):
                            eng.wait_ge(x1_ok, g)
                        eng.wait_ge(h_ok, g + 1)
                        for side in range(2):
                            for j in range(TG):
                                last = eng.transpose(psR[side][:, j * D:(j + 1) * D], hh[:, k, side, j * P:(j + 1) * P],
                                                     ident[:, :])
                        last.then_inc(R_ok, 1)

                    def turn_again(g, k, it):
                        if used(g, 1):
                            eng.wait_ge(q_ok, g)
                        eng.wait_ge(xn_ok, g + 1)
                        for side in range(2):
                            for j in range(TG):
                                last = eng.transpose(psQ[side][:, j * P:(j + 1) * P], xn[:, k % 2, side, j, :], ident[:, :])
                        last.then_inc(Q_ok, 1)

                    def score(g, k, it):
                        if used(g, 2):
                            eng.wait_ge(sc_ok, g - 1)
                        eng.wait_ge(q_ok, g + 1)
                        eng.matmul(psC[k % 2][:, :], score_s[:, :], q[:, k, 0, :], start=True, stop=False)
                        eng.matmul(psC[k % 2][:, :], score_dd[:, :], q[:, k, 1, :], start=False, stop=True).then_inc(C_ok, 1)
                    pipeline(eng, NG, [(8, score), (6, turn_again), (3, rows), (0, turn)])

                @block.scalar
                def _(eng):
                    def affine_s(g, k, it):
                        if later(g):
                            eng.wait_ge(R_ok, g - RING + 1)
                        eng.wait_ge(T_ok, g + 1)
                        eng.activation(hh[:, k, 0, :], psA[0][:, :], ACT.Identity, bias=bc[1][:, :],
                                       scale=gc[1][:, :]).then_inc(hS_ok, 1)

                    def affine_d(g, k, it):
                        eng.wait_ge(handed_ok, g + 1)
                        eng.activation(hh[:, k, 1, :], handed[:, k, :], ACT.Identity, bias=bc[1][:, :],
                                       scale=gc[1][:, :]).then_inc(hD_ok, 1)

                    def root(g, k, it):
                        eng.wait_ge(mv_ok, g + 1)
                        eng.activation(sd[:, k, :, :], mv[:, k, :, :, 1], ACT.Sqrt, bias=eps[:, :]).then_inc(sd_ok, 1)

                    def normalise(g, k, it):
                        eng.wait_ge(off_ok, g + 1)
                        if used(g, 2):
                            eng.wait_ge(Q_ok, g - 1)
                        for side in range(2):
                            for j in range(TG):
                                last = eng.activation(xn[:, k % 2, side, j, :], x1[:, k, side, j, :], ACT.Relu,
                                                      bias=off[:, k, side, j:j + 1], scale=rs[:, k, side, j:j + 1])
                        last.then_inc(xn_ok, 1)

                    def copy_turned(g, k, it):
                        if later(g):
                            eng.wait_ge(C_ok, g - RING + 1)
                            eng.wait_ge(q_st[k], 32 * (it - 1))
                        eng.wait_ge(Q_ok, g + 1)
                        eng.activation(q[:, k, 0, :], psQ[0][:, :], ACT.Copy)
                        eng.activation(q[:, k, 1, :], psQ[1][:, :], ACT.Copy).then_inc(q_ok, 1)

                    def scores(g, k, it):
                        if later(g):
                            eng.wait_ge(sc_st[k], 16 * (it - 1))
                        eng.wait_ge(C_ok, g + 1)
                        eng.activation(sc[:, k, :], psC[k % 2][:, :], ACT.Copy).then_inc(sc_ok, 1)

                    pipeline(eng, NG, [(7, copy_turned), (9, scores), (1, affine_s), (5, normalise), (1, affine_d), (4, root)])

        end_stage()

        with ExitStack() as pc:
            se = sb("s_se", [P, H, EJ], fp32, pc)
            sl = sb("s_sl", [P, H, EJ], fp32, pc)
            mx = sb("s_mx", [P, H, EJ], fp32, pc)
            sm = sb("s_sm", [P, H, EJ], fp32, pc)
            loc = [sb(f"s_loc{k}", [P, H, EJ], fp32, pc) for k in range(2)]
            al3 = sb("s_al3", [P, 2, 3, H, EJ], bf16, pc)
            rest = sb("s_rest", [P, H, EJ], fp32, pc)
            pack = sb("s_pack", [P, 2 * H], fp32, pc)
            row = sb("s_row", [H, 2 * P], fp32, pc)
            car = sb("s_car", [H, P + 1], fp32, pc)
            carry = sb("s_carry", [P, H], fp32, pc)
            psr = ps("s_psr", [P, 512], pc)
            psc = ps("s_psc", [P, 512], pc)
            s_ld, s_link, s_arg, s_exp, s_al, s_st = sems("s_", "ld link arg exp al st")
            name = {k: sem("s_" + k) for k in ("pack", "row", "scanned", "carry")}
            name["n"], name["n_pe"] = [], []

            with nc.Block() as block:
                @block.sync
                def _(eng):
                    for k, t in enumerate((se, sl)):
                        eng.dma_start(t[:, :, :], score_d[k * H:(k + 1) * H, :].rearrange("h (p c) -> p h c", c=EJ)
                                      ).then_inc(s_ld, 16)
                    for side in range(2):
                        eng.wait_ge(s_al, side + 1)
                        for k in range(3):
                            r = 2 * H * k + H * side
                            eng.dma_start(alpha_d[r:r + H, :].rearrange("h (p c) -> p h c", c=EJ),
                                          al3[:, side, k, :, :]).then_inc(s_st, 16)
                    eng.wait_ge(s_st, 16 * 6)

                @block.vector
                def _(eng):
                    link = linker(eng, s_link)
                    eng.wait_ge(s_ld, 32)
                    for t in (se, sl):
                        link(eng.scalar_tensor_tensor(out=t[:, :, :], in0=t[:, :, :], scalar=GAT_SLOPE, in1=t[:, :, :],
                                                      op0=ALU.mult, op1=ALU.max))
                    seg_dve(eng, link, H, se, loc, pack, row, car, carry, psr, psc, name, True, mx)
                    link(eng.tensor_tensor(mx[:, :, :], mx[:, :, :], sl[:, :, :], ALU.max))
                    link(eng.tensor_tensor(se[:, :, :], se[:, :, :], mx[:, :, :], ALU.subtract))
                    link(eng.tensor_tensor(sl[:, :, :], sl[:, :, :], mx[:, :, :], ALU.subtract))
                    eng.sem_inc(s_arg, 1)
                    eng.wait_ge(s_exp, 2)
                    seg_dve(eng, link, H, se, loc, pack, row, car, carry, psr, psc, name, False, sm)
                    link(eng.scalar_tensor_tensor(out=sm[:, :, :], in0=sm[:, :, :], scalar=1e-16, in1=sl[:, :, :],
                                                  op0=ALU.add, op1=ALU.add))
                    link(eng.reciprocal(sm[:, :, :], sm[:, :, :]))
                    for side, t in enumerate((se, sl)):
                        link(eng.tensor_tensor(t[:, :, :], t[:, :, :], sm[:, :, :], ALU.mult))
                        split(eng, link, [al3[:, side, k, :, :] for k in range(3)], t[:, :, :], rest[:, :, :])
                        eng.sem_inc(s_al, 1)

                @block.tensor
                def _(eng):
                    for _ in range(2):
                        seg_pe(eng, H, pack, car, psr, psc, name)

                @block.scalar
                def _(eng):
                    eng.wait_ge(s_arg, 1)
                    eng.activation(se[:, :, :], se[:, :, :], ACT.Exp).then_inc(s_exp, 1)
                    eng.activation(sl[:, :, :], sl[:, :, :], ACT.Exp).then_inc(s_exp, 1)

        end_stage()

        with ExitStack() as pc:
            q = sb("b_q", [P, RING, 2, GE], fp32, pc)
            al = sb("b_al", [6 * H, RING, GE], bf16, pc)
            x1 = sb("b_x1", [P, RING, TG, D], fp32, pc)
            wt = sb("b_wt", [P, 2, 2, GE], fp32, pc)
            msg, own, run, agg = (sb("b_" + s, [P, RING, GE], fp32, pc) for s in ("msg", "own", "run", "agg"))
            z, ex, pos, yy = (sb("b_" + s, [P, RING, GE], fp32, pc) for s in ("z", "ex", "pos", "yy"))
            yo = sb("b_yo", [P, RING, TG, D], fp32, pc)
            islot = sb("b_islot", [P, RING, TG], i32, pc)
            psW = [ps(f"b_psW{k}", [P, GE], pc) for k in range(2)]
            psS = [ps(f"b_psS{k}", [P, GE], pc) for k in range(2)]
            psD = [ps(f"b_psD{k}", [P, GE], pc) for k in range(2)]
            psK = ps("b_psK", [P, GE], pc)
            psY = ps("b_psY", [P, GE], pc)
            (W_ok, wt_ok, P_ok, msg_ok, own_ok, run_ok, agg_ok, K_ok, z_ok, ex_ok, pos_ok, yy_ok, Y_ok, pool_go) = sems(
                "b_", "W_ok wt_ok P_ok msg_ok own_ok run_ok agg_ok K_ok z_ok ex_ok pos_ok yy_ok Y_ok pool_go")
            ld, xld, yo_ok, slot_set, sent = (ring_sems("b_" + s) for s in ("ld", "x_ld", "yo_ok", "slot_set", "sent"))

            with nc.Block() as block:
                @block.sync
                def _(eng):
                    def load(g, k, it):
                        if later(g):
                            eng.wait_ge(K_ok, g - RING + 1)
                        for side, t in enumerate((qs_d, qd_d)):
                            eng.dma_start(q[:, k, side, :], t[bass.ds(g, 1), :, :].rearrange("a p n -> (a p) n")).then_inc(ld[k], 16)
                        eng.dma_start(al[:, k, :], alpha_d[:, bass.ds(g * GE, GE)]).then_inc(ld[k], 16)

                    def load_x(g, k, it):
                        if later(g):
                            eng.wait_ge(yo_ok[k], it - 1)
                        eng.dma_start(x1[:, k, :, :], tile_rows(x1_d, g)).then_inc(xld[k], 16)
                    pipeline(eng, NG, [(0, load), (RING, load_x)])

                @block.tensor
                def _(eng):
                    def spread_weights(g, k, it):
                        if used(g, 1):
                            eng.wait_ge(wt_ok, g)
                        eng.wait_ge(ld[k], 48 * it)
                        for side in range(2):
                            last = eng.matmul(psW[side][:, :], spread[:, side, :], al[:, k, :], start=True, stop=True)
                        last.then_inc(W_ok, 1)

                    def project(g, k, it):
                        if used(g, 2):
                            eng.wait_ge(own_ok, g - 1)
                            eng.wait_ge(msg_ok, g - 1)
                        eng.matmul(psS[k % 2][:, :], wgT[:, :], q[:, k, 0, :], start=True, stop=True)
                        eng.matmul(psD[k % 2][:, :], wgT[:, :], q[:, k, 1, :], start=True, stop=True).then_inc(P_ok, 1)

                    def skip(g, k, it):
                        if used(g, 1):
                            eng.wait_ge(z_ok, g)
                        eng.matmul(psK[:, :], wskT[:, :], q[:, k, 1, :], start=True, stop=True).then_inc(K_ok, 1)

                    def rows(g, k, it):
                        if used(g, 1):
                            eng.wait_ge(yo_ok[(k - 1) % RING], it if k else it - 1)
                        eng.wait_ge(yy_ok, g + 1)
                        for j in range(TG):
                            last = eng.transpose(psY[:, j * D:(j + 1) * D], yy[:, k, j * P:(j + 1) * P], ident[:, :])
                        last.then_inc(Y_ok, 1)
                    pipeline(eng, NG, [(0, spread_weights), (2, skip), (5, rows), (0, project)])

                @block.scalar
                def _(eng):
                    def weights(g, k, it):
                        if used(g, 2):
                            eng.wait_ge(own_ok, g - 1)
                        eng.wait_ge(W_ok, g + 1)
                        eng.activation(wt[:, k % 2, 0, :], psW[0][:, :], ACT.Copy)
                        eng.activation(wt[:, k % 2, 1, :], psW[1][:, :], ACT.Copy).then_inc(wt_ok, 1)

                    def expo(g, k, it):
                        eng.wait_ge(z_ok, g + 1)
                        if later(g):
                            eng.wait_ge(yy_ok, g - RING + 1)
                        eng.activation(ex[:, k, :], z[:, k, :], ACT.Exp).then_inc(ex_ok, 1)
                        eng.activation(pos[:, k, :], z[:, k, :], ACT.Relu).then_inc(pos_ok, 1)
                    pipeline(eng, NG, [(0, weights), (3, expo)])

                @block.vector
                def _(eng):
                    def add_skip(g, k, it):
                        eng.wait_ge(K_ok, g + 1)
                        if later(g):
                            eng.wait_ge(pos_ok, g - RING + 1)
                        eng.wait_ge(agg_ok, g + 1)
                        eng.scalar_tensor_tensor(out=z[:, k, :], in0=psK[:, :], scalar=bias_c[:, :], in1=agg[:, k, :],
                                                 op0=ALU.add, op1=ALU.add).then_inc(z_ok, 1)

                    def elu(g, k, it):
                        if later(g):
                            eng.wait_ge(Y_ok, g - RING + 1)
                        eng.wait_ge(pos_ok, g + 1)
                        eng.scalar_tensor_tensor(out=yy[:, k, :], in0=ex[:, k, :], scalar=1.0, in1=pos[:, k, :],
                                                 op0=ALU.min, op1=ALU.add).then_inc(yy_ok, 1)

                    def weigh(g, k, it):
                        eng.wait_ge(wt_ok, g + 1)
                        eng.wait_ge(P_ok, g + 1)
                        if later(g):
                            eng.wait_ge(agg_ok, g - RING + 1)
                        eng.tensor_tensor(msg[:, k, :], wt[:, k % 2, 0, :], psS[k % 2][:, :], ALU.mult).then_inc(msg_ok, 1)
                        eng.tensor_tensor(own[:, k, :], wt[:, k % 2, 1, :], psD[k % 2][:, :], ALU.mult).then_inc(own_ok, 1)

                    def add_up(g, k, it):
                        if used(g, 1):
                            eng.wait_ge(run_ok, g)
                        eng.wait_ge(msg_ok, g + 1)
                        eng.tensor_tensor_scan(
                            out=run[:, k, :], data0=eq_bc[:, bass.ds(g * GE, GE)], data1=msg[:, k, :],
                            initial=run[:, (k - 1) % RING, GE - 1:GE] if used(g, 1) else 0.0,
                            op0=ALU.mult, op1=ALU.add).then_inc(run_ok, 1)

                    def finish(g, k, it):
                        eng.wait_ge(xld[k], 16 * it)
                        if later(g):
                            eng.wait_ge(sent[k], 16 * TG * (it - 1))
                        eng.tensor_copy(islot[:, k, :], idx_out[:, bass.ds(g * TG, TG)]).then_inc(slot_set[k], 1)
                        eng.wait_ge(Y_ok, g + 1)
                        eng.scalar_tensor_tensor(out=yo[:, k, :, :].rearrange("p j f -> p (j f)"), in0=psY[:, :],
                                                 scalar=-1.0, in1=x1[:, k, :, :].rearrange("p j f -> p (j f)"),
                                                 op0=ALU.add, op1=ALU.add).then_inc(yo_ok[k], 1)

                    def add_own(g, k, it):
                        if later(g):
                            eng.wait_ge(z_ok, g - RING + 1)
                        eng.wait_ge(own_ok, g + 1)
                        eng.wait_ge(run_ok, g + 1)
                        eng.tensor_tensor(agg[:, k, :], run[:, k, :], own[:, k, :], ALU.add).then_inc(agg_ok, 1)
                    pipeline(eng, NG, [(3, add_skip), (2, weigh), (6, finish), (2, add_up), (4, elu), (2, add_own)])

                @block.gpsimd
                def _(eng):
                    def scatter(g, k, it):
                        eng.wait_ge(pool_go, 1)
                        eng.wait_ge(slot_set[k], it)
                        eng.wait_ge(yo_ok[k], it)
                        for j in range(TG):
                            eng.indirect_dma_start(out, bass.IndirectOffsetOnAxis(islot[:, k, j:j + 1], 0), yo[:, k, j, :],
                                                   None, bounds_check=N - 1, oob_is_err=False).then_inc(sent[k], 16)
                    eng.sem_inc(pool_go, 1)
                    pool_pipeline(eng, NG, scatter)
                    for k in range(RING):
                        eng.wait_ge(sent[k], 16 * TG * ((NG + RING - 1 - k) // RING))


_INS = ['x', 'src', 'dst', 'L0_gnn_W1_0', 'L0_gnn_b1_0', 'L0_gnn_W2_0', 'L0_gnn_b2_0', 'L0_gnn_ln_g0', 'L0_gnn_ln_b0',
        'L0_gnn_W1_1', 'L0_gnn_b1_1', 'L0_gnn_W2_1', 'L0_gnn_b2_1', 'L0_gnn_ln_g1', 'L0_gnn_ln_b1', 'L1_gnn_W_gat',
        'L1_gnn_att_src', 'L1_gnn_att_dst', 'L1_gnn_bias', 'L1_gnn_W_skip']


def kernel(**inputs):
    import numpy as _np
    import concourse.bacc as _bacc
    from concourse import mybir as _mybir
    from concourse.bass_utils import run_bass_kernel_spmd as _run

    nc = _bacc.Bacc("TRN2", target_bir_lowering=False, num_devices=1)
    arrays, args = {}, {}
    for name in _INS:
        a = _np.ascontiguousarray(inputs[name])
        arrays[f"in_{name}_dram"] = a
        args[name] = nc.dram_tensor(f"in_{name}_dram", a.shape, _mybir.dt.from_np(a.dtype), kind="ExternalInput").ap()
    x = inputs["x"]
    out = nc.dram_tensor("out_0_dram", x.shape, _mybir.dt.from_np(_np.asarray(x).dtype), kind="ExternalOutput").ap()
    both = lambda key: [args[f"L0_gnn_{key}{l}"] for l in range(2)]
    gnn_kernel(nc, args["x"], args["src"], args["dst"], both("W1_"), both("b1_"), both("W2_"), both("b2_"),
               both("ln_g"), both("ln_b"), args["L1_gnn_W_gat"], args["L1_gnn_att_src"], args["L1_gnn_att_dst"],
               args["L1_gnn_bias"], args["L1_gnn_W_skip"], out)
    r = _run(nc, [arrays], core_ids=[0])
    return r.results[0]["out_0_dram"]
```

```python
import concourse.bass as bass
from concourse import mybir
from contextlib import ExitStack

fp32 = mybir.dt.float32
fp16 = mybir.dt.float16
bf16 = mybir.dt.bfloat16
i32 = mybir.dt.int32
u8 = mybir.dt.uint8
ALU = mybir.AluOpType
ACT = mybir.ActivationFunctionType

D = 128
P = 128
H = 4
C = D // H
TG = 4
GE = TG * P
RING = 4
EPS = 1e-5
BIG = 1e30
SLOPE = 0.01
GAT_SLOPE = 0.2


def pipeline(eng, n, stages, ring=RING):
    lags = max(lag for lag, _ in stages)
    first = lags + ring
    turns = max((n - 1 - first) // ring, 0)

    def peeled(s):
        for lag, f in stages:
            if 0 <= s - lag < n:
                f(s - lag, (s - lag) % ring, (s - lag) // ring + 1)

    for s in range(first):
        peeled(s)
    with eng.Fori(0, turns) as i:
        for s in range(first, first + ring):
            for lag, f in stages:
                f(ring * i + (s - lag), (s - lag) % ring, i + ((s - lag) // ring + 1))
    for s in range(first + ring * turns, n + lags):
        peeled(s)


def pool_pipeline(eng, n, stage, after=None, ring=RING):
    after = after or (lambda g, k, it: None)
    for g in range(ring):
        stage(g, g, 1)
        if g:
            after(g - 1, g - 1, 1)
    with eng.Fori(2, n // ring + 1) as i:
        for k in range(ring):
            stage(ring * i + (k - ring), k, i)
            after(ring * i + (k - ring - 1), (k - 1) % ring, i if k else i - 1)
    for g in range(n // ring * ring, n):
        stage(g, g % ring, g // ring + 1)
        after(g - 1, (g - 1) % ring, (g - 1) // ring + 1)
    after(n - 1, (n - 1) % ring, (n - 1) // ring + 1)


def later(g):
    return not isinstance(g, int) or g >= RING


def gnn_kernel(nc, x, src, dst, W1, b1, W2, b2, ln_g, ln_b, W_gat, att_src, att_dst, gat_bias, W_skip, out):
    N = x.shape[0]
    E = src.shape[0]
    NG = (E + GE - 1) // GE
    NT = NG * TG
    EP = NT * P
    EJ = EP // P
    NONE = EP
    NCOL = 512
    assert NCOL * P > N and NT > P and E > (NT - 1) * P and E > (P - 1) * EJ

    ctx = ExitStack()
    with ctx:
        def sb(name, shape, dt=fp32, c=ctx):
            return c.enter_context(nc.sbuf_tensor(name, shape, dt))

        def ps(name, shape, c, dt=fp32):
            return c.enter_context(nc.psum_tensor(name, shape, dt))

        taken = []

        def sem(name):
            taken.append(nc.alloc_semaphore(name))
            return taken[-1]

        def end_stage():
            nc.clear_and_free_semaphores(list(taken))
            taken.clear()
            nc.all_engine_barrier()

        def dram(name, shape, dt=fp32):
            return nc.dram_tensor(name, shape, dt).ap()

        bounds_d = dram("bounds_d", (P * NCOL, 2), i32)
        eq_d = dram("eq_d", (1, EP), u8)
        eqr_d = dram("eqr_d", (1, EP), u8)
        cnt_d = dram("cnt_d", (6, EP), bf16)
        split_d = dram("split_d", (3, 3 * D), bf16)
        xs_d = dram("xs_d", (EP, D))
        xd_d = dram("xd_d", (EP, D))
        seg1_d = dram("seg1_d", (EP + 1, D))
        seg2_d = dram("seg2_d", (EP + 1, D))
        x1_d = dram("x1_d", (EP, D))
        qs_d = dram("qs_d", (NG, P, GE))
        score_d = dram("score_d", (2 * H, EP))
        alpha_d = dram("alpha_d", (6 * H, EP), bf16)

        ident = sb("ident", [P, P])
        eps = sb("eps", [P, 1])
        eq_bc = sb("eq_bc", [P, EP], u8)
        eqr_bc = sb("eqr_bc", [P, EP], u8)
        idx_sd = sb("idx_sd", [P, NT, 2], i32)
        idx_out = sb("idx_out", [P, NT], i32)
        bnd = sb("bnd", [P, NT, 2], i32)
        is_last = sb("is_last", [P, NT])
        scale_d = sb("scale_d", [P, 2, NT])
        is_first = sb("is_first", [P, NT])
        w1s = [sb(f"w1s{l}", [P, D]) for l in range(2)]
        w1d = [sb(f"w1d{l}", [P, D]) for l in range(2)]
        w2 = [sb(f"w2{l}", [P, D]) for l in range(2)]
        b1c = [sb(f"b1c{l}", [P, 1]) for l in range(2)]
        b2_6 = [sb(f"b2_6{l}", [6, D], bf16) for l in range(2)]
        bias_3 = sb("bias_3", [3, TG, D], bf16)
        ones_3 = sb("ones_3", [3, GE], bf16)
        gc = [sb(f"gc{l}", [P, 1]) for l in range(2)]
        bc = [sb(f"bc{l}", [P, 1]) for l in range(2)]
        wgT = sb("wgT", [P, D])
        wskT = sb("wskT", [P, D])
        wsum = sb("wsum", [P, D])
        score_s = sb("score_s", [P, RING, RING, 2 * H])
        score_dd = sb("score_dd", [P, RING, RING, 2 * H])
        spread = sb("spread", [6 * H, 2, D], bf16)
        bias_c = sb("bias_c", [P, 1])
        empty_bc = sb("empty_bc", [P, 1, D])
        before = sb("before", [P, P])
        iota_h = sb("iota_h", [P, NCOL], fp16)
        part_f = sb("part_f", [P, 2, NT])
        zeros_h = sb("zeros_h", [P, NCOL], fp16)
        eqP = sb("eqP", [P, EJ])
        eqnP = sb("eqnP", [P, EJ])
        lead = [sb(f"lead{k}", [P, EJ]) for k in range(2)]
        neg_eq = [sb(f"neg_eq{k}", [P, EJ]) for k in range(2)]
        neg_lead = [sb(f"neg_lead{k}", [P, EJ]) for k in range(2)]

        def tile_rows(table, g):
            return table[bass.ds(g * GE, GE), :].rearrange("(t p) f -> p t f", p=P)

        def seg_dve(eng, link, heads, v, loc, pack, row, car, carry, psr, psc, name, maximum, total):
            n = len(name["n"]) + 1
            name["n"].append(n)
            op0, op1 = (ALU.add, ALU.max) if maximum else (ALU.mult, ALU.add)
            none = -BIG if maximum else 0.0
            rev = (slice(None), slice(None, None, -1))
            run = neg_lead if maximum else lead
            for k in range(2):
                mask = (neg_eq if maximum else (eqP, eqnP))[k]
                for h in range(heads):
                    last = eng.tensor_tensor_scan(out=loc[k][:, h, rev[k]], data0=mask[:, rev[k]], data1=v[:, h, rev[k]],
                                                  initial=none, op0=op0, op1=op1)
            link(last)
            for k, end in enumerate((EJ - 1, 0)):
                c = 2 * heads * k
                eng.tensor_copy(pack[:, c:c + heads], loc[k][:, 0:heads, end])
                last = eng.tensor_copy(pack[:, c + heads:c + 2 * heads], run[k][:, end:end + 1].to_broadcast([P, heads]))
            link(last)
            eng.sem_inc(name["pack"], 1)
            link(eng.memset(car[0:heads, :, :], none))
            eng.wait_ge(name["row"], n)
            link(eng.tensor_copy(row[0:heads, :, :, :], psr[0:heads, :].rearrange("a (k j p) -> a k j p", k=2, j=2)))
            for k, o in enumerate((slice(1, P + 1), slice(0, P))):
                last = eng.tensor_tensor_scan(out=car[0:heads, k, o][:, rev[k]], data0=row[0:heads, k, 1, rev[k]],
                                              data1=row[0:heads, k, 0, rev[k]], initial=none, op0=op0, op1=op1)
            link(last)
            eng.sem_inc(name["scanned"], 1)
            eng.wait_ge(name["carry"], n)
            link(eng.tensor_copy(carry[:, 0:2 * heads], psc[:, 0:2 * heads]))
            for k in range(2):
                for h in range(heads):
                    c = heads * k + h
                    last = eng.scalar_tensor_tensor(out=loc[k][:, h, :], in0=run[k][:, :], scalar=carry[:, c:c + 1],
                                                    in1=loc[k][:, h, :], op0=op0, op1=op1)
            link(last)
            a, b, t = (z[:, 0:heads, :] for z in (loc[0], loc[1], total))
            link(eng.tensor_tensor(t, a, b, ALU.max if maximum else ALU.add))
            if not maximum:
                link(eng.tensor_tensor(t, t, v[:, 0:heads, :], ALU.subtract))

        def seg_pe(eng, heads, pack, car, psr, psc, name):
            n = len(name["n_pe"]) + 1
            name["n_pe"].append(n)
            eng.wait_ge(name["pack"], n)
            for i in range(4):
                last = eng.transpose(psr[0:heads, i * P:(i + 1) * P], pack[:, i * heads:(i + 1) * heads], ident[:, :])
            last.then_inc(name["row"], 1)
            eng.wait_ge(name["scanned"], n)
            for k, o in enumerate((slice(0, P), slice(1, P + 1))):
                last = eng.transpose(psc[:, k * heads:(k + 1) * heads], car[0:heads, k, o], ident[0:heads, 0:heads])
            last.then_inc(name["carry"], 1)

        def linker(eng, s):
            n = [0]

            def link(ins):
                n[0] += 1
                ins.then_inc(s, 1)
                eng.wait_ge(s, n[0])
            return link

        def split(eng, link, parts, v, rest):
            link(eng.tensor_copy(parts[0], v))
            for k in (1, 2):
                link(eng.tensor_tensor(rest, v if k == 1 else rest, parts[k - 1], ALU.subtract))
                link(eng.tensor_copy(parts[k], rest))

        def used(g, depth):
            return not isinstance(g, int) or g >= depth

        def sems(prefix, names):
            return [sem(prefix + s) for s in names.split()]

        def ring_sems(name, ring=RING):
            return [sem(f"{name}{k}") for k in range(ring)]

        RE = 3
        rows_ctx = ExitStack()
        xg = sb("xg", [P, RE, TG, 2, D], fp32, rows_ctx)
        with ExitStack() as pc:
            islot0 = sb("islot0", [P, RE, TG, 2], i32, pc)
            spread_a = sb("spread_a", [2 * H, D], fp32, pc)
            spread_b = sb("spread_b", [2 * H, D], fp32, pc)
            brow = sb("brow", [1, 3 * D], fp32, pc)
            brest = sb("brest", [1, 3 * D], fp32, pc)
            spread_h = sb("spread_h", [2 * H, 2, D], bf16, pc)
            bsplit = sb("bsplit", [1, 3, 3 * D], bf16, pc)
            cnt2 = sb("cnt2", [P, 2, EJ], bf16, pc)
            ri = sb("ri", [P, 2, 4, P], i32, pc)
            rf = sb("rf", [P, 2, 4, P], fp32, pc)
            tf = sb("tf", [P, 4, 2 * P], fp32, pc)
            pm_i = sb("pm_i", [P, 3, EJ], i32, pc)
            pm = sb("pm", [P, 3, EJ], fp32, pc)
            wraw = sb("wraw", [P, 4, D], fp32, pc)
            wg_raw = sb("wg_raw", [P, D], fp32, pc)
            wsk_raw = sb("wsk_raw", [P, D], fp32, pc)
            att = sb("att", [P, 2 * H], fp32, pc)
            iota_i = sb("iota_i", [P, NCOL], i32, pc)
            dst_i = sb("dst_i", [P, NT], i32, pc)
            part_i = sb("part_i", [P, 2, NT], i32, pc)
            eq8 = sb("eq8", [P, EJ], u8, pc)
            eqr8 = sb("eqr8", [P, EJ], u8, pc)
            eqn_back = sb("eqn_back", [P, EJ], fp32, pc)
            flip = sb("flip", [P, P], fp32, pc)
            zrow = sb("zrow", [1, D], fp32, pc)
            onesP = sb("onesP", [P, 1, EJ], fp32, pc)
            cntP = sb("cntP", [P, 1, EJ], fp32, pc)
            loc = [sb(f"c_loc{k}", [P, 1, EJ], fp32, pc) for k in range(2)]
            pack = sb("c_pack", [P, 4], fp32, pc)
            row = sb("c_row", [1, 2, 2, P], fp32, pc)
            car = sb("c_car", [1, 2, P + 1], fp32, pc)
            carry = sb("c_carry", [P, 2], fp32, pc)
            ptile = ps("ptile", [P, 4, 2 * P], pc)
            pflip = ps("pflip", [P, 512], pc)
            pmisc = ps("pmisc", [P, 512], pc)
            psr = ps("c_psr", [P, 512], pc)
            psc = ps("c_psc", [P, 512], pc)

            s_fill = sem("p_fill")
            s_rows = sem("p_rows")
            s_w = sem("p_w")
            s_att0 = sem("p_att0")
            s_iota = sem("p_iota")
            s_id = sem("p_id")
            s_bef = sem("p_bef")
            s_rf = sem("p_rf")
            s_tile = sem("p_tile")
            s_wT = sem("p_wT")
            s_link = sem("p_link")
            s_eq8 = sem("p_eq8")
            s_back = sem("p_back")
            s_flip = sem("p_flip")
            s_cnt = sem("p_cnt")
            s_st = sem("p_stored")
            s_split = sem("p_split")
            index_ok = sem("p_index_ok")
            early, early_set = sem("p_early"), sem("p_early_set")
            s_spst = sem("p_split_stored")
            s_spread = sem("p_spread")
            s_eqst = sem("p_eq_stored")
            s_eqld = sem("p_eq_loaded")
            name = {k: sem("p_" + k) for k in ("pack", "row", "scanned", "carry")}
            name["n"], name["n_pe"] = [], []
            LT = NT - 1
            last_n = E - LT * P
            pl = P - 1
            pl_n = E - pl * EJ

            loads = []
            for k, a, sh in ((0, src, 0), (1, dst, 0), (3, dst, 1)):
                loads.append((ri[:, 0, k, :], a[sh:sh + P * P].rearrange("(p c) -> p c", c=P)))
                loads.append((ri[0:LT - P, 1, k, :], a[P * P + sh:LT * P + sh].rearrange("(p c) -> p c", c=P)))
                loads.append((ri[LT - P:NT - P, 1, k, 0:last_n - sh], a[LT * P + sh:E].rearrange("(a c) -> a c", a=1)))
            loads.append((ri[0:1, 0, 2, 1:P], dst[0:P - 1].rearrange("(a c) -> a c", a=1)))
            loads.append((ri[1:P, 0, 2, :], dst[P - 1:P * P - 1].rearrange("(p c) -> p c", c=P)))
            loads.append((ri[0:LT - P, 1, 2, :], dst[P * P - 1:LT * P - 1].rearrange("(p c) -> p c", c=P)))
            loads.append((ri[LT - P:NT - P, 1, 2, 0:last_n], dst[LT * P - 1:E - 1].rearrange("(a c) -> a c", a=1)))
            for k, sh in ((0, 0), (2, 1)):
                loads.append((pm_i[0:pl, k, :], dst[sh:pl * EJ + sh].rearrange("(p c) -> p c", c=EJ)))
                loads.append((pm_i[pl:P, k, 0:pl_n - sh], dst[pl * EJ + sh:E].rearrange("(a c) -> a c", a=1)))
            loads.append((pm_i[0:1, 1, 1:EJ], dst[0:EJ - 1].rearrange("(a c) -> a c", a=1)))
            loads.append((pm_i[1:pl, 1, :], dst[EJ - 1:pl * EJ - 1].rearrange("(p c) -> p c", c=EJ)))
            loads.append((pm_i[pl:P, 1, 0:pl_n + 1], dst[pl * EJ - 1:E].rearrange("(a c) -> a c", a=1)))

            weights = [(wraw[:, 2 * l + h, :], W1[l][h * D:(h + 1) * D, :]) for l in range(2) for h in range(2)]
            weights += [(w2[l][:, :], W2[l]) for l in range(2)]
            weights += [(wg_raw[:, :], W_gat), (wsk_raw[:, :], W_skip)]
            col = lambda v: v.rearrange("(p a) -> p a", a=1)
            rw = lambda v: v.rearrange("(a p) -> a p", a=1)
            for l in range(2):
                weights += [(b1c[l][:, :], col(b1[l])), (gc[l][:, :], col(ln_g[l])),
                            (bc[l][:, :], col(ln_b[l])), (brow[:, l * D:(l + 1) * D], rw(b2[l]))]
            weights += [(brow[:, 2 * D:3 * D], rw(gat_bias)), (bias_c[:, :], col(gat_bias)), (empty_bc[:, 0, :], rw(ln_b[1]).to_broadcast([P, D]))]
            for h in range(H):
                weights.append((att[h * C:(h + 1) * C, h:h + 1], att_src[h:h + 1, :].rearrange("a c -> c a")))
                weights.append((att[h * C:(h + 1) * C, H + h:H + h + 1], att_dst[h:h + 1, :].rearrange("a c -> c a")))

            with nc.Block() as block:
                @block.sync
                def _(eng):
                    eng.wait_ge(s_fill, 2)
                    for d, s in loads[0::2]:
                        eng.dma_start(d, s).then_inc(s_rows, 16)
                    eng.wait_ge(s_iota, 6)
                    eng.dma_start(seg1_d[EP:EP + 1, :], zrow[:, :]).then_inc(s_st, 16)
                    eng.dma_start(seg2_d[EP:EP + 1, :], zrow[:, :]).then_inc(s_st, 16)
                    eng.wait_ge(s_eq8, 1)
                    eng.dma_start(eq_d[0, 0:EP].rearrange("(p c) -> p c", c=EJ), eq8[:, :]).then_inc(s_eqst, 16)
                    eng.dma_start(eqr_d[0, :].rearrange("(p c) -> p c", c=EJ), eqr8[:, :]).then_inc(s_eqst, 16)
                    eng.wait_ge(s_cnt, 1)
                    for k in range(6):
                        eng.dma_start(cnt_d[k, :].rearrange("(p c) -> p c", c=EJ), cnt2[:, k // 3, :]).then_inc(s_st, 16)
                    eng.wait_ge(s_spread, 1)
                    for k in range(3):
                        eng.dma_start(spread[2 * H * k:2 * H * (k + 1), :, :], spread_h[:, :, :]).then_inc(s_eqld, 16)
                    eng.wait_ge(s_split, 1)
                    eng.dma_start(split_d.rearrange("(a k) f -> a (k f)", a=1),
                                  bsplit[:, :, :].rearrange("a k f -> a (k f)")).then_inc(s_spst, 16)
                    eng.wait_ge(s_spst, 16)
                    for j in range(TG):
                        eng.dma_start(bias_3[:, j, :], split_d[:, 2 * D:3 * D]).then_inc(s_eqld, 16)
                    eng.wait_ge(s_st, 16 * 8)
                    eng.wait_ge(s_eqld, 16 * (3 + TG))
                    eng.wait_ge(s_eqst, 32)
                    eng.wait_ge(early, 32 * TG * RE)

                @block.scalar
                def _(eng):
                    eng.wait_ge(s_fill, 2)
                    for d, s in loads[1::2]:
                        eng.dma_start(d, s).then_inc(s_rows, 16)
                    eng.wait_ge(s_att0, 1)
                    with nc.allow_non_contiguous_dma(reason="vectors of 128 values, a value per partition"):
                        for d, s in weights:
                            eng.dma_start(d, s).then_inc(s_w, 16)
                    eng.wait_ge(s_w, 16 * len(weights))

                @block.gpsimd
                def _(eng):
                    eng.memset(ri[:, :, :, :], N).then_inc(s_fill, 1)
                    eng.memset(pm_i[:, :, :], N).then_inc(s_fill, 1)
                    eng.memset(att[:, :], 0.0).then_inc(s_att0, 1)
                    eng.iota(iota_i[:, :], [[1, NCOL]], base=0, channel_multiplier=0).then_inc(s_iota, 1)
                    eng.memset(zeros_h[:, :], 0.0).then_inc(s_iota, 1)
                    eng.memset(zrow[:, :], 0.0).then_inc(s_iota, 1)
                    eng.memset(ones_3[:, :], 1.0).then_inc(s_iota, 1)
                    eng.memset(onesP[:, :, :], 1.0).then_inc(s_iota, 1)
                    eng.memset(eps[:, :], EPS).then_inc(s_iota, 1)
                    eng.memset(ident[:, :], 0.0).then_inc(s_id, 1)
                    eng.memset(before[:, :], 1.0).then_inc(s_bef, 1)
                    eng.memset(spread_a[:, :], 1.0).then_inc(s_bef, 1)
                    eng.memset(spread_b[:, :], 1.0).then_inc(s_bef, 1)
                    eng.wait_ge(s_id, 1)
                    eng.affine_select(out=ident[:, :], in_=ident[:, :], compare_op=ALU.not_equal, fill=1.0,
                                      base=0, pattern=[[-1, P]], channel_multiplier=1).then_inc(s_id, 1)
                    eng.memset(flip[:, :], 0.0).then_inc(s_flip, 1)
                    eng.wait_ge(s_flip, 1)
                    eng.affine_select(out=flip[:, :], in_=flip[:, :], compare_op=ALU.not_equal, fill=1.0,
                                      base=1 - P, pattern=[[1, P]], channel_multiplier=1).then_inc(s_flip, 1)
                    eng.wait_ge(s_bef, 3)
                    eng.affine_select(out=before[:, :], in_=before[:, :], compare_op=ALU.is_gt, fill=0.0,
                                      base=0, pattern=[[1, P]], channel_multiplier=-1).then_inc(s_bef, 1)
                    for t, h0 in ((spread_a, 0), (spread_b, H)):
                        eng.affine_select(out=t[:, :], in_=t[:, :], compare_op=ALU.is_ge, fill=0.0,
                                          base=C * h0, pattern=[[1, D]], channel_multiplier=-C).then_inc(s_bef, 1)
                    eng.wait_ge(s_bef, 6)
                    for t, h0 in ((spread_a, 0), (spread_b, H)):
                        eng.affine_select(out=t[:, :], in_=t[:, :], compare_op=ALU.is_gt, fill=0.0,
                                          base=C - C * h0, pattern=[[-1, D]], channel_multiplier=C).then_inc(s_bef, 1)
                    eng.wait_ge(index_ok, 1)
                    for e in range(RE):
                        eng.tensor_copy(islot0[:, e, :, :], idx_sd[:, e * TG:(e + 1) * TG, :]).then_inc(early_set, 1)
                    eng.wait_ge(early_set, RE)
                    for e in range(RE):
                        for j in range(TG):
                            for side in range(2):
                                eng.indirect_dma_start(xg[:, e, j, side, :], None, x,
                                                       bass.IndirectOffsetOnAxis(islot0[:, e, j, side:side + 1], 0)
                                                       ).then_inc(early, 16)

                @block.vector
                def _(eng):
                    link = linker(eng, s_link)
                    eng.wait_ge(s_rows, 16 * len(loads))
                    eng.tensor_copy(rf[:, :, :, :], ri[:, :, :, :]).then_inc(s_rf, 1)
                    eng.wait_ge(s_tile, 1)
                    link(eng.tensor_copy(tf[:, :, :], ptile[:, :, :]))
                    T = slice(0, NT)
                    link(eng.tensor_scalar(idx_sd[:, :, 0], tf[:, 0, T], float(N - 1), None, ALU.min))
                    link(eng.tensor_scalar(idx_sd[:, :, 1], tf[:, 1, T], float(N - 1), None, ALU.min))
                    eng.sem_inc(index_ok, 1)
                    link(eng.tensor_copy(pm[:, :, :], pm_i[:, :, :]))
                    link(eng.tensor_tensor(eqP[:, :], pm[:, 0, :], pm[:, 1, :], ALU.is_equal))
                    link(eng.tensor_tensor(eqnP[:, :], pm[:, 0, :], pm[:, 2, :], ALU.is_equal))
                    eng.tensor_copy(eq8[:, :], eqP[:, :])
                    eng.tensor_copy(eqn_back[:, :], eqnP[:, ::-1]).then_inc(s_back, 1)
                    eng.wait_ge(s_flip, 3)
                    eng.tensor_copy(eqr8[:, :], pflip[:, 0:EJ]).then_inc(s_eq8, 1)
                    for k, m in enumerate((eqP, eqnP)):
                        rev = slice(None, None, -1) if k else slice(None)
                        link(eng.tensor_tensor_scan(out=lead[k][:, rev], data0=m[:, rev], data1=m[:, rev],
                                                    initial=1.0, op0=ALU.mult, op1=ALU.mult))
                        link(eng.tensor_scalar(neg_eq[k][:, :], m[:, :], 1.0, BIG, ALU.subtract, ALU.mult))
                        link(eng.tensor_scalar(neg_lead[k][:, :], lead[k][:, :], 1.0, BIG, ALU.subtract, ALU.mult))
                    link(eng.tensor_tensor(is_first[:, :], tf[:, 1, T], tf[:, 2, T], ALU.not_equal))
                    link(eng.tensor_tensor(is_last[:, :], tf[:, 1, T], tf[:, 3, T], ALU.not_equal))
                    link(eng.scalar_tensor_tensor(out=tf[:, 3, T], in0=tf[:, 1, T], scalar=float(2 * N),
                                                  in1=is_last[:, :], op0=ALU.subtract, op1=ALU.mult))
                    link(eng.tensor_scalar(idx_out[:, :], tf[:, 3, T], float(2 * N), None, ALU.add))
                    link(eng.tensor_copy(dst_i[:, :], tf[:, 1, T]))
                    link(eng.tensor_scalar(part_i[:, 0, :], dst_i[:, :], 9, None, ALU.logical_shift_right))
                    link(eng.tensor_scalar(part_i[:, 1, :], dst_i[:, :], NCOL - 1, None, ALU.bitwise_and))
                    link(eng.tensor_copy(part_f[:, :, :], part_i[:, :, :]))
                    link(eng.tensor_scalar(part_f[:, 1, :], part_f[:, 1, :], -1.0, 1.0, ALU.mult, ALU.add))
                    eng.wait_ge(s_iota, 6)
                    link(eng.tensor_copy(iota_h[:, :], iota_i[:, :]))

                    seg_dve(eng, link, 1, onesP, loc, pack, row, car, carry, psr, psc, name, False, cntP)
                    link(eng.tensor_copy(cnt2[:, 0, :], cntP[:, 0, :]))
                    link(eng.tensor_tensor(cnt2[:, 1, :], cntP[:, 0, :], cnt2[:, 0, :], ALU.subtract))
                    eng.sem_inc(s_cnt, 1)
                    eng.wait_ge(s_w, 16 * len(weights))
                    for l in range(2):
                        link(eng.tensor_copy(w1s[l][:, :], wraw[:, 2 * l + 1, :]))
                        link(eng.tensor_tensor(w1d[l][:, :], wraw[:, 2 * l, :], wraw[:, 2 * l + 1, :], ALU.subtract))
                    link(eng.scalar_tensor_tensor(out=empty_bc[:, 0, :], in0=empty_bc[:, 0, :], scalar=SLOPE,
                                                  in1=empty_bc[:, 0, :], op0=ALU.mult, op1=ALU.max))
                    link(eng.tensor_scalar(empty_bc[:, 0, :], empty_bc[:, 0, :], 1.0, None, ALU.subtract))
                    eng.wait_ge(s_bef, 8)
                    link(eng.tensor_copy(spread_h[:, 0, :], spread_a[:, :]))
                    link(eng.tensor_copy(spread_h[:, 1, :], spread_b[:, :]))
                    eng.sem_inc(s_spread, 1)
                    split(eng, link, [bsplit[:, k, :] for k in range(3)], brow[:, :], brest[:, :])
                    eng.sem_inc(s_split, 1)
                    eng.wait_ge(s_wT, 1)
                    link(eng.tensor_copy(wgT[:, :], pmisc[:, 0:D]))
                    link(eng.tensor_copy(wskT[:, :], pmisc[:, D:2 * D]))
                    link(eng.tensor_tensor(wsum[:, :], wgT[:, :], wskT[:, :], ALU.add))
                    s2 = pmisc[:, 2 * D:2 * D + 2 * H]
                    eng.memset(score_s[:, :, :, :], 0.0)
                    link(eng.memset(score_dd[:, :, :, :], 0.0))
                    for k in range(RING):
                        link(eng.tensor_copy(score_s[:, k, k, 0:H], s2[:, 0:H]))
                        link(eng.tensor_copy(score_dd[:, k, k, 0:H], s2[:, H:2 * H]))
                        link(eng.tensor_tensor(score_dd[:, k, k, H:2 * H], s2[:, H:2 * H], score_s[:, k, k, 0:H], ALU.add))

                @block.tensor
                def _(eng):
                    eng.wait_ge(s_id, 2)
                    eng.wait_ge(s_rf, 1)
                    for k in range(4):
                        for half in range(2):
                            last = eng.transpose(ptile[:, k, half * P:(half + 1) * P], rf[:, half, k, :], ident[:, :])
                    last.then_inc(s_tile, 1)
                    eng.wait_ge(s_back, 1)
                    eng.wait_ge(s_flip, 2)
                    eng.matmul(pflip[:, 0:EJ], flip[:, :], eqn_back[:, :], start=True, stop=True).then_inc(s_flip, 1)
                    eng.wait_ge(s_iota, 6)
                    seg_pe(eng, 1, pack, car, psr, psc, name)
                    eng.wait_ge(s_w, 16 * len(weights))
                    eng.transpose(pmisc[:, 0:D], wg_raw[:, :], ident[:, :])
                    eng.transpose(pmisc[:, D:2 * D], wsk_raw[:, :], ident[:, :])
                    eng.matmul(pmisc[:, 2 * D:2 * D + 2 * H], wg_raw[:, :], att[:, :], start=True,
                               stop=True).then_inc(s_wT, 1)

        end_stage()

        NF = N // GE
        tail = (N - NF * GE) // TG
        ndone = NF + 1
        RD = 6
        assert tail * TG + NF * GE == N and tail <= P and ndone == 2 * NG and NT == 2 * ndone
        with rows_ctx, ExitStack() as pc:
            xt = sb("d_xt", [P, RD, TG, D], fp32, pc)
            x1 = sb("d_x1", [P, RD, TG, D], fp32, pc)
            xn = sb("d_xn", [P, RD, TG, D], fp32, pc)
            st = sb("d_st", [P, RD, TG, 6], fp32, pc)
            mv = sb("d_mv", [P, RD, TG, 2], fp32, pc)
            lnv, r0, sq, hv, rr, rs, off = (sb("d_" + s, [P, RD, TG], fp32, pc) for s in "lnv r0 sq hv rr rs off".split())
            hT = sb("d_hT", [P, RD, GE], fp32, pc)
            ex = sb("d_ex", [P, RD, GE], fp32, pc)
            part = sb("d_part", [P, RD, TG, D], fp32, pc)
            yo = sb("d_yo", [P, RD, TG, D], fp32, pc)
            onehot_p = sb("d_onehot_p", [P, 6, P], fp16, pc)
            ramp = sb("d_ramp", [P, 6, NCOL], fp16, pc)
            some = sb("d_some", [P, NCOL], fp32, pc)
            cum = sb("d_cum", [P, NCOL], fp32, pc)
            hist = sb("d_hist", [P, NCOL], fp32, pc)
            fl = sb("d_fl", [P, 2, NCOL], fp32, pc)
            bnd_i = sb("d_bnd_i", [P, NCOL, 2], i32, pc)
            offs = sb("d_offs", [P, 1], fp32, pc)
            islot = sb("d_islot", [P, RE, TG, 2], i32, pc)
            phist = ps("d_phist", [P, NCOL], pc)
            pbefore = ps("d_pbefore", [P, 512], pc)
            psT = [ps(f"d_psT{k}", [P, GE], pc) for k in range(2)]
            psO = [ps(f"d_psO{k}", [P, GE], pc) for k in range(3)]
            ld, stored = ring_sems("d_ld", RD), ring_sems("d_stored", RD)
            slot_set, got, raw, free = (ring_sems("d_" + s, RE) for s in ("slot_set", "got", "raw", "free"))
            (x1_ok, st_ok, mv_ok, hv_ok, lnv_ok, r0_ok, sq_ok, rr_ok, rs_ok, off_ok, xn_ok, T_ok, h_ok, O_ok, ex_ok,
             part_ok, yo_ok, onehot_ok, ramp_ok, counted, masks_ld, hist_ok, cum_ok, before_ok, bounds_ok, bounds_st, link_ok,
             pool_go) = sems("d_", "x1_ok st_ok mv_ok hv_ok lnv_ok r0_ok sq_ok rr_ok rs_ok off_ok xn_ok T_ok "
                                             "h_ok O_ok ex_ok part_ok yo_ok onehot_ok ramp_ok counted masks_ld hist_ok cum_ok before_ok bounds_ok bounds_st "
                                             "link_ok pool_go")

            def npart(g):
                return tail if isinstance(g, int) and g == NF else P

            def node_rows(t, g):
                n = npart(g)
                return t[bass.ds(g * GE, n * TG), :].rearrange("(p j) f -> p j f", j=TG)

            with nc.Block() as block:
                @block.sync
                def _(eng):
                    def load(g, k, it):
                        n = npart(g)
                        if used(g, RD):
                            eng.wait_ge(x1_ok, g - RD + 1)
                        eng.dma_start(xt[0:n, k, :, :], node_rows(x, g)).then_inc(ld[k], 16)
                        if isinstance(g, int) and g == RD + 2:
                            eng.dma_start(eq_bc[:, :], eq_d.to_broadcast([P, EP])).then_inc(masks_ld, 16)
                        if isinstance(g, int) and g == 2 * RD + 2:
                            eng.dma_start(eqr_bc[:, :], eqr_d.to_broadcast([P, EP])).then_inc(masks_ld, 16)

                    def store(g, k, it):
                        n = npart(g)
                        eng.wait_ge(yo_ok, g + 1)
                        eng.dma_start(node_rows(out, g), yo[0:n, k, :, :]).then_inc(stored[k], 16)

                    def edge_rows(g, k, it):
                        s, e = k // 2, RE * it + (k // 2 - RE)
                        if k % 2 == 0:
                            if not isinstance(it, int) or it > 1:
                                eng.wait_ge(got[s], 32 * TG * (it - 1))
                            eng.dma_start(tile_rows(xs_d, e), xg[:, s, :, 0, :]).then_inc(raw[s], 16)
                            eng.dma_start(tile_rows(xd_d, e), xg[:, s, :, 1, :]).then_inc(raw[s], 16)
                        else:
                            eng.wait_ge(raw[s], 32 * it)
                            eng.sem_inc(free[s], 1)
                    for s in range(RE):
                        eng.sem_inc(free[s], 1)
                    pipeline(eng, ndone, [(0, load), (12, store), (0, edge_rows)], RD)
                    eng.wait_ge(masks_ld, 16 * 6)
                    eng.wait_ge(bounds_ok, 1)
                    eng.dma_start(bounds_d.rearrange("(p c) k -> p (c k)", p=P),
                                  bnd_i[:, :, :].rearrange("p c k -> p (c k)")).then_inc(bounds_st, 16)
                    eng.wait_ge(bounds_st, 16)
                    for k in range(RD):
                        eng.wait_ge(stored[k], 16 * ((ndone + RD - 1 - k) // RD))

                @block.gpsimd
                def _(eng):
                    def gather(e, s, it):
                        if isinstance(e, int) and e < RE:
                            eng.sem_inc(slot_set[s], 1)
                            return
                        eng.wait_ge(free[s], it)
                        eng.tensor_copy(islot[:, s, :, :], idx_sd[:, bass.ds(e * TG, TG), :]).then_inc(slot_set[s], 1)
                        eng.wait_ge(pool_go, 1)
                        eng.wait_ge(slot_set[s], it)
                        for j in range(TG):
                            for side in range(2):
                                eng.indirect_dma_start(
                                    xg[:, s, j, side, :], None, x,
                                    bass.IndirectOffsetOnAxis(islot[:, s, j, side:side + 1], 0)).then_inc(got[s], 16)
                    eng.sem_inc(pool_go, 1)
                    pool_pipeline(eng, NG, gather, ring=RE)

                @block.vector
                def _(eng):
                    def add(g, k, it):
                        n = npart(g)
                        if used(g, RD):
                            eng.wait_ge(part_ok, g - RD + 1)
                        eng.wait_ge(ld[k], 16 * it)
                        eng.tensor_tensor(x1[0:n, k, :, :], xt[0:n, k, :, :],
                                          empty_bc[0:n, :, :].to_broadcast([n, TG, D]), ALU.add).then_inc(x1_ok, 1)

                    def root_step_1(g, k, it):
                        n = npart(g)
                        eng.wait_ge(sq_ok, g + 1)
                        eng.wait_ge(hv_ok, g + 1)
                        eng.tensor_tensor(rr[0:n, k, :], sq[0:n, k, :], hv[0:n, k, :], ALU.mult).then_inc(rr_ok, 1)

                    def stats(g, k, it):
                        n = npart(g)
                        eng.wait_ge(x1_ok, g + 1)
                        for j in range(TG):
                            last = eng.bn_stats(st[0:n, k, j, :], x1[0:n, k, j, :])
                        last.then_inc(st_ok, 1)

                    def one_hots(g, k, it):
                        if used(g, 3):
                            eng.wait_ge(counted, g - 2)
                        for t in range(2):
                            last = eng.tensor_scalar(onehot_p[:, (2 * k + t) % 6, :], iota_h[:, 0:P],
                                                     part_f[:, 0, bass.ds(2 * g + t, 1)], None, ALU.is_equal)
                        last = eng.tensor_scalar(ramp[:, 2 * k % 6, :], iota_h[:, :], part_f[:, 1, bass.ds(2 * g, 1)], 0.0,
                                                 ALU.add, ALU.max)
                        last.then_inc(onehot_ok, 1)

                    def root_step_2(g, k, it):
                        n = npart(g)
                        if used(g, RD):
                            eng.wait_ge(xn_ok, g - RD + 1)
                        eng.wait_ge(rr_ok, g + 1)
                        eng.scalar_tensor_tensor(out=rs[0:n, k, :], in0=rr[0:n, k, :], scalar=1.5, in1=r0[0:n, k, :],
                                                 op0=ALU.add, op1=ALU.mult).then_inc(rs_ok, 1)

                    def out_part(g, k, it):
                        n = npart(g)
                        eng.wait_ge(ex_ok, g + 1)
                        eng.scalar_tensor_tensor(out=part[0:n, k, :, :].rearrange("p j f -> p (j f)"), in0=ex[0:n, k, :],
                                                 scalar=1.0, in1=x1[0:n, k, :, :].rearrange("p j f -> p (j f)"),
                                                 op0=ALU.min, op1=ALU.add).then_inc(part_ok, 1)

                    def offset(g, k, it):
                        n = npart(g)
                        eng.wait_ge(rs_ok, g + 1)
                        if not isinstance(g, int):
                            eng.wait_ge(st_ok, g + 2)
                        eng.scalar_tensor_tensor(out=off[0:n, k, :], in0=mv[0:n, k, :, 0], scalar=-1.0, in1=rs[0:n, k, :],
                                                 op0=ALU.mult, op1=ALU.mult).then_inc(off_ok, 1)

                    def aggregate(g, k, it):
                        n = npart(g)
                        if isinstance(g, int):
                            eng.wait_ge(st_ok, g + 1)
                        for j in range(TG):
                            last = eng.bn_aggr(mv[0:n, k, j, :], st[0:n, k, j, :])
                        last.then_inc(mv_ok, 1)

                    def finish(g, k, it):
                        n = npart(g)
                        eng.wait_ge(part_ok, g + 1)
                        if used(g, RD):
                            eng.wait_ge(stored[k], 16 * (it - 1))
                        eng.scalar_tensor_tensor(out=yo[0:n, k, :, :].rearrange("p j f -> p (j f)"), in0=psO[k % 3][0:n, :],
                                                 scalar=0.0, in1=part[0:n, k, :, :].rearrange("p j f -> p (j f)"),
                                                 op0=ALU.max, op1=ALU.add).then_inc(yo_ok, 1)

                    def half_variance(g, k, it):
                        n = npart(g)
                        eng.wait_ge(mv_ok, g + 1)
                        eng.tensor_scalar(hv[0:n, k, :], mv[0:n, k, :, 1], EPS, -0.5, ALU.add, ALU.mult).then_inc(hv_ok, 1)
                    link = linker(eng, link_ok)

                    def sums_of_counts(g, k, it):
                        if not isinstance(g, int) or g < ndone - 1:
                            return
                        eng.wait_ge(hist_ok, 1)
                        link(eng.tensor_copy(some[:, :], phist[:, :]))
                        link(eng.tensor_copy(cum[:, 0:1], some[:, 0:1]))
                        link(eng.tensor_tensor(cum[:, 1:NCOL], some[:, 1:NCOL], some[:, 0:NCOL - 1], ALU.subtract))
                        eng.sem_inc(cum_ok, 1)
                        link(eng.tensor_copy(hist[:, 0:1], cum[:, 0:1]))
                        link(eng.tensor_tensor(hist[:, 1:NCOL], cum[:, 1:NCOL], cum[:, 0:NCOL - 1], ALU.subtract))
                        link(eng.tensor_scalar(some[:, :], hist[:, :], 1.0, None, ALU.min))

                    def bounds(g, k, it):
                        if not isinstance(g, int) or g < ndone - 1:
                            return
                        eng.wait_ge(before_ok, 1)
                        link(eng.tensor_copy(offs[:, :], pbefore[:, 0:1]))
                        link(eng.tensor_scalar(cum[:, :], cum[:, :], offs[:, 0:1], float(NONE), ALU.add, ALU.subtract))
                        link(eng.tensor_tensor(fl[:, 0, :], cum[:, :], hist[:, :], ALU.subtract))
                        link(eng.tensor_scalar(fl[:, 1, :], cum[:, :], 1.0, None, ALU.subtract))
                        for j in range(2):
                            link(eng.tensor_tensor(fl[:, j, :], fl[:, j, :], some[:, :], ALU.mult))
                            link(eng.tensor_scalar(bnd_i[:, :, j], fl[:, j, :], float(NONE), None, ALU.add))
                        eng.sem_inc(bounds_ok, 1)
                    pipeline(eng, ndone, [(0, add), (1, root_step_1), (0, stats), (1, root_step_2), (5, out_part), (1, offset),
                                          (5, finish), (0, aggregate), (0, half_variance), (0, one_hots), (2, sums_of_counts),
                                          (3, bounds)], RD)

                @block.tensor
                def _(eng):
                    def count(g, k, it):
                        eng.wait_ge(onehot_ok, g + 1)
                        eng.wait_ge(ramp_ok, g + 1)
                        for t in range(2):
                            b = (2 * k + t) % 6
                            last = eng.matmul(phist[:, :], onehot_p[:, b, :], ramp[:, b, :], start=False, stop=False)
                        last.then_inc(counted, 1)
                        if isinstance(g, int) and g == ndone - 1:
                            eng.matmul(phist[:, :], zeros_h[:, 0:P], zeros_h[:, :], start=False, stop=True).then_inc(hist_ok, 1)

                    def edges_before(g, k, it):
                        if isinstance(g, int) and g == ndone - 1:
                            eng.wait_ge(cum_ok, 1)
                            eng.matmul(pbefore[:, 0:1], before[:, :], cum[:, NCOL - 1:NCOL], start=True,
                                       stop=True).then_inc(before_ok, 1)

                    def turn(g, k, it):
                        n = npart(g)
                        eng.wait_ge(xn_ok, g + 1)
                        if used(g, 2):
                            eng.wait_ge(h_ok, g - 1)
                        for j in range(TG):
                            last = eng.transpose(psT[k % 2][:, j * P:j * P + n], xn[0:n, k, j, :], ident[0:n, 0:n])
                        last.then_inc(T_ok, 1)

                    def project(g, k, it):
                        n = npart(g)
                        if used(g, 3):
                            eng.wait_ge(yo_ok, g - 2)
                        eng.wait_ge(h_ok, g + 1)
                        eng.matmul(psO[k % 3][0:n, :], ones_3[:, 0:n], bias_3[:, :, :].rearrange("a j f -> a (j f)"),
                                   start=True, stop=False)
                        for j in range(TG):
                            last = eng.matmul(psO[k % 3][0:n, j * D:(j + 1) * D], hT[:, k, j * P:j * P + n], wsum[:, :],
                                              start=False, stop=j == TG - 1)
                        last.then_inc(O_ok, 1)
                    eng.matmul(phist[:, :], zeros_h[:, 0:P], zeros_h[:, :], start=True, stop=False)
                    pipeline(eng, ndone, [(1, count), (3, project), (1, turn), (2, edges_before)], RD)

                @block.scalar
                def _(eng):
                    def copy_turned(g, k, it):
                        n = npart(g)
                        eng.wait_ge(T_ok, g + 1)
                        if used(g, RD):
                            eng.wait_ge(O_ok, g - RD + 1)
                        v = lambda t: t.rearrange("p (j n) -> p j n", j=TG)[:, :, 0:n]
                        eng.activation(v(hT[:, k, :]), v(psT[k % 2][:, :]), ACT.Copy).then_inc(h_ok, 1)

                    def normalise(g, k, it):
                        n = npart(g)
                        eng.wait_ge(off_ok, g + 1)
                        if used(g, RD):
                            eng.wait_ge(T_ok, g - RD + 1)
                        for j in range(TG):
                            last = eng.activation(xn[0:n, k, j, :], x1[0:n, k, j, :], ACT.Relu,
                                                  bias=off[0:n, k, j:j + 1], scale=rs[0:n, k, j:j + 1])
                        last.then_inc(xn_ok, 1)

                    def expo(g, k, it):
                        n = npart(g)
                        eng.wait_ge(O_ok, g + 1)
                        if used(g, RD):
                            eng.wait_ge(part_ok, g - RD + 1)
                        eng.activation(ex[0:n, k, :], psO[k % 3][0:n, :], ACT.Exp).then_inc(ex_ok, 1)

                    def root(g, k, it):
                        n = npart(g)
                        eng.wait_ge(mv_ok, g + 1)
                        eng.activation(lnv[0:n, k, :], mv[0:n, k, :, 1], ACT.Ln, bias=eps[0:n, :]).then_inc(lnv_ok, 1)
                        if used(g, RD):
                            eng.wait_ge(rs_ok, g - RD + 1)
                        eng.wait_ge(lnv_ok, g + 1)
                        eng.activation(r0[0:n, k, :], lnv[0:n, k, :], ACT.Exp, scale=-0.5).then_inc(r0_ok, 1)
                        eng.wait_ge(r0_ok, g + 1)
                        eng.activation(sq[0:n, k, :], r0[0:n, k, :], ACT.Square).then_inc(sq_ok, 1)
                    def ramps(g, k, it):
                        if used(g, 3):
                            eng.wait_ge(counted, g - 2)
                        eng.activation(ramp[:, (2 * k + 1) % 6, :], iota_h[:, :], ACT.Relu,
                                       bias=part_f[:, 1, bass.ds(2 * g + 1, 1)]).then_inc(ramp_ok, 1)
                    eng.preload_act_table_set("natural_log_exp_and_others")
                    for l in range(2):
                        for k in range(2):
                            eng.dma_start(b2_6[l][3 * k:3 * k + 3, :], split_d[:, l * D:(l + 1) * D]).then_inc(masks_ld, 16)
                    pipeline(eng, ndone, [(0, root), (4, expo), (3, copy_turned), (1, normalise), (0, ramps)], RD)

        end_stage()

        def conv(l):
            pre = f"v{l}_"
            rev = slice(None, None, -1) if l else slice(None)
            table = (seg1_d, seg2_d)[l]
            is_end = (is_last, is_first)[l]
            wd, ws, w2l = w1d[l], w1s[l], w2[l]

            def place(g):
                return g * -1 + (NG - 1) if l else g

            def mask(g):
                return (eqr_bc if l else eq_bc)[:, bass.ds(g * GE, GE)]

            with ExitStack() as pc:
                if l == 0:
                    xg = sb(pre + "xg", [P, RING, TG, 2, D], fp32, pc)
                    xn = sb(pre + "xn", [P, RING, TG, 2, D], fp32, pc)
                    st = sb(pre + "st", [P, RING, TG, 2, 6], fp32, pc)
                    mv = sb(pre + "mv", [P, RING, TG, 2, 2], fp32, pc)
                    sd = sb(pre + "sd", [P, RING, TG, 2], fp32, pc)
                    rs = sb(pre + "rs", [P, RING, TG, 2], fp32, pc)
                    off = sb(pre + "off", [P, RING, TG, 2], fp32, pc)
                    bslot = sb(pre + "bslot", [P, RING, TG, 2], i32, pc)
                else:
                    zg = sb(pre + "zg", [P, RING, TG, D], fp32, pc)
                    zd = sb(pre + "zd", [P, RING, TG, D], fp32, pc)
                    handed = sb(pre + "handed", [P, RING, GE], fp32, pc)
                islot = sb(pre + "islot", [P, RING, TG], i32, pc)
                hx = sb(pre + "hx", [P, RING, 2, GE], fp32, pc)
                hid = sb(pre + "hid", [P, RING, GE], fp32, pc)
                run = sb(pre + "run", [P, RING, GE], fp32, pc)
                zst = sb(pre + "zst", [P, RING, TG, 6], fp32, pc)
                zmv = sb(pre + "zmv", [P, RING, TG, 2], fp32, pc)
                zsd = sb(pre + "zsd", [P, RING, TG], fp32, pc)
                zrs = sb(pre + "zrs", [P, RING, TG], fp32, pc)
                zsc = sb(pre + "zsc", [P, RING, TG], fp32, pc)
                zof = sb(pre + "zof", [P, RING, TG], fp32, pc)
                zr = sb(pre + "zr", [P, RING, TG, D], fp32, pc)
                cnt = sb(pre + "cnt", [6, RING, GE], bf16, pc)
                psS = ps(pre + "psS", [P, GE], pc)
                psD = ps(pre + "psD", [P, GE], pc)
                psM = [ps(pre + f"psM{k}", [P, GE], pc) for k in range(2)]
                psZ = [ps(pre + f"psZ{k}", [P, GE], pc) for k in range(RING)]
                (st_ok, mv_ok, sd_ok, rs_ok, off_ok, xn_ok, T_ok, hS_ok, handed_ok, hD_ok, h_ok, M_ok, hid_ok, bent_ok, run_ok, Z_ok,
                 zst_ok, zmv_ok, zsd_ok, zrs_ok, zsc_ok, zof_ok, zr_ok, pool_go) = sems(
                    pre, "st_ok mv_ok sd_ok rs_ok off_ok xn_ok T_ok hS_ok handed_ok hD_ok h_ok M_ok hid_ok bent_ok run_ok Z_ok "
                    "zst_ok zmv_ok zsd_ok zrs_ok zsc_ok zof_ok zr_ok pool_go")
                slot_set, free, got, ld, cld, stored = (ring_sems(pre + s) for s in (
                    "slot_set", "free", "got", "ld", "cnt_ld", "stored"))

                with nc.Block() as block:
                    @block.gpsimd
                    def _(eng):
                        def look(g, k, it):
                            eng.tensor_copy(islot[:, k, :], idx_sd[:, bass.ds(g * TG, TG), 0]).then_inc(slot_set[k], 1)
                            eng.wait_ge(pool_go, 1)
                            eng.wait_ge(slot_set[k], it)
                            for j in range(TG):
                                eng.indirect_dma_start(bslot[:, k, j, :], None, bounds_d,
                                                       bass.IndirectOffsetOnAxis(islot[:, k, j:j + 1], 0)
                                                       ).then_inc(got[k], 16)

                        def keep(g, k, it):
                            eng.wait_ge(got[k], 16 * TG * it)
                            eng.tensor_copy(bnd[:, bass.ds(g * TG, TG), :], bslot[:, k, :, :]).then_inc(free[k], 1)

                        def gather(g, k, it):
                            eng.wait_ge(free[k], it)
                            eng.tensor_copy(islot[:, k, :], bnd[:, bass.ds(place(g) * TG, TG), 1]).then_inc(slot_set[k], 1)
                            eng.wait_ge(pool_go, 1)
                            eng.wait_ge(slot_set[k], it)
                            for j in range(TG):
                                eng.indirect_dma_start(
                                    zg[:, k, j, :], None, seg1_d,
                                    bass.IndirectOffsetOnAxis(islot[:, k, j:j + 1], 0)).then_inc(got[k], 16)
                        eng.sem_inc(pool_go, 1)
                        if l == 0:
                            pool_pipeline(eng, NG, look, keep)
                        else:
                            pool_pipeline(eng, NG, gather)

                    @block.sync
                    def _(eng):
                        def load(g, k, it):
                            if l == 0:
                                if later(g):
                                    eng.wait_ge(xn_ok, g - RING + 1)
                                eng.dma_start(xg[:, k, :, 0, :], tile_rows(xs_d, g)).then_inc(ld[k], 16)
                                eng.dma_start(xg[:, k, :, 1, :], tile_rows(xd_d, g)).then_inc(ld[k], 16)
                            else:
                                if later(g):
                                    eng.wait_ge(T_ok, g - RING + 1)
                                eng.dma_start(zd[:, k, :, :], tile_rows(seg1_d, place(g))).then_inc(ld[k], 16)

                        def load_counts(g, k, it):
                            if later(g):
                                eng.wait_ge(Z_ok, g - RING + 1)
                            eng.dma_start(cnt[:, k, :], cnt_d[:, bass.ds(place(g) * GE, GE)]).then_inc(cld[k], 16)

                        def release(g, k, it):
                            eng.wait_ge(T_ok, g + 1)
                            eng.sem_inc(free[k], 1)

                        def store(g, k, it):
                            eng.wait_ge(zr_ok, g + 1)
                            eng.dma_start(tile_rows(table, place(g)), zr[:, k, :, :]).then_inc(stored[k], 16)
                        if l == 0:
                            pipeline(eng, NG, [(0, load), (6, load_counts), (13, store)])
                        else:
                            for k in range(RING):
                                eng.sem_inc(free[k], 1)
                            pipeline(eng, NG, [(0, load), (RING, release), (6, load_counts), (13, store)])
                        for k in range(RING):
                            eng.wait_ge(stored[k], 16 * ((NG + RING - 1 - k) // RING))

                    @block.vector
                    def _(eng):
                        def x_stats(g, k, it):
                            eng.wait_ge(ld[k], 32 * it)
                            for j in range(TG):
                                for side in range(2):
                                    last = eng.bn_stats(st[:, k, j, side, :], xg[:, k, j, side, :])
                            last.then_inc(st_ok, 1)

                        def z_stats(g, k, it):
                            eng.wait_ge(Z_ok, g + 1)
                            for j in range(TG):
                                last = eng.bn_stats(zst[:, k, j, :], psZ[k][:, j * D:(j + 1) * D])
                            last.then_inc(zst_ok, 1)

                        def bend_hidden(g, k, it):
                            eng.wait_ge(hid_ok, g + 1)
                            eng.scalar_tensor_tensor(out=hid[:, k, :], in0=hid[:, k, :], scalar=SLOPE, in1=hid[:, k, :],
                                                     op0=ALU.mult, op1=ALU.max).then_inc(bent_ok, 1)

                        def add_up(g, k, it):
                            if not isinstance(g, int):
                                eng.wait_ge(zst_ok, g - 1)
                                if l == 0:
                                    eng.wait_ge(st_ok, g + 7)
                            if later(g):
                                eng.wait_ge(Z_ok, g - RING + 1)
                            if used(g, 1):
                                eng.wait_ge(run_ok, g)
                            eng.wait_ge(bent_ok, g + 1)
                            end = 0 if l else GE - 1
                            eng.tensor_tensor_scan(
                                out=run[:, k, rev], data0=mask(g), data1=hid[:, k, rev],
                                initial=run[:, (k - 1) % RING, end:end + 1] if used(g, 1) else 0.0,
                                op0=ALU.mult, op1=ALU.add).then_inc(run_ok, 1)

                        def x_aggregate(g, k, it):
                            if isinstance(g, int):
                                eng.wait_ge(st_ok, g + 1)
                            for j in range(TG):
                                for side in range(2):
                                    last = eng.bn_aggr(mv[:, k, j, side, :], st[:, k, j, side, :])
                            last.then_inc(mv_ok, 1)

                        def z_aggregate(g, k, it):
                            if isinstance(g, int):
                                eng.wait_ge(zst_ok, g + 1)
                            for j in range(TG):
                                last = eng.bn_aggr(zmv[:, k, j, :], zst[:, k, j, :])
                            last.then_inc(zmv_ok, 1)

                        def x_scales(g, k, it):
                            eng.wait_ge(sd_ok, g + 1)
                            eng.reciprocal(rs[:, k, :, :], sd[:, k, :, :]).then_inc(rs_ok, 1)

                        def x_offsets(g, k, it):
                            if later(g):
                                eng.wait_ge(xn_ok, g - RING + 1)
                            eng.wait_ge(rs_ok, g + 1)
                            eng.scalar_tensor_tensor(out=off[:, k, :, :], in0=mv[:, k, :, :, 0], scalar=-1.0,
                                                     in1=rs[:, k, :, :], op0=ALU.mult, op1=ALU.mult).then_inc(off_ok, 1)

                        def bend(g, k, it):
                            eng.wait_ge(hS_ok, g + 1)
                            eng.wait_ge(hD_ok, g + 1)
                            eng.scalar_tensor_tensor(out=hx[:, k, :, :], in0=hx[:, k, :, :], scalar=SLOPE,
                                                     in1=hx[:, k, :, :], op0=ALU.mult, op1=ALU.max).then_inc(h_ok, 1)

                        def hand_on(g, k, it):
                            if later(g):
                                eng.wait_ge(hD_ok, g - RING + 1)
                            if used(g, 1):
                                eng.wait_ge(handed_ok, g)
                            eng.wait_ge(T_ok, g + 1)
                            eng.tensor_tensor_scan(
                                out=handed[:, k, rev], data0=mask(g), data1=psD[:, rev],
                                initial=handed[:, (k - 1) % RING, 0:1] if used(g, 1) else 0.0,
                                op0=ALU.mult, op1=ALU.add).then_inc(handed_ok, 1)

                        def z_scale_1(g, k, it):
                            eng.wait_ge(zsd_ok, g + 1)
                            eng.reciprocal(zrs[:, k, :], zsd[:, k, :]).then_inc(zrs_ok, 1)

                        def z_scale_2(g, k, it):
                            if later(g):
                                eng.wait_ge(zr_ok, g - RING + 1)
                            eng.wait_ge(zrs_ok, g + 1)
                            eng.tensor_tensor(zsc[:, k, :], zrs[:, k, :], is_end[:, bass.ds(place(g) * TG, TG)],
                                              ALU.mult).then_inc(zsc_ok, 1)

                        def z_offset(g, k, it):
                            eng.wait_ge(zsc_ok, g + 1)
                            eng.scalar_tensor_tensor(out=zof[:, k, :], in0=zmv[:, k, :, 0], scalar=-1.0, in1=zsc[:, k, :],
                                                     op0=ALU.mult, op1=ALU.mult).then_inc(zof_ok, 1)

                        def input_d(g, k, it):
                            if later(g):
                                eng.wait_ge(M_ok, g - RING + 1)
                            eng.wait_ge(T_ok, g + 1)
                            eng.tensor_copy(hx[:, k, 1, :], psD[:, :]).then_inc(hD_ok, 1)
                        if l == 0:
                            pipeline(eng, NG, [(0, x_stats), (1, x_scales), (9, z_scale_1), (6, bend_hidden), (1, x_offsets),
                                               (9, z_scale_2), (8, z_stats), (9, z_offset), (3, input_d), (6, add_up),
                                               (0, x_aggregate), (8, z_aggregate)])
                        else:
                            pipeline(eng, NG, [(3, bend), (9, z_scale_1), (8, z_stats), (9, z_scale_2), (6, bend_hidden),
                                               (1, hand_on), (9, z_offset), (6, add_up), (8, z_aggregate)])

                    @block.tensor
                    def _(eng):
                        def turn(g, k, it):
                            if used(g, 1):
                                eng.wait_ge(hS_ok, g)
                                eng.wait_ge(hD_ok if l == 0 else handed_ok, g)
                            if l == 0:
                                eng.wait_ge(xn_ok, g + 1)
                            else:
                                eng.wait_ge(ld[k], 16 * it)
                                eng.wait_ge(got[k], 16 * TG * it)
                            for j in range(TG):
                                c = slice(j * P, (j + 1) * P)
                                eng.transpose(psS[:, c], xn[:, k, j, 0, :] if l == 0 else zg[:, k, j, :], ident[:, :])
                                last = eng.transpose(psD[:, c], xn[:, k, j, 1, :] if l == 0 else zd[:, k, j, :], ident[:, :])
                            last.then_inc(T_ok, 1)

                        def hidden(g, k, it):
                            if used(g, 2):
                                eng.wait_ge(hid_ok, g - 1)
                            if l == 0:
                                eng.wait_ge(hS_ok, g + 1)
                                eng.wait_ge(hD_ok, g + 1)
                            else:
                                eng.wait_ge(h_ok, g + 1)
                            eng.matmul(psM[k % 2][:, :], ws[:, :], hx[:, k, 0, :], start=True, stop=False)
                            eng.matmul(psM[k % 2][:, :], wd[:, :], hx[:, k, 1, :], start=False, stop=True).then_inc(M_ok, 1)

                        def second(g, k, it):
                            if later(g):
                                eng.wait_ge(zr_ok, g - RING + 1)
                            eng.wait_ge(cld[k], 16 * it)
                            eng.wait_ge(run_ok, g + 1)
                            for j in range(TG):
                                o = psZ[k][:, j * D:(j + 1) * D]
                                c = slice(j * P, (j + 1) * P)
                                eng.matmul(o, cnt[:, k, c], b2_6[l][:, :], start=True, stop=False)
                                last = eng.matmul(o, run[:, k, c], w2l[:, :], start=False, stop=True)
                            last.then_inc(Z_ok, 1)
                        pipeline(eng, NG, [(7, second), (4, hidden), (2 - 2 * l, turn)])

                    @block.scalar
                    def _(eng):
                        def x_root(g, k, it):
                            eng.wait_ge(mv_ok, g + 1)
                            eng.activation(sd[:, k, :, :], mv[:, k, :, :, 1], ACT.Sqrt, bias=eps[:, :]).then_inc(sd_ok, 1)

                        def x_normalise(g, k, it):
                            eng.wait_ge(off_ok, g + 1)
                            if later(g):
                                eng.wait_ge(T_ok, g - RING + 1)
                            for j in range(TG):
                                for side in range(2):
                                    last = eng.activation(xn[:, k, j, side, :], xg[:, k, j, side, :], ACT.Relu,
                                                          bias=off[:, k, j, side:side + 1], scale=rs[:, k, j, side:side + 1])
                            last.then_inc(xn_ok, 1)

                        def input_s(g, k, it):
                            if later(g):
                                eng.wait_ge(M_ok, g - RING + 1)
                            eng.wait_ge(T_ok, g + 1)
                            eng.activation(hx[:, k, 0, :], psS[:, :], ACT.Identity, bias=bc[0][:, :],
                                           scale=gc[0][:, :]).then_inc(hS_ok, 1)

                        def inputs(g, k, it):
                            if later(g):
                                eng.wait_ge(M_ok, g - RING + 1)
                            eng.wait_ge(T_ok, g + 1)
                            if l == 0:
                                eng.activation(hx[:, k, 0, :], psS[:, :], ACT.Copy).then_inc(hS_ok, 1)
                            else:
                                eng.wait_ge(handed_ok, g + 1)
                                eng.activation(hx[:, k, 1, :], handed[:, k, :], ACT.Identity, bias=bc[0][:, :],
                                               scale=gc[0][:, :]).then_inc(hD_ok, 1)

                        def biased(g, k, it):
                            if later(g):
                                eng.wait_ge(run_ok, g - RING + 1)
                            eng.wait_ge(M_ok, g + 1)
                            eng.activation(hid[:, k, :], psM[k % 2][:, :], ACT.Identity, bias=b1c[l][:, :]).then_inc(hid_ok, 1)

                        def z_root(g, k, it):
                            eng.wait_ge(zmv_ok, g + 1)
                            eng.activation(zsd[:, k, :], zmv[:, k, :, 1], ACT.Sqrt, bias=eps[:, :]).then_inc(zsd_ok, 1)

                        def z_normalise(g, k, it):
                            if later(g):
                                eng.wait_ge(stored[k], 16 * (it - 1))
                            eng.wait_ge(zof_ok, g + 1)
                            for j in range(TG):
                                last = eng.activation(zr[:, k, j, :], psZ[k][:, j * D:(j + 1) * D], ACT.Identity,
                                                      bias=zof[:, k, j:j + 1], scale=zsc[:, k, j:j + 1])
                            last.then_inc(zr_ok, 1)
                        if l == 0:
                            pipeline(eng, NG, [(0, x_root), (8, z_root), (3, inputs), (5, biased), (9, z_normalise), (1, x_normalise)])
                        else:
                            pipeline(eng, NG, [(1, input_s), (8, z_root), (5, biased), (1, inputs), (9, z_normalise)])

        conv(0)
        end_stage()
        conv(1)
        end_stage()

        with ExitStack() as pc:
            zg = sb("a_zg", [P, RING, TG, D], fp32, pc)
            zd = sb("a_zd", [P, RING, TG, D], fp32, pc)
            xr = sb("a_xr", [P, RING, 2, TG, D], fp32, pc)
            x1 = sb("a_x1", [P, RING, 2, TG, D], fp32, pc)
            hh = sb("a_hh", [P, RING, 2, GE], fp32, pc)
            handed = sb("a_handed", [P, RING, GE], fp32, pc)
            st = sb("a_st", [P, RING, 2, TG, 6], fp32, pc)
            mv = sb("a_mv", [P, RING, 2, TG, 2], fp32, pc)
            sd = sb("a_sd", [P, RING, 2, TG], fp32, pc)
            rs = sb("a_rs", [P, RING, 2, TG], fp32, pc)
            xn = sb("a_xn", [P, 2, 2, TG, D], fp32, pc)
            q = sb("a_q", [P, RING, 2, GE], fp32, pc)
            off = sb("a_off", [P, RING, 2, TG], fp32, pc)
            sc = sb("a_sc", [RING * 2 * H, GE], fp32, pc)
            islot = sb("a_islot", [P, RING, TG], i32, pc)
            psA = [ps(f"a_psA{k}", [P, GE], pc) for k in range(2)]
            psR = [ps(f"a_psR{k}", [P, GE], pc) for k in range(2)]
            psQ = [ps(f"a_psQ{k}", [P, GE], pc) for k in range(2)]
            psC = ps("a_psC", [RING * 2 * H, GE], pc)
            (kept, T_ok, hS_ok, handed_ok, hD_ok, h_ok, R_ok, x1_ok, st_ok, mv_ok, sd_ok, rs_ok, off_ok, xn_ok, Q_ok, q_ok,
             C_ok, sc_ok, pool_go) = sems("a_", "kept T_ok hS_ok handed_ok hD_ok h_ok R_ok x1_ok st_ok mv_ok sd_ok rs_ok off_ok xn_ok "
                                    "Q_ok q_ok C_ok sc_ok pool_go")
            slot_set, free, got, zld, xld, x1_st, q_st = (ring_sems("a_" + s) for s in (
                "slot_set", "free", "got", "zd_ld", "x_ld", "x1_st", "q_st"))
            sc_st = sem("a_sc_st")

            def closes(g, k):
                return k == RING - 1 or (isinstance(g, int) and g == NG - 1)

            with nc.Block() as block:
                @block.gpsimd
                def _(eng):
                    def gather(g, k, it):
                        eng.wait_ge(free[k], it)
                        eng.tensor_copy(islot[:, k, :], bnd[:, bass.ds(g * TG, TG), 0]).then_inc(slot_set[k], 1)
                        eng.wait_ge(pool_go, 1)
                        eng.wait_ge(slot_set[k], it)
                        for j in range(TG):
                            eng.indirect_dma_start(zg[:, k, j, :], None, seg2_d,
                                                   bass.IndirectOffsetOnAxis(islot[:, k, j:j + 1], 0)).then_inc(got[k], 16)
                    eng.sem_inc(pool_go, 1)
                    pool_pipeline(eng, NG, gather)

                @block.sync
                def _(eng):
                    def load_z(g, k, it):
                        if later(g):
                            eng.wait_ge(T_ok, g - RING + 1)
                        eng.dma_start(zd[:, k, :, :], tile_rows(seg2_d, g)).then_inc(zld[k], 16)

                    def load_x(g, k, it):
                        if later(g):
                            eng.wait_ge(x1_ok, g - RING + 1)
                        eng.dma_start(xr[:, k, 0, :, :], tile_rows(xs_d, g)).then_inc(xld[k], 16)
                        eng.dma_start(xr[:, k, 1, :, :], tile_rows(xd_d, g)).then_inc(xld[k], 16)

                    def release(g, k, it):
                        eng.wait_ge(T_ok, g + 1)
                        eng.sem_inc(free[k], 1)

                    def store_x1(g, k, it):
                        eng.wait_ge(x1_ok, g + 1)
                        eng.dma_start(tile_rows(x1_d, g), x1[:, k, 1, :, :]).then_inc(x1_st[k], 16)

                    def store_q(g, k, it):
                        eng.wait_ge(q_ok, g + 1)
                        eng.dma_start(qs_d[bass.ds(g, 1), :, :].rearrange("a p n -> (a p) n"), q[:, k, 0, :]).then_inc(q_st[k], 16)

                    def store_scores(g, k, it):
                        if closes(g, k):
                            eng.wait_ge(sc_ok, it)
                            for j in range(k + 1):
                                eng.dma_start(score_d[:, bass.ds((g - (k - j)) * GE, GE)], sc[2 * H * j:2 * H * (j + 1), :]
                                              ).then_inc(sc_st, 16)
                    for k in range(RING):
                        eng.sem_inc(free[k], 1)
                    pipeline(eng, NG, [(0, load_z), (RING, release), (RING, load_x), (9, store_x1), (12, store_q),
                                       (14, store_scores)])
                    for k in range(RING):
                        n = (NG + RING - 1 - k) // RING
                        eng.wait_ge(x1_st[k], 16 * n)
                        eng.wait_ge(q_st[k], 16 * n)
                    eng.wait_ge(sc_st, 16 * NG)

                @block.vector
                def _(eng):
                    def bend(g, k, it):
                        eng.wait_ge(hS_ok, g + 1)
                        eng.wait_ge(hD_ok, g + 1)
                        eng.scalar_tensor_tensor(out=hh[:, k, :, :], in0=hh[:, k, :, :], scalar=SLOPE,
                                                 in1=hh[:, k, :, :], op0=ALU.mult, op1=ALU.max).then_inc(h_ok, 1)

                    def add_x(g, k, it):
                        eng.wait_ge(xld[k], 32 * it)
                        if later(g):
                            eng.wait_ge(x1_st[k], 16 * (it - 1))
                            eng.wait_ge(xn_ok, g - RING + 1)
                        eng.wait_ge(R_ok, g + 1)
                        f = lambda t, side: t[:, k, side, :, :].rearrange("p j f -> p (j f)")
                        eng.tensor_tensor(f(x1, 0), psR[0][:, :], f(xr, 0), ALU.add)
                        eng.tensor_tensor(f(x1, 1), psR[1][:, :], f(xr, 1), ALU.add).then_inc(x1_ok, 1)
                        eng.wait_ge(x1_ok, g + 1)
                        for side in range(2):
                            for j in range(TG):
                                last = eng.bn_stats(st[:, k, side, j, :], x1[:, k, side, j, :])
                        last.then_inc(st_ok, 1)

                    def hand_on(g, k, it):
                        if not isinstance(g, int):
                            eng.wait_ge(st_ok, g - 2)
                        if later(g):
                            eng.wait_ge(hD_ok, g - RING + 1)
                        if used(g, 1):
                            eng.wait_ge(handed_ok, g)
                        eng.wait_ge(T_ok, g + 1)
                        eng.tensor_tensor_scan(
                            out=handed[:, k, :], data0=eq_bc[:, bass.ds(g * GE, GE)], data1=psA[1][:, :],
                            initial=handed[:, (k - 1) % RING, GE - 1:GE] if used(g, 1) else 0.0,
                            op0=ALU.mult, op1=ALU.add).then_inc(handed_ok, 1)

                    def aggregate(g, k, it):
                        if isinstance(g, int):
                            eng.wait_ge(st_ok, g + 1)
                        for side in range(2):
                            for j in range(TG):
                                last = eng.bn_aggr(mv[:, k, side, j, :], st[:, k, side, j, :])
                        last.then_inc(mv_ok, 1)

                    def scales(g, k, it):
                        if later(g):
                            eng.wait_ge(kept, g - RING + 1)
                        eng.wait_ge(sd_ok, g + 1)
                        eng.reciprocal(rs[:, k, :, :], sd[:, k, :, :]).then_inc(rs_ok, 1)

                    def offsets(g, k, it):
                        if later(g):
                            eng.wait_ge(xn_ok, g - RING + 1)
                        eng.wait_ge(rs_ok, g + 1)
                        eng.scalar_tensor_tensor(out=off[:, k, :, :], in0=mv[:, k, :, :, 0], scalar=-1.0, in1=rs[:, k, :, :],
                                                 op0=ALU.mult, op1=ALU.mult).then_inc(off_ok, 1)
                    def keep_scales(g, k, it):
                        eng.wait_ge(off_ok, g + 1)
                        eng.tensor_copy(scale_d[:, 0, bass.ds(g * TG, TG)], rs[:, k, 1, :])
                        eng.tensor_copy(scale_d[:, 1, bass.ds(g * TG, TG)], off[:, k, 1, :]).then_inc(kept, 1)
                    pipeline(eng, NG, [(4, add_x), (5, scales), (1, hand_on), (5, offsets), (2, bend), (5, keep_scales),
                                       (4, aggregate)])

                @block.tensor
                def _(eng):
                    def turn(g, k, it):
                        if used(g, 1):
                            eng.wait_ge(hS_ok, g)
                            eng.wait_ge(handed_ok, g)
                        eng.wait_ge(zld[k], 16 * it)
                        eng.wait_ge(got[k], 16 * TG * it)
                        for j in range(TG):
                            eng.transpose(psA[0][:, j * P:(j + 1) * P], zg[:, k, j, :], ident[:, :])
                            last = eng.transpose(psA[1][:, j * P:(j + 1) * P], zd[:, k, j, :], ident[:, :])
                        last.then_inc(T_ok, 1)

                    def rows(g, k, it):
                        if used(g, 1):
                            eng.wait_ge(x1_ok, g)
                        eng.wait_ge(h_ok, g + 1)
                        for side in range(2):
                            for j in range(TG):
                                last = eng.transpose(psR[side][:, j * D:(j + 1) * D], hh[:, k, side, j * P:(j + 1) * P],
                                                     ident[:, :])
                        last.then_inc(R_ok, 1)

                    def turn_again(g, k, it):
                        if used(g, 1):
                            eng.wait_ge(q_ok, g)
                        eng.wait_ge(xn_ok, g + 1)
                        for side in range(2):
                            for j in range(TG):
                                last = eng.transpose(psQ[side][:, j * P:(j + 1) * P], xn[:, k % 2, side, j, :], ident[:, :])
                        last.then_inc(Q_ok, 1)

                    def score(g, k, it):
                        if k == 0 and later(g):
                            eng.wait_ge(sc_ok, it - 1)
                        eng.wait_ge(q_ok, g + 1)
                        eng.matmul(psC[:, :], score_s[:, k, :, :].rearrange("p j h -> p (j h)"), q[:, k, 0, :],
                                   start=k == 0, stop=False)
                        eng.matmul(psC[:, :], score_dd[:, k, :, :].rearrange("p j h -> p (j h)"), q[:, k, 1, :],
                                   start=False, stop=closes(g, k)).then_inc(C_ok, 1)
                    pipeline(eng, NG, [(3, rows), (6, turn_again), (0, turn), (8, score)])

                @block.scalar
                def _(eng):
                    def affine_s(g, k, it):
                        if later(g):
                            eng.wait_ge(R_ok, g - RING + 1)
                        eng.wait_ge(T_ok, g + 1)
                        eng.activation(hh[:, k, 0, :], psA[0][:, :], ACT.Identity, bias=bc[1][:, :],
                                       scale=gc[1][:, :]).then_inc(hS_ok, 1)

                    def affine_d(g, k, it):
                        eng.wait_ge(handed_ok, g + 1)
                        eng.activation(hh[:, k, 1, :], handed[:, k, :], ACT.Identity, bias=bc[1][:, :],
                                       scale=gc[1][:, :]).then_inc(hD_ok, 1)

                    def root(g, k, it):
                        eng.wait_ge(mv_ok, g + 1)
                        eng.activation(sd[:, k, :, :], mv[:, k, :, :, 1], ACT.Sqrt, bias=eps[:, :]).then_inc(sd_ok, 1)

                    def normalise(g, k, it):
                        eng.wait_ge(off_ok, g + 1)
                        if used(g, 2):
                            eng.wait_ge(Q_ok, g - 1)
                        for side in range(2):
                            for j in range(TG):
                                last = eng.activation(xn[:, k % 2, side, j, :], x1[:, k, side, j, :], ACT.Relu,
                                                      bias=off[:, k, side, j:j + 1], scale=rs[:, k, side, j:j + 1])
                        last.then_inc(xn_ok, 1)

                    def copy_turned(g, k, it):
                        if later(g):
                            eng.wait_ge(C_ok, g - RING + 1)
                            eng.wait_ge(q_st[k], 16 * (it - 1))
                        eng.wait_ge(Q_ok, g + 1)
                        eng.activation(q[:, k, 0, :], psQ[0][:, :], ACT.Copy)
                        eng.activation(q[:, k, 1, :], psQ[1][:, :], ACT.Copy).then_inc(q_ok, 1)

                    def scores(g, k, it):
                        if closes(g, k):
                            if later(g):
                                eng.wait_ge(sc_st, 16 * RING * (it - 1))
                            eng.wait_ge(C_ok, g + 1)
                            eng.activation(sc[:, :], psC[:, :], ACT.Copy).then_inc(sc_ok, 1)

                    pipeline(eng, NG, [(7, copy_turned), (9, scores), (1, affine_s), (5, normalise), (1, affine_d), (4, root)])

        end_stage()

        with ExitStack() as pc:
            se = sb("s_se", [P, H, EJ], fp32, pc)
            sl = sb("s_sl", [P, H, EJ], fp32, pc)
            mx = sb("s_mx", [P, H, EJ], fp32, pc)
            sm = sb("s_sm", [P, H, EJ], fp32, pc)
            loc = [sb(f"s_loc{k}", [P, H, EJ], fp32, pc) for k in range(2)]
            al3 = sb("s_al3", [P, 2, 3, H, EJ], bf16, pc)
            rest = [sb(f"s_rest{k}", [P, H, EJ], fp32, pc) for k in range(2)]
            pack = sb("s_pack", [P, 4 * H], fp32, pc)
            row = sb("s_row", [H, 2, 2, P], fp32, pc)
            car = sb("s_car", [H, 2, P + 1], fp32, pc)
            carry = sb("s_carry", [P, 2 * H], fp32, pc)
            psr = ps("s_psr", [P, 512], pc)
            psc = ps("s_psc", [P, 512], pc)
            s_ld, s_link, s_arg, s_exp, s_al, s_st = sems("s_", "ld link arg exp al st")
            s_part, s_rest = ring_sems("s_part", 2), ring_sems("s_rest", 2)
            name = {k: sem("s_" + k) for k in ("pack", "row", "scanned", "carry")}
            name["n"], name["n_pe"] = [], []

            with nc.Block() as block:
                @block.sync
                def _(eng):
                    for k, t in enumerate((se, sl)):
                        eng.dma_start(t[:, :, :], score_d[k * H:(k + 1) * H, :].rearrange("h (p c) -> p h c", c=EJ)
                                      ).then_inc(s_ld, 16)
                    for side in range(2):
                        for k in range(3):
                            eng.wait_ge(s_part[side], k + 1)
                            r = 2 * H * k + H * side
                            eng.dma_start(alpha_d[r:r + H, :].rearrange("h (p c) -> p h c", c=EJ),
                                          al3[:, side, k, :, :]).then_inc(s_st, 16)
                    eng.wait_ge(s_st, 16 * 6)

                @block.vector
                def _(eng):
                    link = linker(eng, s_link)
                    eng.wait_ge(s_ld, 32)
                    for t in (se, sl):
                        link(eng.scalar_tensor_tensor(out=t[:, :, :], in0=t[:, :, :], scalar=GAT_SLOPE, in1=t[:, :, :],
                                                      op0=ALU.mult, op1=ALU.max))
                    seg_dve(eng, link, H, se, loc, pack, row, car, carry, psr, psc, name, True, mx)
                    link(eng.tensor_tensor(mx[:, :, :], mx[:, :, :], sl[:, :, :], ALU.max))
                    link(eng.tensor_tensor(se[:, :, :], se[:, :, :], mx[:, :, :], ALU.subtract))
                    link(eng.tensor_tensor(sl[:, :, :], sl[:, :, :], mx[:, :, :], ALU.subtract))
                    eng.sem_inc(s_arg, 1)
                    eng.wait_ge(s_exp, 2)
                    seg_dve(eng, link, H, se, loc, pack, row, car, carry, psr, psc, name, False, sm)
                    link(eng.scalar_tensor_tensor(out=sm[:, :, :], in0=sm[:, :, :], scalar=1e-16, in1=sl[:, :, :],
                                                  op0=ALU.add, op1=ALU.add))
                    link(eng.reciprocal(sm[:, :, :], sm[:, :, :]))
                    for t in (se, sl):
                        eng.tensor_tensor(t[:, :, :], t[:, :, :], sm[:, :, :], ALU.mult).then_inc(s_al, 1)
                    for side, t in enumerate((se, sl)):
                        eng.wait_ge(s_al, side + 1)
                        eng.wait_ge(s_part[side], 1)
                        eng.tensor_tensor(rest[side][:, :, :], t[:, :, :], al3[:, side, 0, :, :], ALU.subtract
                                          ).then_inc(s_rest[side], 1)
                    for side in range(2):
                        eng.wait_ge(s_part[side], 2)
                        eng.tensor_tensor(rest[side][:, :, :], rest[side][:, :, :], al3[:, side, 1, :, :], ALU.subtract
                                          ).then_inc(s_rest[side], 1)

                @block.tensor
                def _(eng):
                    for _ in range(2):
                        seg_pe(eng, H, pack, car, psr, psc, name)

                @block.scalar
                def _(eng):
                    eng.wait_ge(s_arg, 1)
                    eng.activation(se[:, :, :], se[:, :, :], ACT.Exp).then_inc(s_exp, 1)
                    eng.activation(sl[:, :, :], sl[:, :, :], ACT.Exp).then_inc(s_exp, 1)
                    for side, t in enumerate((se, sl)):
                        eng.wait_ge(s_al, side + 1)
                        eng.activation(al3[:, side, 0, :, :], t[:, :, :], ACT.Copy).then_inc(s_part[side], 1)
                    for k in (1, 2):
                        for side in range(2):
                            eng.wait_ge(s_rest[side], k)
                            eng.activation(al3[:, side, k, :, :], rest[side][:, :, :], ACT.Copy).then_inc(s_part[side], 1)

        end_stage()

        RB = 8
        with ExitStack() as pc:
            x1 = sb("b_x1", [P, RB, TG, D], fp32, pc)
            xn = sb("b_xn", [P, 2, TG, D], fp32, pc)
            qd = sb("b_qd", [P, RING, GE], fp32, pc)
            qs = sb("b_qs", [P, RING, GE], fp32, pc)
            al = sb("b_al", [6 * H, RING, GE], bf16, pc)
            wt = sb("b_wt", [P, 2, 2, GE], fp32, pc)
            msg, own, run, agg = (sb("b_" + s, [P, RING, GE], fp32, pc) for s in ("msg", "own", "run", "agg"))
            z, ex, pos, yy = (sb("b_" + s, [P, RING, GE], fp32, pc) for s in ("z", "ex", "pos", "yy"))
            yo = sb("b_yo", [P, RB, TG, D], fp32, pc)
            islot = sb("b_islot", [P, RB, TG], i32, pc)
            psT = ps("b_psT", [P, GE], pc)
            psW = [ps(f"b_psW{k}", [P, GE], pc) for k in range(2)]
            psS = ps("b_psS", [P, GE], pc)
            psD = ps("b_psD", [P, GE], pc)
            psK = [ps(f"b_psK{k}", [P, GE], pc) for k in range(2)]
            psY = ps("b_psY", [P, GE], pc)
            (xn_ok, T_ok, qd_ok, W_ok, wt_ok, P_ok, msg_ok, own_ok, run_ok, agg_ok, K_ok, z_ok, ex_ok, pos_ok, yy_ok, Y_ok,
             pool_go) = sems("b_", "xn_ok T_ok qd_ok W_ok wt_ok P_ok msg_ok own_ok run_ok agg_ok K_ok z_ok ex_ok pos_ok "
                             "yy_ok Y_ok pool_go")
            ld, xld, yo_ok, slot_set, sent = (ring_sems("b_" + s, RB) for s in ("ld", "x_ld", "yo_ok", "slot_set", "sent"))

            def later4(g):
                return used(g, RING)

            def k4(k):
                return k % RING

            with nc.Block() as block:
                @block.sync
                def _(eng):
                    def load_x(g, k, it):
                        if used(g, RB):
                            eng.wait_ge(yo_ok[k], it - 1)
                        eng.dma_start(x1[:, k, :, :], tile_rows(x1_d, g)).then_inc(xld[k], 16)

                    def load(g, k, it):
                        if later4(g):
                            eng.wait_ge(P_ok, g - RING + 1)
                        eng.dma_start(qs[:, k4(k), :], qs_d[bass.ds(g, 1), :, :].rearrange("a p n -> (a p) n")).then_inc(ld[k], 16)
                        eng.dma_start(al[:, k4(k), :], alpha_d[:, bass.ds(g * GE, GE)]).then_inc(ld[k], 16)
                    pipeline(eng, NG, [(0, load_x), (0, load)], RB)

                @block.tensor
                def _(eng):
                    def turn(g, k, it):
                        if used(g, 1):
                            eng.wait_ge(qd_ok, g)
                        eng.wait_ge(xn_ok, g + 1)
                        for j in range(TG):
                            last = eng.transpose(psT[:, j * P:(j + 1) * P], xn[:, k % 2, j, :], ident[:, :])
                        last.then_inc(T_ok, 1)

                    def spread_weights(g, k, it):
                        if used(g, 1):
                            eng.wait_ge(wt_ok, g)
                        eng.wait_ge(ld[k], 32 * it)
                        for side in range(2):
                            last = eng.matmul(psW[side][:, :], spread[:, side, :], al[:, k4(k), :], start=True, stop=True)
                        last.then_inc(W_ok, 1)

                    def project(g, k, it):
                        if used(g, 1):
                            eng.wait_ge(own_ok, g)
                            eng.wait_ge(msg_ok, g)
                        eng.wait_ge(qd_ok, g + 1)
                        eng.matmul(psS[:, :], wgT[:, :], qs[:, k4(k), :], start=True, stop=True)
                        eng.matmul(psD[:, :], wgT[:, :], qd[:, k4(k), :], start=True, stop=True).then_inc(P_ok, 1)

                    def skip(g, k, it):
                        if used(g, 2):
                            eng.wait_ge(z_ok, g - 1)
                        eng.matmul(psK[k % 2][:, :], wskT[:, :], qd[:, k4(k), :], start=True, stop=True).then_inc(K_ok, 1)

                    def rows(g, k, it):
                        if used(g, 1):
                            eng.wait_ge(yo_ok[(k - 1) % RB], it if k else it - 1)
                        eng.wait_ge(yy_ok, g + 1)
                        for j in range(TG):
                            last = eng.transpose(psY[:, j * D:(j + 1) * D], yy[:, k4(k), j * P:(j + 1) * P], ident[:, :])
                        last.then_inc(Y_ok, 1)
                    pipeline(eng, NG, [(2, project), (3, skip), (0, spread_weights), (0, turn), (6, rows)], RB)

                @block.scalar
                def _(eng):
                    def normalise(g, k, it):
                        eng.wait_ge(xld[k], 16 * it)
                        if used(g, 2):
                            eng.wait_ge(T_ok, g - 1)
                        for j in range(TG):
                            last = eng.activation(xn[:, k % 2, j, :], x1[:, k, j, :], ACT.Relu,
                                                  bias=scale_d[:, 1, bass.ds(g * TG + j, 1)],
                                                  scale=scale_d[:, 0, bass.ds(g * TG + j, 1)])
                        last.then_inc(xn_ok, 1)

                    def copy_turned(g, k, it):
                        if later4(g):
                            eng.wait_ge(K_ok, g - RING + 1)
                        eng.wait_ge(T_ok, g + 1)
                        eng.activation(qd[:, k4(k), :], psT[:, :], ACT.Copy).then_inc(qd_ok, 1)

                    def weights(g, k, it):
                        if used(g, 2):
                            eng.wait_ge(own_ok, g - 1)
                        eng.wait_ge(W_ok, g + 1)
                        eng.activation(wt[:, k % 2, 0, :], psW[0][:, :], ACT.Copy)
                        eng.activation(wt[:, k % 2, 1, :], psW[1][:, :], ACT.Copy).then_inc(wt_ok, 1)

                    def expo(g, k, it):
                        eng.wait_ge(z_ok, g + 1)
                        if later4(g):
                            eng.wait_ge(yy_ok, g - RING + 1)
                        eng.activation(ex[:, k4(k), :], z[:, k4(k), :], ACT.Exp).then_inc(ex_ok, 1)
                        eng.activation(pos[:, k4(k), :], z[:, k4(k), :], ACT.Relu).then_inc(pos_ok, 1)
                    pipeline(eng, NG, [(1, copy_turned), (1, weights), (0, normalise), (4, expo)], RB)

                @block.vector
                def _(eng):
                    def add_skip(g, k, it):
                        eng.wait_ge(K_ok, g + 1)
                        if later4(g):
                            eng.wait_ge(pos_ok, g - RING + 1)
                        eng.wait_ge(agg_ok, g + 1)
                        eng.scalar_tensor_tensor(out=z[:, k4(k), :], in0=psK[k % 2][:, :], scalar=bias_c[:, :],
                                                 in1=agg[:, k4(k), :], op0=ALU.add, op1=ALU.add).then_inc(z_ok, 1)

                    def elu(g, k, it):
                        if later4(g):
                            eng.wait_ge(Y_ok, g - RING + 1)
                        eng.wait_ge(pos_ok, g + 1)
                        eng.scalar_tensor_tensor(out=yy[:, k4(k), :], in0=ex[:, k4(k), :], scalar=1.0, in1=pos[:, k4(k), :],
                                                 op0=ALU.min, op1=ALU.add).then_inc(yy_ok, 1)

                    def weigh(g, k, it):
                        eng.wait_ge(wt_ok, g + 1)
                        eng.wait_ge(P_ok, g + 1)
                        if later4(g):
                            eng.wait_ge(agg_ok, g - RING + 1)
                        eng.tensor_tensor(msg[:, k4(k), :], wt[:, k % 2, 0, :], psS[:, :], ALU.mult).then_inc(msg_ok, 1)
                        eng.tensor_tensor(own[:, k4(k), :], wt[:, k % 2, 1, :], psD[:, :], ALU.mult).then_inc(own_ok, 1)

                    def add_up(g, k, it):
                        if used(g, 1):
                            eng.wait_ge(run_ok, g)
                        eng.wait_ge(msg_ok, g + 1)
                        eng.tensor_tensor_scan(
                            out=run[:, k4(k), :], data0=eq_bc[:, bass.ds(g * GE, GE)], data1=msg[:, k4(k), :],
                            initial=run[:, (k - 1) % RING, GE - 1:GE] if used(g, 1) else 0.0,
                            op0=ALU.mult, op1=ALU.add).then_inc(run_ok, 1)

                    def finish(g, k, it):
                        if used(g, RB):
                            eng.wait_ge(sent[k], 16 * TG * (it - 1))
                        eng.tensor_copy(islot[:, k, :], idx_out[:, bass.ds(g * TG, TG)]).then_inc(slot_set[k], 1)
                        eng.wait_ge(xld[k], 16 * it)
                        eng.wait_ge(Y_ok, g + 1)
                        eng.scalar_tensor_tensor(out=yo[:, k, :, :].rearrange("p j f -> p (j f)"), in0=psY[:, :],
                                                 scalar=-1.0, in1=x1[:, k, :, :].rearrange("p j f -> p (j f)"),
                                                 op0=ALU.add, op1=ALU.add).then_inc(yo_ok[k], 1)

                    def add_own(g, k, it):
                        if later4(g):
                            eng.wait_ge(z_ok, g - RING + 1)
                        eng.wait_ge(own_ok, g + 1)
                        eng.wait_ge(run_ok, g + 1)
                        eng.tensor_tensor(agg[:, k4(k), :], run[:, k4(k), :], own[:, k4(k), :], ALU.add).then_inc(agg_ok, 1)
                    pipeline(eng, NG, [(3, weigh), (4, add_skip), (7, finish), (3, add_up), (5, elu), (3, add_own)], RB)

                @block.gpsimd
                def _(eng):
                    def scatter(g, k, it):
                        eng.wait_ge(pool_go, 1)
                        eng.wait_ge(slot_set[k], it)
                        eng.wait_ge(yo_ok[k], it)
                        for j in range(TG):
                            eng.indirect_dma_start(out, bass.IndirectOffsetOnAxis(islot[:, k, j:j + 1], 0), yo[:, k, j, :],
                                                   None, bounds_check=N - 1, oob_is_err=False).then_inc(sent[k], 16)
                    eng.sem_inc(pool_go, 1)
                    pool_pipeline(eng, NG, scatter, ring=RB)
                    for k in range(RB):
                        eng.wait_ge(sent[k], 16 * TG * ((NG + RB - 1 - k) // RB))


_INS = ['x', 'src', 'dst', 'L0_gnn_W1_0', 'L0_gnn_b1_0', 'L0_gnn_W2_0', 'L0_gnn_b2_0', 'L0_gnn_ln_g0', 'L0_gnn_ln_b0',
        'L0_gnn_W1_1', 'L0_gnn_b1_1', 'L0_gnn_W2_1', 'L0_gnn_b2_1', 'L0_gnn_ln_g1', 'L0_gnn_ln_b1', 'L1_gnn_W_gat',
        'L1_gnn_att_src', 'L1_gnn_att_dst', 'L1_gnn_bias', 'L1_gnn_W_skip']


def kernel(**inputs):
    import numpy as _np
    import concourse.bacc as _bacc
    from concourse import mybir as _mybir
    from concourse.bass_utils import run_bass_kernel_spmd as _run

    nc = _bacc.Bacc("TRN2", target_bir_lowering=False, num_devices=1)
    arrays, args = {}, {}
    for name in _INS:
        a = _np.ascontiguousarray(inputs[name])
        arrays[f"in_{name}_dram"] = a
        args[name] = nc.dram_tensor(f"in_{name}_dram", a.shape, _mybir.dt.from_np(a.dtype), kind="ExternalInput").ap()
    x = inputs["x"]
    out = nc.dram_tensor("out_0_dram", x.shape, _mybir.dt.from_np(_np.asarray(x).dtype), kind="ExternalOutput").ap()
    both = lambda key: [args[f"L0_gnn_{key}{l}"] for l in range(2)]
    gnn_kernel(nc, args["x"], args["src"], args["dst"], both("W1_"), both("b1_"), both("W2_"), both("b2_"),
               both("ln_g"), both("ln_b"), args["L1_gnn_W_gat"], args["L1_gnn_att_src"], args["L1_gnn_att_dst"],
               args["L1_gnn_bias"], args["L1_gnn_W_skip"], out)
    r = _run(nc, [arrays], core_ids=[0])
    return r.results[0]["out_0_dram"]
```
